# Optimizing a Trainium2 kernel written in Bass

```python
import numpy as np
import jax
import jax.numpy as jnp

def _softmax(x, axis=-1):
    return jax.nn.softmax(x, axis=axis)

def _gelu(x):
    return jax.nn.gelu(x, approximate=True)

def _silu(x):
    return jax.nn.silu(x)

def _sigmoid(x):
    return jax.nn.sigmoid(x)

def _layernorm(x, axis=-1, eps=1e-05):
    m = jnp.mean(x, axis=axis, keepdims=True)
    v = jnp.var(x, axis=axis, keepdims=True)
    return (x - m) / jnp.sqrt(v + eps)

def _scatter_add(tgt, idx, src, axis=0):
    return tgt.at[idx].add(src)

def _segment_sum(src, seg, n):
    return jax.ops.segment_sum(src, seg, n)
kernel_name = 'mk_gps_d1_gnn_r32_7830a0'

def setup_inputs(seed: int=0):
    np.random.seed(seed)
    _w = jnp.asarray

    def _rec_inputs():
        import jax
        import jax.numpy as jnp
        _gk = jax.random.key(seed)
        x = -0.0003713 + 1 * jax.random.normal(jax.random.fold_in(_gk, 1), (3125, 256), jnp.float32)
        _s = jax.random.randint(jax.random.fold_in(_gk, 2), (25000,), 0, 3125, jnp.int32)
        _d = jax.random.randint(jax.random.fold_in(_gk, 3), (25000,), 0, 3125, jnp.int32)
        _loop = jnp.arange(3125, dtype=jnp.int32)
        src = jnp.concatenate([_s, _d, _loop])
        dst = jnp.concatenate([_d, _s, _loop])
        _o = jnp.argsort(dst, stable=True)
        src = src[_o]
        dst = dst[_o]
        edge_type_64 = jax.random.randint(jax.random.fold_in(_gk, 12), (53125,), 0, 64, jnp.int32)
        return (x, src, dst, edge_type_64)
    x, src, dst, edge_type_64 = _rec_inputs()

    def _L0_gnn_setup():
        import jax, jax.numpy as jnp
        import numpy as np
        N_NODES = 50000
        N_EDGES = 15625
        IN_DIM = 256
        HID = 64
        HEADS = 4
        N_REL = 64
        key = jax.random.key(seed)
        ks = jax.random.split(key, 16)
        s = 0.02
        return {'node_features': jax.random.normal(ks[0], (N_NODES, IN_DIM), jnp.float32), 'edge_index': jax.random.randint(ks[1], (2, N_EDGES), 0, N_NODES, jnp.int32), 'edge_relations': jax.random.randint(ks[2], (N_EDGES,), 0, N_REL, jnp.int32), 'query_emb': jax.random.normal(ks[3], (IN_DIM,), jnp.float32), 'Wq': jax.random.normal(ks[4], (IN_DIM, HID * HEADS), jnp.float32) * s, 'bq': jnp.zeros((HID * HEADS,), jnp.float32), 'Wk': jax.random.normal(ks[5], (IN_DIM, HID * HEADS), jnp.float32) * s, 'bk': jnp.zeros((HID * HEADS,), jnp.float32), 'Wv': jax.random.normal(ks[6], (IN_DIM, HID * HEADS), jnp.float32) * s, 'bv': jnp.zeros((HID * HEADS,), jnp.float32), 'rel_w': jax.random.normal(ks[7], (N_REL, HID), jnp.float32) * s, 'Wo': jax.random.normal(ks[8], (HID * HEADS, IN_DIM), jnp.float32) * s, 'bo': jnp.zeros((IN_DIM,), jnp.float32), 'gamma': jnp.ones((IN_DIM,), jnp.float32), 'beta': jnp.zeros((IN_DIM,), jnp.float32)}
    _L0_gnn_all = _L0_gnn_setup()
    _L0_gnn_in = {k: v for k, v in _L0_gnn_all.items() if k in ('query_emb', 'Wq', 'bq', 'Wk', 'bk', 'Wv', 'bv', 'rel_w', 'Wo', 'bo', 'gamma', 'beta')}
    del _L0_gnn_all

    def _L0_mix_setup():
        import jax, jax.numpy as jnp
        import numpy as np
        NUM_HEADS = 8
        key = jax.random.key(seed)
        ks = jax.random.split(key, 5)
        B, N, C = (8, 512, 256)
        x = jax.random.normal(ks[0], (B, N, C), dtype=jnp.float32)
        Wq = jax.random.normal(ks[1], (C, C), dtype=jnp.float32) * 0.02
        Wkv = jax.random.normal(ks[2], (2 * C, C), dtype=jnp.float32) * 0.02
        Wproj = jax.random.normal(ks[3], (C, C), dtype=jnp.float32) * 0.02
        bproj = jnp.zeros((C,), dtype=jnp.float32)
        return {'x': x, 'Wq': Wq, 'Wkv': Wkv, 'Wproj': Wproj, 'bproj': bproj}
    _L0_mix_all = _L0_mix_setup()
    _L0_mix_in = {k: v for k, v in _L0_mix_all.items() if k in ('Wq', 'Wkv', 'Wproj', 'bproj')}
    del _L0_mix_all

    def _L0_ffn_setup():
        import jax, jax.numpy as jnp
        import numpy as np
        B, T, D, H, E = (16, 128, 256, 512, 8)
        key = jax.random.key(seed)
        ks = jax.random.split(key, 5)
        x = jax.random.normal(ks[0], (B, T, D), dtype=jnp.float32)
        gate_w = jax.random.normal(ks[1], (D, E), dtype=jnp.float32) * 0.02
        gate_b = jnp.zeros((E,), dtype=jnp.float32)
        W1 = jax.random.normal(ks[2], (E, D, H), dtype=jnp.float32) * 0.02
        b1 = jnp.zeros((E, H), dtype=jnp.float32)
        W2 = jax.random.normal(ks[3], (E, H, D), dtype=jnp.float32) * 0.02
        b2 = jnp.zeros((E, D), dtype=jnp.float32)
        return {'x': x, 'gate_w': gate_w, 'gate_b': gate_b, 'W1': W1, 'b1': b1, 'W2': W2, 'b2': b2}
    _L0_ffn_all = _L0_ffn_setup()
    _L0_ffn_in = {k: v for k, v in _L0_ffn_all.items() if k in ('gate_w', 'gate_b', 'W1', 'b1', 'W2', 'b2')}
    del _L0_ffn_all
    return {'x': x, 'src': src, 'dst': dst, 'edge_type_64': edge_type_64, 'L0_gnn_query_emb': _L0_gnn_in['query_emb'], 'L0_gnn_Wq': _L0_gnn_in['Wq'], 'L0_gnn_bq': _L0_gnn_in['bq'], 'L0_gnn_Wk': _L0_gnn_in['Wk'], 'L0_gnn_bk': _L0_gnn_in['bk'], 'L0_gnn_Wv': _L0_gnn_in['Wv'], 'L0_gnn_bv': _L0_gnn_in['bv'], 'L0_gnn_rel_w': _L0_gnn_in['rel_w'], 'L0_gnn_Wo': _L0_gnn_in['Wo'], 'L0_gnn_bo': _L0_gnn_in['bo'], 'L0_gnn_gamma': _L0_gnn_in['gamma'], 'L0_gnn_beta': _L0_gnn_in['beta'], 'L0_mix_Wq': _L0_mix_in['Wq'], 'L0_mix_Wkv': _L0_mix_in['Wkv'], 'L0_mix_Wproj': _L0_mix_in['Wproj'], 'L0_mix_bproj': _L0_mix_in['bproj'], 'L0_ffn_gate_w': _L0_ffn_in['gate_w'], 'L0_ffn_gate_b': _L0_ffn_in['gate_b'], 'L0_ffn_W1': _L0_ffn_in['W1'], 'L0_ffn_b1': _L0_ffn_in['b1'], 'L0_ffn_W2': _L0_ffn_in['W2'], 'L0_ffn_b2': _L0_ffn_in['b2']}

def reference(x, src, dst, edge_type_64, L0_gnn_query_emb, L0_gnn_Wq, L0_gnn_bq, L0_gnn_Wk, L0_gnn_bk, L0_gnn_Wv, L0_gnn_bv, L0_gnn_rel_w, L0_gnn_Wo, L0_gnn_bo, L0_gnn_gamma, L0_gnn_beta, L0_mix_Wq, L0_mix_Wkv, L0_mix_Wproj, L0_mix_bproj, L0_ffn_gate_w, L0_ffn_gate_b, L0_ffn_W1, L0_ffn_b1, L0_ffn_W2, L0_ffn_b2):
    import jax
    import jax.numpy as jnp

    def _L0_gnn_ref(node_features, edge_index, edge_relations, query_emb, Wq, bq, Wk, bk, Wv, bv, rel_w, Wo, bo, gamma, beta):
        import jax, jax.numpy as jnp
        import numpy as np
        N_NODES = 50000
        N_EDGES = 15625
        IN_DIM = 256
        HID = 64
        HEADS = 4
        N_REL = 64
        N = node_features.shape[0]
        D = rel_w.shape[1]
        H = Wq.shape[1] // D
        enh = node_features + 0.1 * query_emb[None, :]
        Q = (enh @ Wq + bq).reshape(N, H, D)
        K = (enh @ Wk + bk).reshape(N, H, D)
        V = (enh @ Wv + bv).reshape(N, H, D)
        src, dst = (edge_index[0], edge_index[1])
        rel = rel_w[edge_relations]
        mod_k = K[src] + 0.2 * rel[:, None, :]
        scores = jnp.einsum('ehd,ehd->eh', Q[dst], mod_k) / D ** 0.5
        seg_max = jax.ops.segment_max(scores, dst, num_segments=N)
        ex = jnp.exp(scores - seg_max[dst])
        denom = jax.ops.segment_sum(ex, dst, num_segments=N)
        w = ex / denom[dst]
        agg = jax.ops.segment_sum(w[:, :, None] * V[src], dst, num_segments=N)
        deg = jax.ops.segment_sum(jnp.ones((src.shape[0],), jnp.float32), dst, num_segments=N)
        msgs = jnp.where(deg[:, None, None] > 0, agg, V)
        out = msgs.reshape(N, H * D) @ Wo + bo
        x = out + node_features
        mu = jnp.mean(x, axis=-1, keepdims=True)
        var = jnp.var(x, axis=-1, keepdims=True)
        return (x - mu) / jnp.sqrt(var + 1e-05) * gamma + beta

    def _L0_mix_ref(x, Wq, Wkv, Wproj, bproj):
        import jax, jax.numpy as jnp
        import numpy as np
        NUM_HEADS = 8
        B, N, C = x.shape
        h = NUM_HEADS
        d = C // h
        q = jnp.einsum('bnc,oc->bno', x, Wq).reshape(B, N, h, d).transpose(0, 2, 1, 3)
        kv = jnp.einsum('bnc,oc->bno', x, Wkv).reshape(B, N, 2, h, d)
        k = kv[:, :, 0].transpose(0, 2, 1, 3)
        v = kv[:, :, 1].transpose(0, 2, 1, 3)
        q = jax.nn.elu(q) + 1.0
        k = jax.nn.elu(k) + 1.0
        k_sum = k.sum(axis=2)
        D_inv = 1.0 / jnp.maximum(jnp.einsum('bhnd,bhd->bhn', q, k_sum), 1e-06)
        context = jnp.einsum('bhnd,bhne->bhde', k, v)
        attn = jnp.einsum('bhnd,bhde->bhne', q, context) * D_inv[..., None]
        out = attn.transpose(0, 2, 1, 3).reshape(B, N, C)
        out = jnp.einsum('bnc,oc->bno', out, Wproj) + bproj
        return out

    def _L0_ffn_ref(x, gate_w, gate_b, W1, b1, W2, b2):
        import jax, jax.numpy as jnp
        import numpy as np
        B, T, D, H, E = (16, 128, 256, 512, 8)
        Bb, Tt, Dd = x.shape
        Ee = gate_w.shape[1]
        xf = x.reshape(-1, Dd)
        N = xf.shape[0]
        logits = xf @ gate_w + gate_b
        probs = jax.nn.softmax(logits, axis=-1)
        top2_vals, top2_idx = jax.lax.top_k(probs, 2)
        cw = jnp.zeros((N, Ee), dtype=xf.dtype).at[jnp.arange(N)[:, None], top2_idx].add(top2_vals)

        def step(acc, params):
            w1, bb1, w2, bb2, we = params
            h = jax.nn.gelu(xf @ w1 + bb1, approximate=False)
            y = h @ w2 + bb2
            return (acc + we[:, None] * y, None)
        out, _ = jax.lax.scan(step, jnp.zeros_like(xf), (W1, b1, W2, b2, cw.T))
        return out.reshape(Bb, Tt, Dd)
    edge_index = jnp.stack([src, dst])
    xn = _layernorm(x, axis=-1)
    x = x + _L0_gnn_ref(xn, edge_index, edge_type_64, L0_gnn_query_emb, L0_gnn_Wq, L0_gnn_bq, L0_gnn_Wk, L0_gnn_bk, L0_gnn_Wv, L0_gnn_bv, L0_gnn_rel_w, L0_gnn_Wo, L0_gnn_bo, L0_gnn_gamma, L0_gnn_beta) + _L0_mix_ref(xn[None], L0_mix_Wq, L0_mix_Wkv, L0_mix_Wproj, L0_mix_bproj)[0]
    x = x + _L0_ffn_ref(_layernorm(x, axis=-1)[None], L0_ffn_gate_w, L0_ffn_gate_b, L0_ffn_W1, L0_ffn_b1, L0_ffn_W2, L0_ffn_b2)[0]
    return x

_drawn_inputs = setup_inputs


def setup_inputs(seed=0):
    import zlib

    import numpy as np

    out = dict(_drawn_inputs(seed))
    spreads = {'L0_gnn_bq': (0.0, 0.8),
     'L0_gnn_bk': (0.0, 0.8),
     'L0_gnn_bv': (0.0, 0.5),
     'L0_gnn_bo': (0.0, 0.1),
     'L0_gnn_gamma': (1.0, 0.2),
     'L0_gnn_beta': (0.0, 0.1),
     'L0_mix_bproj': (0.0, 0.1),
     'L0_ffn_gate_b': (0.0, 0.8),
     'L0_ffn_b1': (0.0, 0.8),
     'L0_ffn_b2': (0.0, 0.627)}
    factors = {'L0_gnn_query_emb': 8.0,
     'L0_gnn_Wq': 8.0,
     'L0_gnn_Wk': 8.0,
     'L0_gnn_Wv': 4.122,
     'L0_gnn_rel_w': 8.0,
     'L0_gnn_Wo': 2.717,
     'L0_mix_Wq': 8.0,
     'L0_mix_Wkv': 8.0,
     'L0_mix_Wproj': 8.0,
     'L0_ffn_gate_w': 3.976,
     'L0_ffn_W1': 5.741,
     'L0_ffn_W2': 5.402}
    for name, (base, spread) in spreads.items():
        noise = np.random.default_rng([zlib.crc32(name.encode()), seed]).standard_normal(out[name].shape)
        drawn = base * np.exp(spread * noise) if base else spread * noise
        out[name] = jnp.asarray(drawn.astype(out[name].dtype))
    for name, factor in factors.items():
        out[name] = (out[name] * factor).astype(out[name].dtype)
    return out
```

```python
from contextlib import ExitStack

import concourse.bass as bass
from concourse import mybir

F32 = mybir.dt.float32
I32 = mybir.dt.int32
ALU = mybir.AluOpType
ACT = mybir.ActivationFunctionType
AX = mybir.AxisListType

P = 128
N = 3125
C = 256
NT = (N + P - 1) // P
E_REAL = 53125
ET = (E_REAL + P - 1) // P
H, D = 4, 64
NREL = 64
MD = 32
NS = ET + NT - 1
SC = 4
SP_ = NS // SC
G = 4
BIG = 1.0e30
EPS = 1.0e-5
NEXP, HID = 8, 512
PADDST = 4095
assert SC * SP_ == NS and NS % (2 * G) == 0


class Seq:

    def __init__(self, eng, sem, base=0, per=None):
        self.eng, self.sem, self.base, self.n, self.per = eng, sem, base, 0, per

    def __call__(self, ins):
        ins.then_inc(self.sem, 1)
        self.n += 1
        self.eng.wait_ge(self.sem, self.base + self.n)

    def close(self):
        assert self.per is None or self.n == self.per, (self.n, self.per)


def wait(eng, sem, count):
    if isinstance(count, int) and count <= 0:
        return
    eng.wait_ge(sem, count)


def phase_project(nc, sem, T, d):
    s_ld, s_x, s_v, s_a, s_t, s_tc, s_mm = (sem(n) for n in
        ("pj_loads", "pj_x", "pj_vector", "pj_scalar", "pj_transposed", "pj_xnT", "pj_products"))
    s_id, s_one, s_kv, s_ctx, s_e, s_sq, s_xn, s_kvb, s_k, s_mn, s_ev = (sem(n) for n in
        ("pj_iota", "pj_const", "pj_kv_stored", "pj_context", "pj_exp", "pj_sqrt", "pj_xn", "pj_kv_ready", "pj_k", "pj_min", "pj_evac"))
    X, W, WQM, rstd, nmr = T["X"], T["W"], T["WQM"], T["rstd"], T["nmr"]
    stats, xnb, xnT, kvb, mn, ex, kb, vb = (T[n] for n in ("stats", "xnb", "xnT", "kvb", "mn", "ex", "kb", "vb"))
    ps_t, ps_n, ps_q, ps_c = T["ps_t"], T["ps_n"], T["ps_q"], T["ps_c"]
    NLOAD = 8 + 4 + 1
    with nc.Block() as block:
        @block.sync
        def _(sp):
            for t in range(0, NT, 5):
                sp.dma_start(X[:, t:t + 5, :], d["x"][t * P:(t + 5) * P, :].rearrange("(t p) c -> p t c", p=P)).then_inc(s_x, 16)
            for j, n in enumerate(("g_Wq", "g_Wk", "g_Wv")):
                sp.dma_start(W[:, :, j * C:(j + 1) * C], d[n].rearrange("(k p) n -> p k n", p=P)).then_inc(s_ld, 16)
            sp.dma_start(W[:, :, 3 * C:5 * C], d["m_WkvT"].rearrange("(k p) n -> p k n", p=P)).then_inc(s_ld, 16)
            sp.dma_start(WQM[:, :, :], d["m_WqT"].rearrange("(k p) n -> p k n", p=P)).then_inc(s_ld, 16)
            for j, n in enumerate(("g_bq", "g_bk", "g_bv")):
                sp.dma_start(T["brow"][0:1, j * C:(j + 1) * C], d[n].rearrange("(a n) -> a n", a=1)).then_inc(s_ld, 16)
            for k in range(2):
                sp.dma_start(T["qe"][:, k:k + 1], d["g_query"][k * P:(k + 1) * P].rearrange("(p a) -> p a", a=1)).then_inc(s_ld, 16)
            with sp.Fori(0, NT, 1) as i:
                sp.wait_ge(s_kvb, 2 * i + 2)
                sp.dma_start(d["ktab"][bass.ds(i * P, P), :], kvb[:, 0:C]).then_inc(s_kv, 16)
                sp.dma_start(d["vtab"][bass.ds(i * P, P), :], kvb[:, C:2 * C]).then_inc(s_kv, 16)
            sp.wait_ge(s_kv, 32 * NT)

        @block.gpsimd
        def _(pool):
            pool.iota(T["iota_i"][:, :], [[1, P]], base=0, channel_multiplier=0).then_inc(s_id, 1)
            pool.iota(T["iota_pi"][:, :], [[1, 1]], base=0, channel_multiplier=1).then_inc(s_id, 1)
            pool.iota(T["node_i"][:, :], [[P, NT]], base=0, channel_multiplier=1).then_inc(s_id, 1)

        @block.vector
        def _(v):
            q = Seq(v, s_v)
            v.memset(T["onesr"][:, :], 1.0).then_inc(s_one, 1)
            v.memset(T["zero"][:, :], 0.0).then_inc(s_one, 1)
            v.wait_ge(s_id, 3)
            q(v.tensor_copy(T["iota_f"][:, :], T["iota_i"][:, :]))
            q(v.tensor_copy(T["iota_p"][:, :], T["iota_pi"][:, :]))
            q(v.tensor_copy(T["mask"][:, :], T["node_i"][:, :]))
            q(v.tensor_scalar(T["mask"][:, :], T["mask"][:, :], float(N), None, ALU.is_lt))
            v.tensor_scalar(T["ident"][:, :], T["iota_f"][:, :], T["iota_p"][:, 0:1], None, ALU.is_equal).then_inc(s_one, 1)
            for t in range(NT):
                if t % 5 == 0:
                    v.wait_ge(s_x, 80)
                q(v.bn_stats(stats[:, 0:6], X[:, t, :]))
                q(v.bn_aggr(T["mv"][:, t, :], stats[:, 0:6]))
            q(v.tensor_scalar(rstd[:, :], T["mv"][:, :, 1], EPS, None, ALU.add))
            v.engine_nop().then_inc(s_sq, 1)
            v.wait_ge(s_a, 1)
            q(v.reciprocal(rstd[:, :], rstd[:, :]))
            q(v.tensor_tensor(nmr[:, :], T["mv"][:, :, 0], rstd[:, :], ALU.mult))
            q(v.tensor_scalar(nmr[:, :], nmr[:, :], -1.0, None, ALU.mult))
            v.wait_ge(s_ld, 16 * 10)
            q(v.tensor_scalar(T["qe"][:, :], T["qe"][:, :], 0.1, None, ALU.mult))
            v.wait_ge(s_one, 3)
            for k in range(2):
                q(v.tensor_scalar(T["qbc"][:, k, :], T["onesr"][:, :], T["qe"][:, k:k + 1], None, ALU.mult))
            v.engine_nop().then_inc(s_sq, 1)
            v.wait_ge(s_mm, 1)
            q(v.tensor_copy(T["bias"][:, 0:512], ps_n[:, 0, :]))
            q(v.tensor_copy(T["bias"][:, 512:768], ps_n[:, 1, 0:256]))
            q(v.tensor_scalar(T["bias"][:, 0:C], T["bias"][:, 0:C], 0.125, None, ALU.mult))
            n0 = q.n
            v.memset(T["vb"][:, :, :], 0.0).then_inc(s_v, 1)
            n0 += 1
            def tile(i):
                q = Seq(v, s_v, i * 3 + n0, 3)
                wait(v, s_t, i)
                v.tensor_scalar(xnb[:, :], X[:, bass.ds(i, 1), :].rearrange("p a c -> p (a c)"), rstd[:, bass.ds(i, 1)],
                                nmr[:, bass.ds(i, 1)], ALU.mult, ALU.add).then_inc(s_xn, 1)
                v.wait_ge(s_mm, i + 2)
                v.scalar_tensor_tensor(out=T["QN"][:, bass.ds(i * C, C)], in0=ps_n[:, 0, 0:C], scalar=0.125,
                                       in1=T["bias"][:, 0:C], op0=ALU.mult, op1=ALU.add).then_inc(s_ev, 1)
                wait(v, s_kv, i * 32)
                v.tensor_tensor(kvb[:, 0:C], ps_n[:, 0, C:2 * C], T["bias"][:, C:2 * C], ALU.add).then_inc(s_kvb, 1)
                v.tensor_tensor(kvb[:, C:2 * C], ps_n[:, 1, 0:C], T["bias"][:, 2 * C:3 * C], ALU.add).then_inc(s_kvb, 1)
                wait(v, s_e, i)
                v.tensor_scalar(mn[:, 0:C], ps_n[:, 1, C:2 * C], 0.0, None, ALU.min).then_inc(s_mn, 1)
                v.tensor_scalar(mn[:, C:2 * C], ps_q[:, 0:C], 0.0, None, ALU.min).then_inc(s_mn, 1)
                wait(v, s_ctx, i)
                q(v.tensor_copy(vb[:, :, 0:P], ps_n[:, 2, 0:C].rearrange("p (a c) -> p a c", a=2)))
                v.wait_ge(s_e, i + 1)
                q(v.scalar_tensor_tensor(out=kb[:, :], in0=ps_n[:, 1, C:2 * C], scalar=0.0, in1=ex[:, 0:C], op0=ALU.max, op1=ALU.add))
                q(v.scalar_tensor_tensor(out=T["QT"][:, :, bass.ds(i * P, P)], in0=ps_q[:, 0:C].rearrange("p (a c) -> p a c", a=2),
                                         scalar=0.0, in1=ex[:, C:2 * C].rearrange("p (a c) -> p a c", a=2), op0=ALU.max, op1=ALU.add))
                q.close()
                v.tensor_copy(vb[:, :, P:P + 1], T["mask"][:, bass.ds(i, 1)].unsqueeze(1).broadcast_to([P, 2, 1])).then_inc(s_k, 1)

            tile(0)
            with v.Fori(1, NT, 1) as i:
                tile(i)
            v.wait_ge(s_ctx, NT + 1)
            q = Seq(v, s_v, n0 + 3 * NT)
            q(v.tensor_copy(T["CTX"][:, :, :], ps_c[:, :, :]))

        @block.scalar
        def _(a):
            a.wait_ge(s_sq, 1)
            a.activation(rstd[:, :], rstd[:, :], ACT.Sqrt).then_inc(s_a, 1)
            with a.Fori(0, NT, 1) as i:
                a.wait_ge(s_t, i + 1)
                a.copy(xnT[:, :, :], ps_t[:, :, :]).then_inc(s_tc, 1)
                a.wait_ge(s_mn, 2 * i + 2)
                a.activation(ex[:, :], mn[:, :], ACT.Exp).then_inc(s_e, 1)

        @block.tensor
        def _(pe):
            pe.wait_ge(s_one, 3)
            pe.wait_ge(s_ld, 160)
            pe.wait_ge(s_sq, 2)
            for b, (c0, c1) in enumerate(((0, 512), (512, 768))):
                for k in range(2):
                    pe.matmul(ps_n[:, b, 0:c1 - c0], T["qbc"][:, k, :], W[:, k, c0:c1], start=(k == 0), stop=False)
                m = pe.matmul(ps_n[:, b, 0:c1 - c0], T["onesr"][0:1, :], T["brow"][0:1, c0:c1], start=False, stop=True)
            m.then_inc(s_mm, 1)
            for a in range(2):
                pe.matmul(ps_c[:, a, :], T["zero"][:, 0:P], T["zero"][:, 0:P + 1], start=True, stop=False, skip_group_check=True)
            def tile(i):
                pe.wait_ge(s_xn, i + 1)
                pe.transpose(ps_t[:, 0, :], xnb[:, 0:P], T["ident"][:, :])
                pe.transpose(ps_t[:, 1, :], xnb[:, P:C], T["ident"][:, :]).then_inc(s_t, 1)
                pe.wait_ge(s_tc, i + 1)
                wait(pe, s_k, i)
                for b, (c0, c1) in enumerate(((0, 512), (512, 1024), (1024, 1280))):
                    for k in range(2):
                        pe.matmul(ps_n[:, b, 0:c1 - c0], xnT[:, k, :], W[:, k, c0:c1], start=(k == 0), stop=(k == 1))
                for o in range(2):
                    for k in range(2):
                        m = pe.matmul(ps_q[:, o * P:(o + 1) * P], WQM[:, k, o * P:(o + 1) * P], xnT[:, k, :],
                                      start=(k == 0), stop=(k == 1))
                m.then_inc(s_mm, 1)
                pe.wait_ge(s_k, i + 1)
                for a in range(2):
                    m = pe.matmul(ps_c[:, a, :], kb[:, a * P:(a + 1) * P], vb[:, a, :], start=False, stop=False, skip_group_check=True)
                m.then_inc(s_ctx, 1)

            tile(0)
            with pe.Fori(1, NT, 1) as i:
                tile(i)
            for a in range(2):
                m = pe.matmul(ps_c[:, a, :], T["zero"][:, 0:P], T["zero"][:, 0:P + 1], start=False, stop=True, skip_group_check=True)
            m.then_inc(s_ctx, 1)


def phase_steps(nc, sem, T, d):
    s_ld, s_v, s_io, s_pe, s_cp, s_g, s_st, s_rdy, s_tr, s_ev = (sem("st_" + n) for n in
        ("loads", "vector", "iota", "products", "copied", "gathered", "stored", "ready", "transposed", "evac"))
    EI, rows, DL = T["EI"], T["rows"], T["DL"]
    with nc.Block() as block:
        @block.sync
        def _(sp):
            sp.dma_start(T["last_i"][0:1, :], d["edges"][:, P - 1:P].rearrange("t a -> a t"), allow_slow_non_contiguous=True).then_inc(s_ld, 16)
            sp.wait_ge(s_rdy, 2)
            for c in range(SC):
                sp.dma_start(d["dl_rows"][c * SP_:(c + 1) * SP_, :], DL[0:SP_, c, :]).then_inc(s_st, 16)
                sp.dma_start(d["ty_rows"][c * SP_:(c + 1) * SP_, :], rows[0:SP_, c, :]).then_inc(s_st, 16)
            sp.wait_ge(s_st, 2 * SC * 16)

        @block.gpsimd
        def _(pool):
            pool.iota(T["t_i"][0:1, :], [[1, ET]], base=0, channel_multiplier=0).then_inc(s_io, 1)
            pool.iota(T["s_i"][:, :], [[SP_, SC]], base=0, channel_multiplier=1).then_inc(s_io, 1)
            pool.wait_ge(s_cp, 1)
            for c in range(SC):
                pool.indirect_dma_start(EI[0:SP_, c, :], None, d["edges"], bass.IndirectOffsetOnAxis(ap=T["tI"][0:SP_, c:c + 1], axis=0)).then_inc(s_g, 16)

        @block.vector
        def _(v):
            q = Seq(v, s_v)
            v.wait_ge(s_ld, 16)
            v.wait_ge(s_io, 2)
            q(v.tensor_scalar(T["last_i"][0:1, :], T["last_i"][0:1, :], 7, None, ALU.logical_shift_right))
            q(v.tensor_copy(T["hi"][0:1, :], T["last_i"][0:1, :]))
            q(v.tensor_scalar(T["hi"][0:1, :], T["hi"][0:1, :], float(NT - 1), None, ALU.min))
            q(v.tensor_copy(T["st"][0:1, :], T["t_i"][0:1, :]))
            v.tensor_tensor(T["st"][0:1, 1:ET], T["st"][0:1, 1:ET], T["hi"][0:1, 0:ET - 1], ALU.add).then_inc(s_rdy, 1)
            q(v.tensor_copy(T["s_f"][:, :], T["s_i"][:, :]))
            v.wait_ge(s_pe, 1)
            for c in range(SC):
                q(v.tensor_scalar(T["junk"][:, :], T["ps_a"][:, 0:ET], T["s_f"][:, c:c + 1], None, ALU.is_le, ALU.add,
                                  accum_out=T["cnt"][:, c:c + 1]))
            q(v.tensor_scalar(T["cnt"][:, :], T["cnt"][:, :], -1.0, None, ALU.add))
            q(v.tensor_tensor(T["bS"][:, :], T["s_f"][:, :], T["cnt"][:, :], ALU.subtract))
            v.tensor_copy(T["tI"][:, :], T["cnt"][:, :]).then_inc(s_cp, 1)
            q(v.tensor_scalar(T["b128"][:, :], T["bS"][:, :], float(P), None, ALU.mult))
            v.wait_ge(s_pe, 2)
            q(v.tensor_copy(T["bRow"][0:1, :], T["ps_a"][0:1, 0:NS]))
            v.wait_ge(s_g, 16 * SC)
            R = SP_
            for c in range(SC):
                q(v.tensor_copy(DL[0:R, c, :], EI[0:R, c, 0:P]))
                q(v.tensor_scalar(DL[0:R, c, :], DL[0:R, c, :], T["b128"][0:R, c:c + 1], -1.0, ALU.subtract, ALU.max))
                q(v.tensor_scalar(DL[0:R, c, :], DL[0:R, c, :], float(P), None, ALU.min))
                q(v.tensor_scalar(T["valid"][0:R, c, :], DL[0:R, c, :], 0.0, None, ALU.is_ge))
                q(v.tensor_scalar(T["junk"][0:R, 0:P], DL[0:R, c, :], float(P), None, ALU.is_lt))
                q(v.tensor_tensor(T["valid"][0:R, c, :], T["valid"][0:R, c, :], T["junk"][0:R, 0:P], ALU.mult))
                for nb, pen in ((1, "penf"), (2, "penb")):
                    q(v.tensor_tensor(T[pen][0:R, c, :], EI[0:R, c, 0:P], EI[0:R, c, nb * P:(nb + 1) * P], ALU.not_equal))
                    q(v.tensor_tensor(T[pen][0:R, c, :], T[pen][0:R, c, :], T["valid"][0:R, c, :], ALU.mult))
                    q(v.tensor_scalar(T[pen][0:R, c, :], T[pen][0:R, c, :], -BIG, None, ALU.mult))
                q(v.tensor_scalar(T["valid"][0:R, c, :], T["valid"][0:R, c, :], -1.0, BIG, ALU.add, ALU.mult))
                q(v.tensor_copy(T["srow"][0:R, c, :], EI[0:R, c, 3 * P:4 * P]))
                q(v.tensor_copy(rows[0:R, c, :], EI[0:R, c, 4 * P:5 * P]))
            v.engine_nop().then_inc(s_rdy, 1)
            v.wait_ge(s_pe, 3)
            q(v.tensor_copy(T["SRC"][:, :], T["ps_a"][:, 0:NS]))
            q(v.tensor_copy(T["DC"][:, :], T["ps_b"][:, 0:NS]))

        @block.tensor
        def _(pe):
            pe.wait_ge(s_rdy, 1)
            pe.matmul(T["ps_a"][:, 0:ET], T["onesr"][0:1, :], T["st"][0:1, :], start=True, stop=True).then_inc(s_pe, 1)
            pe.wait_ge(s_v, 12)
            for c in range(SC):
                m = pe.transpose(T["ps_a"][0:1, c * SP_:(c + 1) * SP_], T["bS"][0:SP_, c:c + 1], T["ident"][0:SP_, 0:SP_])
            m.then_inc(s_pe, 1)
            pe.wait_ge(s_rdy, 2)
            for c in range(SC):
                pe.transpose(T["ps_a"][:, c * SP_:(c + 1) * SP_], T["srow"][0:SP_, c, :], T["ident"][0:SP_, 0:SP_])
                m = pe.transpose(T["ps_b"][:, c * SP_:(c + 1) * SP_], DL[0:SP_, c, :], T["ident"][0:SP_, 0:SP_])
            m.then_inc(s_pe, 1)


def phase_scores(nc, sem, T, d):
    s_bc = [sem(f"sc_rows{h}") for h in range(2)]
    s_g = [[sem(f"sc_gathered{h}{k}") for k in range(G)] for h in range(2)]
    s_ix, s_oh, s_q, s_ku, s_pr, s_done, s_ld, s_rel = (sem("sc_" + n) for n in
        ("indices", "onehots", "products", "modified", "multiplied", "reduced", "loads", "relations"))
    NIT = NS // (2 * G)
    with nc.Block() as block:
        @block.sync
        def _(sp):
            sp.dma_start(T["rel"][:, :], d["g_rel_w"]).then_inc(s_ld, 16)

            def group(j, h):
                wait(sp, s_oh, 2 * (j * 2 + h) - 2)
                s0 = (j * 2 + h) * G
                sp.dma_start(T["dlb"][:, h, :], d["dl_rows"][bass.ds(s0, G), :].rearrange("s e -> (s e)").unsqueeze(0).broadcast_to([P, G * P])).then_inc(s_bc[h], 16)
                sp.dma_start(T["tyb"][:, h, :], d["ty_rows"][bass.ds(s0, G), :].rearrange("s e -> (s e)").unsqueeze(0).broadcast_to([NREL, G * P])).then_inc(s_bc[h], 16)
            group(0, 0)
            group(0, 1)
            with sp.Fori(1, NIT, 1) as j:
                group(j, 0)
                group(j, 1)

        @block.scalar
        def _(a):
            def group(j, h):
                wait(a, s_ku, 2 * j + h - 1)
                a.copy(T["ixs"][:, h, :], T["SRC"][:, bass.ds((2 * j + h) * G, G)]).then_inc(s_ix, 1)
            group(0, 0)
            group(0, 1)
            with a.Fori(1, NIT, 1) as j:
                group(j, 0)
                group(j, 1)

        @block.gpsimd
        def _(pool):
            with pool.Fori(0, NIT, 1) as j:
                for h in range(2):
                    pool.wait_ge(s_ix, 2 * j + h + 1)
                    pool.nop(nofuse=True)
                    for k in range(G):
                        pool.indirect_dma_start(T["KG"][:, (h * G + k) * C:(h * G + k + 1) * C], None, d["ktab"],
                                                bass.IndirectOffsetOnAxis(ap=T["ixs"][:, h, k:k + 1], axis=0)).then_inc(s_g[h][k], 16)

        @block.tensor
        def _(pe):
            pe.wait_ge(s_rel, 1)

            def group(j, h):
                g = 2 * j + h
                pe.wait_ge(s_oh, 2 * g + 2)
                wait(pe, s_pr, g - 1)
                with ExitStack() as regs:
                    for k in range(G):
                        b = pe.value_load(T["bRow"][0:1, bass.ds(g * G + k, 1)], min_val=0, max_val=NT - 1)
                        pe.matmul(T["ps_qe"][:, h, k, :], T["PT"][:, h, k * P:(k + 1) * P], T["QN"][:, bass.ds(b * C, C)], start=True, stop=True)
                        m = pe.matmul(T["ps_u"][:, h, k, :], T["OT"][:, h, k * P:(k + 1) * P], T["rel"][:, :], start=True, stop=True)
                m.then_inc(s_q, 1)
            group(0, 0)
            group(0, 1)
            with pe.Fori(1, NIT, 1) as j:
                group(j, 0)
                group(j, 1)

        @block.vector
        def _(v):
            v.wait_ge(s_ld, 16)
            v.tensor_scalar(T["rel"][:, :], T["rel"][:, :], 0.2, None, ALU.mult).then_inc(s_rel, 1)

            def group(j, h):
                g = 2 * j + h
                v.wait_ge(s_bc[h], 32 * j + 32)
                wait(v, s_q, g - 1)
                v.tensor_scalar(T["PT"][:, h, :], T["dlb"][:, h, :], T["iota_p"][:, 0:1], None, ALU.is_equal).then_inc(s_oh, 1)
                v.tensor_scalar(T["OT"][:, h, :], T["tyb"][:, h, :], T["iota_p"][0:NREL, 0:1], None, ALU.is_equal).then_inc(s_oh, 1)

            def finish(j, h):
                g = 2 * j + h
                for k in range(G):
                    v.wait_ge(s_g[h][k], 16 * j + 16)
                v.wait_ge(s_q, g + 1)
                KG = T["KG"][:, h * G * C:(h + 1) * G * C]
                v.tensor_tensor(T["KU"][:, :].rearrange("p (s h d) -> p s h d", s=G, h=H), KG.rearrange("p (s h d) -> p s h d", s=G, h=H),
                                T["ps_u"][:, h, :, :].unsqueeze(2).broadcast_to([P, G, H, D]), ALU.add).then_inc(s_ku, 1)
                v.wait_ge(s_ku, g + 1)
                v.tensor_tensor(T["KU"][:, :], T["KU"][:, :], T["ps_qe"][:, h, :, :].rearrange("p s c -> p (s c)"), ALU.mult).then_inc(s_pr, 1)
                v.wait_ge(s_pr, g + 1)
                v.tensor_reduce(T["S"][:, bass.ds(g * G * H, G * H)], T["KU"][:, :].rearrange("p (x d) -> p x d", d=D), AX.X, ALU.add).then_inc(s_done, 1)
                v.wait_ge(s_done, g + 1)
            group(0, 0)
            group(0, 1)
            finish(0, 0)
            with v.Fori(1, NIT, 1) as j:
                group(j, 0)
                finish(j - 1, 1)
                group(j, 1)
                finish(j, 0)
            finish(NIT - 1, 1)
def phase_softmax_weights(nc, sem, T, d):
    s_v, s_pe, s_in, s_lr, s_e, s_c, s_x, s_ev = (sem("sm_" + n) for n in
        ("vector", "rows", "ready", "ends", "ends_turned", "carry", "exp", "evac"))
    R, B = SP_, SC * H
    ST, SX, F, penL, LR, E4, CR = (T[n] for n in ("ST", "SX", "F", "penL", "LR", "E4", "CR"))
    S4 = T["S"][:, :].rearrange("p (c s h) -> p c h s", c=SC, h=H)

    def flat(t):
        return t[0:R, :, :].rearrange("p b e -> p (b e)")

    def by_head(pen):
        return pen[0:R, :, :].unsqueeze(2).broadcast_to([R, SC, H, P])

    with nc.Block() as block:
        @block.tensor
        def _(pe):
            for c in range(SC):
                for h in range(H):
                    m = pe.transpose(T["ps_s"][0:R, c, h * P:(h + 1) * P], S4[:, c, h, :], T["ident"][:, :])
            m.then_inc(s_pe, 1)
            for w in range(2):
                pe.wait_ge(s_lr, w + 1)
                for x in range(2):
                    for c in range(SC):
                        m = pe.transpose(T["ps_e"][0:H, x, c * SP_:(c + 1) * SP_], LR[0:R, x, c * H:(c + 1) * H], T["ident"][0:R, 0:R])
                m.then_inc(s_e, 1)
                pe.wait_ge(s_c, w + 1)
                for c in range(SC):
                    m = pe.transpose(T["ps_c2"][0:R, c * H:(c + 1) * H], CR[0:H, c * SP_:(c + 1) * SP_], T["ident"][0:H, 0:H])
                m.then_inc(s_pe, 1)
            pe.wait_ge(s_x, 1)
            for c in range(SC):
                for h in range(H):
                    m = pe.transpose(T["ps_s"][:, c, h * P:h * P + R], ST[0:R, c * H + h, :], T["ident"][0:R, 0:R])
            m.then_inc(s_pe, 1)

        @block.scalar
        def _(a):
            a.wait_ge(s_in, 1)
            a.activation(ST[0:R, :, :], ST[0:R, :, :], ACT.Exp).then_inc(s_x, 1)

        @block.vector
        def _(v):
            q = Seq(v, s_v)
            v.wait_ge(s_pe, 1)
            q(v.tensor_tensor(ST[0:R, :, :].rearrange("p (c h) e -> p c h e", h=H), T["ps_s"][0:R, :, :].rearrange("p c (h e) -> p c h e", h=H),
                              by_head(T["valid"]), ALU.add))
            q(v.tensor_copy(flat(SX), flat(ST)))

            def direction(w, src, out, pen, edge, end, order):
                q(v.tensor_copy(penL[0:R, :, :].rearrange("p (c h) e -> p c h e", h=H), by_head(pen)))
                q(v.memset(penL[0:R, :, edge:edge + 1], -BIG))
                q(v.tensor_tensor_scan(order(out), order(penL), order(src), -BIG, ALU.add, ALU.max))
                q(v.tensor_copy(LR[0:R, 0, :], out[0:R, :, end]))
                q(v.tensor_reduce(T["rp"][0:R, :], pen[0:R, :, :], AX.X, ALU.min))
                v.tensor_copy(LR[0:R, 1, :].rearrange("p (c h) -> p c h", h=H),
                              T["rp"][0:R, :].unsqueeze(2).broadcast_to([R, SC, H])).then_inc(s_lr, 1)
                v.wait_ge(s_e, w + 1)
                q(v.tensor_copy(T["E2"][0:H, :, :], T["ps_e"][0:H, :, 0:NS]))
                if w == 0:
                    q(v.tensor_tensor_scan(E4[0:H, :], T["E2"][0:H, 1, :], T["E2"][0:H, 0, :], -BIG, ALU.add, ALU.max))
                    q(v.memset(CR[0:H, 0:1], -BIG))
                    v.tensor_copy(CR[0:H, 1:NS], E4[0:H, 0:NS - 1]).then_inc(s_c, 1)
                else:
                    q(v.tensor_tensor_scan(E4[0:H, ::-1], T["E2"][0:H, 1, ::-1], T["E2"][0:H, 0, ::-1], -BIG, ALU.add, ALU.max))
                    q(v.memset(CR[0:H, NS - 1:NS], -BIG))
                    v.tensor_copy(CR[0:H, 0:NS - 1], E4[0:H, 1:NS]).then_inc(s_c, 1)
                v.wait_ge(s_pe, w + 2)
                q(v.tensor_tensor(T["inj"][0:R, :].rearrange("p (c h) -> p c h", h=H), T["ps_c2"][0:R, :].rearrange("p (c h) -> p c h", h=H),
                                  pen[0:R, :, edge:edge + 1].broadcast_to([R, SC, H]), ALU.add))
                q(v.tensor_tensor(src[0:R, :, edge], src[0:R, :, edge], T["inj"][0:R, :], ALU.max))
                q(v.tensor_tensor_scan(order(out), order(penL), order(src), -BIG, ALU.add, ALU.max))

            direction(0, SX, F, T["penf"], 0, P - 1, flat)
            direction(1, F, SX, T["penb"], P - 1, 0, lambda t: flat(t)[:, ::-1])
            v.tensor_tensor(flat(ST), flat(ST), flat(SX), ALU.subtract).then_inc(s_in, 1)
            v.wait_ge(s_pe, 4)
            for c in range(SC):
                q(v.tensor_copy(S4[:, c, :, :], T["ps_s"][:, c, :].rearrange("p (h s) -> p h s", h=H)[:, :, 0:R]))


def phase_aggregate(nc, sem, T, d):
    s_g = [[sem(f"ag_gathered{h}{k}") for k in range(G)] for h in range(2)]
    s_ix, s_oh, s_w, s_o, s_acc = (sem("ag_" + n) for n in ("indices", "onehots", "weighted", "products", "added"))
    NIT = NS // (2 * G)
    A = C + H
    with nc.Block() as block:
        @block.scalar
        def _(a):
            def group(j, h):
                wait(a, s_w, 2 * j + h - 1)
                a.copy(T["ixv"][:, h, :], T["SRC"][:, bass.ds((2 * j + h) * G, G)]).then_inc(s_ix, 1)
            group(0, 0)
            group(0, 1)
            with a.Fori(1, NIT, 1) as j:
                group(j, 0)
                group(j, 1)

        @block.gpsimd
        def _(pool):
            with pool.Fori(0, NIT, 1) as j:
                for h in range(2):
                    pool.wait_ge(s_ix, 2 * j + h + 1)
                    pool.nop(nofuse=True)
                    for k in range(G):
                        pool.indirect_dma_start(T["VG"][:, (h * G + k) * C:(h * G + k + 1) * C], None, d["vtab"],
                                                bass.IndirectOffsetOnAxis(ap=T["ixv"][:, h, k:k + 1], axis=0)).then_inc(s_g[h][k], 16)

        @block.tensor
        def _(pe):
            def group(j, h):
                g = 2 * j + h
                pe.wait_ge(s_oh, (g + 1) * G)
                pe.wait_ge(s_w, g + 1)
                wait(pe, s_acc, (g - 1) * G)
                for k in range(G):
                    o = T["ps_o"][:, h * G + k, :]
                    lhs = T["PM"][:, h, k, :]
                    pe.matmul(o[:, 0:C], lhs, T["WV"][:, h, k * C:(k + 1) * C], start=True, stop=True)
                    pe.matmul(o[:, C:A], lhs, T["S"][:, bass.ds((g * G + k) * H, H)], start=True, stop=True).then_inc(s_o, 1)
            group(0, 0)
            group(0, 1)
            with pe.Fori(1, NIT, 1) as j:
                group(j, 0)
                group(j, 1)

        @block.vector
        def _(v):
            v.memset(T["ACC"][:, :], 0.0).then_inc(s_acc, 1)

            def onehots(j, h):
                g = 2 * j + h
                wait(v, s_o, (g - 1) * G)
                for k in range(G):
                    v.tensor_scalar(T["PM"][:, h, k, :], T["iota_f"][:, :], T["DC"][:, bass.ds(g * G + k, 1)], None, ALU.is_equal).then_inc(s_oh, 1)
                for k in range(G):
                    v.wait_ge(s_g[h][k], 16 * j + 16)
                v.tensor_tensor(T["WV"][:, h, :].rearrange("p (x d) -> p x d", d=D),
                                T["VG"][:, h * G * C:(h + 1) * G * C].rearrange("p (x d) -> p x d", d=D),
                                T["S"][:, bass.ds(g * G * H, G * H)].unsqueeze(2).broadcast_to([P, G * H, D]), ALU.mult).then_inc(s_w, 1)

            def add(j, h):
                g = 2 * j + h
                for k in range(G):
                    b = v.value_load(T["bRow"][0:1, bass.ds(g * G + k, 1)], min_val=0, max_val=NT - 1)
                    v.wait_ge(s_o, g * G + k + 1)
                    v.wait_ge(s_acc, g * G + k + 1)
                    acc = T["ACC"][:, bass.ds(b * A, A)]
                    v.tensor_tensor(acc, acc, T["ps_o"][:, h * G + k, 0:A], ALU.add).then_inc(s_acc, 1)
            onehots(0, 0)
            onehots(0, 1)
            add(0, 0)
            with v.Fori(1, NIT, 1) as j:
                onehots(j, 0)
                add(j - 1, 1)
                onehots(j, 1)
                add(j, 0)
            add(NIT - 1, 1)
def phase_combine(nc, sem, T, d):
    s_ld, s_w, s_vt, s_i, s_v, s_c, s_pe, s_ct, s_m, s_a, s_t, s_tc, s_y, s_q, s_sq, s_g, s_xf, s_nd, s_ra, s_gl = (sem("cb_" + n) for n in
        ("loads", "weights", "v_rows", "iota", "vector", "context", "context_turned", "context_copied", "mix_matrix", "scalar",
         "turned", "turned_copied", "rows", "mixed", "variance", "gates", "normed", "denominators", "reciprocals", "logits"))
    A = C + H
    X, rstd, nmr, QT, ACC, Y = (T[n] for n in ("X", "rstd", "nmr", "QT", "ACC", "Y"))
    CH = [(n0, min(512, NT * P - n0)) for n0 in range(0, NT * P, 512)]
    with nc.Block() as block:
        @block.sync
        def _(sp):
            sp.dma_start(T["Wo"][:, :, :], d["g_Wo"].rearrange("(k p) n -> p k n", p=P)).then_inc(s_ld, 16)
            sp.dma_start(T["WP"][:, :, :], d["m_WprojT"].rearrange("(k p) n -> p k n", p=P)).then_inc(s_ld, 16)
            sp.dma_start(T["GW"][:, :, :], d["f_gate_w"].rearrange("(k p) n -> p k n", p=P)).then_inc(s_ld, 16)
            for j, n in enumerate(("g_bo", "m_bproj")):
                sp.dma_start(T["brow2"][0:1, j * C:(j + 1) * C], d[n].rearrange("(a n) -> a n", a=1)).then_inc(s_ld, 16)
            sp.dma_start(T["gbrow"][0:1, :], d["f_gate_b"].rearrange("(a n) -> a n", a=1)).then_inc(s_ld, 16)
            for n in ("gamma", "beta"):
                sp.dma_start(T[n][:, :], d["g_" + n].rearrange("(a n) -> a n", a=1).broadcast_to([P, C])).then_inc(s_ld, 16)

            def rows(i):
                wait(sp, s_vt, i)
                sp.dma_start(T["Vt"][:, :], d["vtab"][bass.ds(i * P, P), :]).then_inc(s_w, 16)
            rows(0)
            with sp.Fori(1, NT, 1) as i:
                rows(i)

        @block.gpsimd
        def _(pool):
            pool.iota(T["bd_o"][:, :], [[0, P]], base=0, channel_multiplier=1).then_inc(s_i, 1)
            pool.iota(T["rank_i"][:, :], [[-1, NEXP]], base=NEXP, channel_multiplier=0).then_inc(s_i, 1)
            pool.iota(T["bd_e"][:, :], [[1, P]], base=0, channel_multiplier=0).then_inc(s_i, 1)

        @block.vector
        def _(v):
            q = Seq(v, s_v)
            v.wait_ge(s_i, 3)
            q(v.tensor_copy(T["rank"][:, :], T["rank_i"][:, :]))
            q(v.tensor_scalar(T["bd_o"][:, :], T["bd_o"][:, :], 5, None, ALU.logical_shift_right))
            q(v.tensor_scalar(T["bd_e"][:, :], T["bd_e"][:, :], 5, None, ALU.logical_shift_right))
            q(v.tensor_tensor(T["BD"][:, :], T["bd_o"][:, :], T["bd_e"][:, :], ALU.is_equal))
            for a in range(2):
                q(v.tensor_scalar(T["KS"][:, a, :], T["BD"][:, :], T["CTX"][:, a, P:P + 1], None, ALU.mult))
                v.tensor_tensor(T["CB"][:, a, :], T["CTX"][:, a, 0:P], T["BD"][:, :], ALU.mult).then_inc(s_c, 1)
            v.wait_ge(s_pe, 1)
            v.tensor_copy(T["CT"][:, :, :], T["ps_s2"][:, 0:2 * P].rearrange("p (a c) -> p a c", a=2)).then_inc(s_ct, 1)
            v.wait_ge(s_pe, 2)
            v.tensor_copy(T["M"][:, :, :], T["ps_s2"][:, :].rearrange("p (a c) -> p a c", a=2)).then_inc(s_m, 1)
            for j, (a, n0, w) in enumerate([(a, n0, w) for a in range(2) for n0, w in CH]):
                v.wait_ge(s_nd, j + 1)
                wait(v, s_ra, j)
                q(v.tensor_scalar(T["dv"][:, 0:w], T["ps_d"][:, j % 2, 0:w], 1e-6, None, ALU.max))
                q(v.reciprocal(T["dv"][:, 0:w], T["dv"][:, 0:w]))
                v.tensor_tensor(QT[:, a, n0:n0 + w], QT[:, a, n0:n0 + w], T["dv"][:, 0:w], ALU.mult).then_inc(s_ra, 1)
            n0 = q.n

            def statistics(q, i):
                v.nop(nofuse=True)
                q(v.bn_stats(T["stats2"][:, 0:6], T["yb"][:, :]))
                v.nop(nofuse=True)
                q(v.bn_aggr(T["mvb"][:, :], T["stats2"][:, 0:6]))
                q(v.tensor_scalar(T["mv2"][:, bass.ds(i * 2, 2)], T["mvb"][:, :], 1.0, None, ALU.mult))

            def head(i):
                q = Seq(v, s_v, i * 11 + n0, 11)
                acc = ACC[:, bass.ds(i * A, A)]
                den = ACC[:, bass.ds(i * A + C, H)]
                q(v.tensor_scalar(T["iz"][:, :], den, 0.0, None, ALU.is_equal))
                q(v.tensor_tensor(T["dn"][:, :], den, T["iz"][:, :], ALU.add))
                q(v.reciprocal(T["dn"][:, :], T["dn"][:, :]))
                v.wait_ge(s_w, i * 16 + 16)
                m3 = T["msg"][:, :].rearrange("p (h d) -> p h d", h=H)
                q(v.tensor_tensor(m3, T["Vt"][:, :].rearrange("p (h d) -> p h d", h=H), T["iz"][:, :].unsqueeze(2).broadcast_to([P, H, D]), ALU.mult))
                q(v.tensor_tensor(T["msg"][:, :], T["msg"][:, :], ACC[:, bass.ds(i * A, C)], ALU.add))
                v.tensor_tensor(m3, m3, T["dn"][:, :].unsqueeze(2).broadcast_to([P, H, D]), ALU.mult).then_inc(s_vt, 1)
                q(v.tensor_scalar(T["xn2"][:, :], X[:, bass.ds(i, 1), :].rearrange("p a c -> p (a c)"), rstd[:, bass.ds(i, 1)], nmr[:, bass.ds(i, 1)], ALU.mult, ALU.add))
                v.wait_ge(s_y, i + 1)
                q(v.tensor_tensor(T["yb"][:, :], T["xn2"][:, :], T["ps_y"][:, 0:C], ALU.add))
                q(v.tensor_scalar(Y[:, bass.ds(i * C, C)], T["yb"][:, :], 1.0, None, ALU.mult))
                statistics(q, i)
                x = X[:, bass.ds(i, 1), :].rearrange("p a c -> p (a c)")
                v.tensor_tensor(x, x, T["ps_y"][:, C:2 * C], ALU.add).then_inc(s_q, 1)
                q.close()
            head(0)
            with v.Fori(1, NT, 1) as i:
                head(i)
            q = Seq(v, s_v, n0 + 11 * NT)

            def inverse_deviation(k):
                mv = T["mv2"][:, :].rearrange("p (t a) -> p t a", a=2)
                v.tensor_scalar(rstd[:, :], mv[:, :, 1], EPS, None, ALU.add).then_inc(s_sq, 1)
                v.wait_ge(s_a, k)
                q(v.reciprocal(rstd[:, :], rstd[:, :]))
                q(v.tensor_tensor(nmr[:, :], mv[:, :, 0], rstd[:, :], ALU.mult))
                q(v.tensor_scalar(nmr[:, :], nmr[:, :], -1.0, None, ALU.mult))
            inverse_deviation(1)
            n1 = q.n + n0 + 11 * NT

            def middle(i):
                q = Seq(v, s_v, i * 8 + n1, 8)
                y = Y[:, bass.ds(i * C, C)]
                x = X[:, bass.ds(i, 1), :].rearrange("p a c -> p (a c)")
                q(v.tensor_scalar(y, y, rstd[:, bass.ds(i, 1)], nmr[:, bass.ds(i, 1)], ALU.mult, ALU.add))
                q(v.tensor_tensor(y, y, T["gamma"][:, :], ALU.mult))
                q(v.tensor_tensor(y, y, T["beta"][:, :], ALU.add))
                q(v.tensor_tensor(T["yb"][:, :], x, y, ALU.add))
                q(v.tensor_scalar(x, T["yb"][:, :], 1.0, None, ALU.mult))
                statistics(q, i)
                q.close()
            with v.Fori(0, NT, 1) as i:
                middle(i)
            q = Seq(v, s_v, n1 + 8 * NT)
            inverse_deviation(2)

            def last(i):
                v.wait_ge(s_t, i + NT)
                v.tensor_scalar(T["xn2"][:, :], X[:, bass.ds(i, 1), :].rearrange("p a c -> p (a c)"), rstd[:, bass.ds(i, 1)], nmr[:, bass.ds(i, 1)],
                                ALU.mult, ALU.add).then_inc(s_xf, 1)
                v.wait_ge(s_gl, i + 1)
                v.tensor_scalar(T["LG"][:, bass.ds(i, 1), :].rearrange("p a e -> p (a e)"), T["ps_y"][:, 0:NEXP], 1.0, None, ALU.mult).then_inc(s_g, 1)
            last(0)
            with v.Fori(1, NT, 1) as i:
                last(i)
            q = Seq(v, s_v, q.n + n1 + 8 * NT)
            v.wait_ge(s_g, NT)
            LG, W1b, mx, eq = T["LG"], T["CW"], T["mx"], T["eq"]
            b3 = lambda t: t[:, :].unsqueeze(2).broadcast_to([P, NT, NEXP])
            q(v.tensor_reduce(mx[:, :], LG[:, :, :], AX.X, ALU.max))
            v.tensor_tensor(LG[:, :, :], LG[:, :, :], b3(mx), ALU.subtract).then_inc(s_sq, 1)
            v.wait_ge(s_a, 3)
            q(v.tensor_reduce(mx[:, :], LG[:, :, :], AX.X, ALU.add))
            q(v.reciprocal(mx[:, :], mx[:, :]))
            q(v.tensor_tensor(LG[:, :, :], LG[:, :, :], b3(mx), ALU.mult))
            q(v.memset(T["CW"][:, :, :], 0.0))
            for r in range(2):
                q(v.tensor_reduce(mx[:, :], LG[:, :, :], AX.X, ALU.max))
                q(v.tensor_tensor(eq[:, :, :], LG[:, :, :], b3(mx), ALU.is_equal))
                q(v.tensor_tensor(eq[:, :, :], eq[:, :, :], T["rank"][:, :].unsqueeze(1).broadcast_to([P, NT, NEXP]), ALU.mult))
                q(v.tensor_reduce(T["fr"][:, :], eq[:, :, :], AX.X, ALU.max))
                q(v.tensor_tensor(eq[:, :, :], T["rank"][:, :].unsqueeze(1).broadcast_to([P, NT, NEXP]), b3(T["fr"]), ALU.is_equal))
                q(v.tensor_tensor(T["sel"][:, :, :], eq[:, :, :], LG[:, :, :], ALU.mult))
                q(v.tensor_tensor(T["CW"][:, :, :], T["CW"][:, :, :], T["sel"][:, :, :], ALU.add))
                q(v.tensor_scalar(eq[:, :, :], eq[:, :, :], -2.0, None, ALU.mult))
                q(v.tensor_tensor(LG[:, :, :], LG[:, :, :], eq[:, :, :], ALU.add))

        @block.scalar
        def _(a):
            def head(i):
                a.wait_ge(s_t, i + 1)
                wait(a, s_y, i)
                a.copy(T["mT"][:, :, :], T["ps_t2"][:, :, :]).then_inc(s_tc, 1)
                a.copy(T["qs"][:, :, :], QT[:, :, bass.ds(i * P, P)]).then_inc(s_tc, 1)
            a.wait_ge(s_ra, 2 * len(CH))
            head(0)
            with a.Fori(1, NT, 1) as i:
                head(i)
            a.wait_ge(s_sq, 1)
            a.activation(rstd[:, :], rstd[:, :], ACT.Sqrt).then_inc(s_a, 1)
            a.wait_ge(s_sq, 2)
            a.activation(rstd[:, :], rstd[:, :], ACT.Sqrt).then_inc(s_a, 1)
            with a.Fori(0, NT, 1) as i:
                a.wait_ge(s_t, i + NT + 1)
                a.copy(T["mT"][:, :, :], T["ps_t2"][:, :, :]).then_inc(s_tc, 1)
                a.copy(T["XF"][:, :, bass.ds(i * P, P)], T["ps_t2"][:, :, :]).then_inc(s_tc, 1)
            a.wait_ge(s_sq, 3)
            a.activation(T["LG"][:, :, :], T["LG"][:, :, :], ACT.Exp).then_inc(s_a, 1)

        @block.tensor
        def _(pe):
            pe.wait_ge(s_c, 2)
            for a in range(2):
                m = pe.transpose(T["ps_s2"][:, a * P:(a + 1) * P], T["CB"][:, a, :], T["ident"][:, :])
            m.then_inc(s_pe, 1)
            pe.wait_ge(s_ld, 16 * 8)
            pe.wait_ge(s_ct, 1)
            for a in range(2):
                m = pe.matmul(T["ps_s2"][:, a * C:(a + 1) * C], T["CT"][:, a, :], T["WP"][:, a, :], start=True, stop=True)
            m.then_inc(s_pe, 1)
            for j, (a, n0, w) in enumerate([(a, n0, w) for a in range(2) for n0, w in CH]):
                wait(pe, s_ra, j - 1)
                pe.matmul(T["ps_d"][:, j % 2, 0:w], T["KS"][:, a, :], QT[:, a, n0:n0 + w], start=True, stop=True).then_inc(s_nd, 1)
            pe.wait_ge(s_m, 1)

            def head(i):
                pe.wait_ge(s_vt, i + 1)
                pe.transpose(T["ps_t2"][:, 0, :], T["msg"][:, 0:P], T["ident"][:, :])
                pe.transpose(T["ps_t2"][:, 1, :], T["msg"][:, P:C], T["ident"][:, :]).then_inc(s_t, 1)
                pe.wait_ge(s_tc, 2 * i + 2)
                wait(pe, s_q, i)
                for k in range(2):
                    pe.matmul(T["ps_y"][:, 0:C], T["mT"][:, k, :], T["Wo"][:, k, :], start=(k == 0), stop=False)
                pe.matmul(T["ps_y"][:, 0:C], T["onesr"][0:1, :], T["brow2"][0:1, 0:C], start=False, stop=True)
                for k in range(2):
                    pe.matmul(T["ps_y"][:, C:2 * C], T["qs"][:, k, :], T["M"][:, k, :], start=(k == 0), stop=False)
                pe.matmul(T["ps_y"][:, C:2 * C], T["onesr"][0:1, :], T["brow2"][0:1, C:2 * C], start=False, stop=True).then_inc(s_y, 1)
            head(0)
            with pe.Fori(1, NT, 1) as i:
                head(i)

            def gates(i):
                pe.wait_ge(s_xf, i + 1)
                pe.transpose(T["ps_t2"][:, 0, :], T["xn2"][:, 0:P], T["ident"][:, :])
                pe.transpose(T["ps_t2"][:, 1, :], T["xn2"][:, P:C], T["ident"][:, :]).then_inc(s_t, 1)
                pe.wait_ge(s_tc, 2 * NT + 2 * i + 2)
                wait(pe, s_g, i)
                for k in range(2):
                    pe.matmul(T["ps_y"][:, 0:NEXP], T["mT"][:, k, :], T["GW"][:, k, :], start=(k == 0), stop=False)
                pe.matmul(T["ps_y"][:, 0:NEXP], T["onesr"][0:1, :], T["gbrow"][0:1, :], start=False, stop=True).then_inc(s_gl, 1)
            pe.wait_ge(s_q, NT)
            gates(0)
            with pe.Fori(1, NT, 1) as i:
                gates(i)
def phase_experts(nc, sem, T, d):
    s_w = [sem(f"ex_weights{h}") for h in range(2)]
    s_b, s_h, s_hg, s_y, s_acc, s_ct, s_cc, s_o = (sem("ex_" + n) for n in
        ("b2", "hidden", "activated", "rows", "added", "weights_turned", "weights_copied", "stored"))
    TC = 5
    NCH, CW_ = NT // TC, TC * P
    HC = HID // P
    X, XF = T["X"], T["XF"]
    with nc.Block() as block:
        @block.sync
        def _(sp):
            sp.dma_start(T["b2"][:, :], d["f_b2"]).then_inc(s_b, 16)
            for e in range(NEXP):
                if e >= 2:
                    sp.wait_ge(s_acc, NT + (e - 1) * NT)
                sp.dma_start(T["W1"][:, e % 2, :, :], d["f_W1"][e].rearrange("(k p) n -> p k n", p=P)).then_inc(s_w[e % 2], 16)
                sp.dma_start(T["W2"][:, e % 2, :, :], d["f_W2"][e].rearrange("(k p) n -> p k n", p=P)).then_inc(s_w[e % 2], 16)
                sp.dma_start(T["b1"][:, e % 2, :], d["f_b1"][e].rearrange("(k p) -> p k", p=P), allow_slow_non_contiguous=True).then_inc(s_w[e % 2], 16)
            sp.wait_ge(s_acc, NT * (NEXP + 1))
            for t in range(NT):
                r = min(P, N - t * P)
                sp.dma_start(d["out"][t * P:t * P + r, :], X[0:r, t, :]).then_inc(s_o, 16)
            sp.wait_ge(s_o, 16 * NT)

        @block.tensor
        def _(pe):
            pe.wait_ge(s_b, 16)
            for t in range(NT):
                if t:
                    pe.wait_ge(s_cc, t)
                pe.transpose(T["ps_w"][0:NEXP, 0:P], T["CW"][:, t, :], T["ident"][:, :]).then_inc(s_ct, 1)
                pe.wait_ge(s_cc, t + 1)
                if t:
                    pe.wait_ge(s_acc, t)
                pe.matmul(T["ps_o2"][:, 0, 0:C], T["cT"][0:NEXP, :], T["b2"][:, :], start=True, stop=True).then_inc(s_y, 1)
            for e in range(NEXP):
                pe.wait_ge(s_w[e % 2], 48 * (e // 2 + 1))

                def chunk(j):
                    g = e * NCH + j
                    for m in range(HC):
                        if e > 0 or not isinstance(j, int):
                            pe.wait_ge(s_hg, (g - 1) * HC + m + 1)
                        for w in range(2):
                            for k in range(2):
                                r = pe.matmul(T["ps_h"][:, m % 2, w, 0:CW_ // 2], T["W1"][:, e % 2, k, m * P:(m + 1) * P],
                                              XF[:, k, bass.ds(j * CW_ + w * CW_ // 2, CW_ // 2)], start=(k == 0), stop=(k == 1))
                        r.then_inc(s_h, 1)
                        if m < HC - 1 and m >= 1:
                            pe.wait_ge(s_hg, g * HC + m)
                    pe.wait_ge(s_hg, (g + 1) * HC)
                    for t in range(TC):
                        n = g * TC + t
                        pe.wait_ge(s_acc, (n - 1 if t else n) + NT)
                        for m in range(HC):
                            r = pe.matmul(T["ps_o2"][:, t % 2, 0:C],
                                          T["HT"][:, m, t * P:(t + 1) * P], T["W2"][:, e % 2, m, :], start=(m == 0), stop=(m == HC - 1))
                        r.then_inc(s_y, 1)
                chunk(0)
                with pe.Fori(1, NCH, 1) as j:
                    chunk(j)

        @block.scalar
        def _(a):
            for t in range(NT):
                a.wait_ge(s_ct, t + 1)
                a.copy(T["cT"][0:NEXP, :], T["ps_w"][0:NEXP, 0:P]).then_inc(s_cc, 1)
            for e in range(NEXP):
                a.wait_ge(s_w[e % 2], 48 * (e // 2 + 1))

                def chunk(j):
                    g = e * NCH + j
                    a.wait_ge(s_y, g * TC + NT)
                    for m in range(HC):
                        a.wait_ge(s_h, g * HC + m + 1)
                        a.activation(T["HT"][:, m, :].rearrange("p (w n) -> p w n", w=2), T["ps_h"][:, m % 2, :, 0:CW_ // 2], ACT.Gelu,
                                     bias=T["b1"][:, e % 2, m:m + 1]).then_inc(s_hg, 1)
                chunk(0)
                with a.Fori(1, NCH, 1) as j:
                    chunk(j)

        @block.vector
        def _(v):
            for t in range(NT):
                v.wait_ge(s_y, t + 1)
                v.tensor_tensor(X[:, t, :], X[:, t, :], T["ps_o2"][:, 0, 0:C], ALU.add).then_inc(s_acc, 1)
            for e in range(NEXP):
                with v.Fori(0, NCH, 1) as j:
                    for t in range(TC):
                        n = (e * NCH + j) * TC + t
                        v.wait_ge(s_y, n + 1 + NT)
                        v.wait_ge(s_acc, n + NT)
                        x = X[:, bass.ds(j * TC + t, 1), :].rearrange("p a c -> p (a c)")
                        v.scalar_tensor_tensor(out=x, in0=T["ps_o2"][:, t % 2, 0:C], scalar=T["CW"][:, bass.ds(j * TC + t, 1), e:e + 1].rearrange("p a b -> p (a b)"),
                                               in1=x, op0=ALU.mult, op1=ALU.add).then_inc(s_acc, 1)
DRAM_IN = ["x", "edges", "g_query", "g_Wq", "g_bq", "g_Wk", "g_bk", "g_Wv", "g_bv", "g_rel_w", "g_Wo", "g_bo", "g_gamma",
           "g_beta", "m_WqT", "m_WkvT", "m_WprojT", "m_bproj", "f_gate_w", "f_gate_b", "f_W1", "f_b1", "f_W2", "f_b2"]


def build(nc, d, dbg=None):
    d["ktab"] = nc.dram_tensor("ktab", (NT * P, C), F32).ap()
    d["vtab"] = nc.dram_tensor("vtab", (NT * P, C), F32).ap()
    d["dl_rows"] = nc.dram_tensor("dl_rows", (NS, P), F32).ap()
    d["ty_rows"] = nc.dram_tensor("ty_rows", (NS, P), F32).ap()
    with ExitStack() as ctx:
        def sem(name):
            return ctx.enter_context(nc.semaphore(name))

        T = {}

        def sbuf(stack, spec):
            for n, (shape, dt) in spec.items():
                T[n] = stack.enter_context(nc.sbuf_tensor(n, list(shape), dt))

        def psum(stack, spec):
            for n, (shape, dt) in spec.items():
                T[n] = stack.enter_context(nc.psum_tensor(n, list(shape), dt))

        sbuf(ctx, {"X": ((P, NT, C), F32), "rstd": ((P, NT), F32), "nmr": ((P, NT), F32), "QT": ((P, 2, NT * P), F32),
                   "CTX": ((P, 2, P + 1), F32), "iota_f": ((P, P), F32), "iota_p": ((P, 1), F32), "ident": ((P, P), F32),
                   "onesr": ((P, P), F32), "zero": ((P, P + 1), F32)})
        sbuf(ctx, {"CW": ((P, NT, NEXP), F32), "ACC": ((P, NT * (C + H)), F32)})
        with ExitStack() as gnn:
            sbuf(gnn, {"QN": ((P, NT * C), F32)})
            with ExitStack() as ph:
                sbuf(ph, {"W": ((P, 2, 5 * C), F32), "WQM": ((P, 2, C), F32), "brow": ((1, 3 * C), F32), "qe": ((P, 2), F32),
                          "qbc": ((P, 2, P), F32), "bias": ((P, 3 * C), F32), "stats": ((P, 6), F32), "mv": ((P, NT, 2), F32),
                          "xnb": ((P, C), F32), "xnT": ((P, 2, P), F32), "kvb": ((P, 2 * C), F32), "mn": ((P, 2 * C), F32),
                          "ex": ((P, 2 * C), F32), "kb": ((P, C), F32), "vb": ((P, 2, P + 1), F32), "mask": ((P, NT), F32),
                          "iota_i": ((P, P), I32), "iota_pi": ((P, 1), I32), "node_i": ((P, NT), I32)})
                psum(ph, {"ps_n": ((P, 3, 512), F32), "ps_q": ((P, 512), F32), "ps_t": ((P, 2, P), F32), "ps_c": ((P, 2, P + 1), F32)})
                phase_project(nc, sem, T, d)
            sbuf(gnn, {"SRC": ((P, NS), I32), "DC": ((P, NS), F32), "bRow": ((1, NS), I32), "penf": ((P, SC, P), F32),
                       "penb": ((P, SC, P), F32), "valid": ((P, SC, P), F32), "S": ((P, NS * H), F32)})
            with ExitStack() as ph:
                sbuf(ph, {"last_i": ((1, ET), I32), "t_i": ((1, ET), I32), "hi": ((1, ET), F32), "st": ((1, ET), F32),
                          "s_i": ((P, SC), I32), "s_f": ((P, SC), F32), "junk": ((P, ET), F32), "cnt": ((P, SC), F32),
                          "bS": ((P, SC), F32), "b128": ((P, SC), F32), "tI": ((P, SC), I32), "EI": ((P, SC, 5 * P), I32),
                          "DL": ((P, SC, P), F32), "rows": ((P, SC, P), F32), "srow": ((P, SC, P), F32)})
                psum(ph, {"ps_a": ((P, 512), F32), "ps_b": ((P, 512), F32)})
                phase_steps(nc, sem, T, d)
            with ExitStack() as ph:
                sbuf(ph, {"dlb": ((P, 2, G * P), F32), "tyb": ((NREL, 2, G * P), F32), "ixs": ((P, 2, G), I32),
                          "KG": ((P, 2 * G * C), F32), "PT": ((P, 2, G * P), F32), "OT": ((NREL, 2, G * P), F32),
                          "rel": ((NREL, D), F32), "KU": ((P, G * C), F32)})
                psum(ph, {"ps_qe": ((P, 2, G, C), F32), "ps_u": ((P, 2, G, 2 * D), F32)})
                T["ps_u"] = T["ps_u"][:, :, :, 0:D]
                phase_scores(nc, sem, T, d)
            with ExitStack() as ph:
                sbuf(ph, {"ST": ((P, SC * H, P), F32), "SX": ((P, SC * H, P), F32), "F": ((P, SC * H, P), F32),
                          "penL": ((P, SC * H, P), F32), "LR": ((P, 2, SC * H), F32), "rp": ((P, SC), F32),
                          "E2": ((H, 2, NS), F32), "E4": ((H, NS), F32), "CR": ((H, NS), F32), "inj": ((P, SC * H), F32)})
                psum(ph, {"ps_s": ((P, SC, 512), F32), "ps_e": ((P, 2, 512), F32), "ps_c2": ((P, SC * H), F32)})
                phase_softmax_weights(nc, sem, T, d)
            with ExitStack() as ph:
                sbuf(ph, {"VG": ((P, 2 * G * C), F32), "WV": ((P, 2, G * C), F32), "PM": ((P, 2, G, P), F32), "ixv": ((P, 2, G), I32)})
                psum(ph, {"ps_o": ((P, 2 * G, 512), F32)})
                phase_aggregate(nc, sem, T, d)
            if dbg == "S":
                s_o = sem("s_o")
                with nc.Block() as block:
                    @block.sync
                    def _(sp):
                        sp.dma_start(d["out_S"], T["S"][:, :]).then_inc(s_o, 16)
                        sp.dma_start(d["out_A"], T["ACC"][:, :]).then_inc(s_o, 16)
                        sp.wait_ge(s_o, 32)
                return
        sbuf(ctx, {"XF": ((P, 2, NT * P), F32)})
        with ExitStack() as ph:
            sbuf(ph, {"Y": ((P, NT * C), F32), "Wo": ((P, 2, C), F32), "WP": ((P, 2, C), F32), "GW": ((P, 2, NEXP), F32),
                      "brow2": ((1, 2 * C), F32), "gbrow": ((1, NEXP), F32), "gamma": ((P, C), F32), "beta": ((P, C), F32),
                      "Vt": ((P, C), F32), "bd_o": ((P, P), I32), "bd_e": ((P, P), I32), "BD": ((P, P), F32), "KS": ((P, 2, P), F32),
                      "CB": ((P, 2, P), F32), "CT": ((P, 2, P), F32), "M": ((P, 2, C), F32), "dv": ((P, 512), F32),
                      "iz": ((P, H), F32), "dn": ((P, H), F32), "msg": ((P, C), F32), "xn2": ((P, C), F32), "stats2": ((P, 6), F32),
                      "mv2": ((P, NT * 2), F32), "mvb": ((P, 2), F32), "yb": ((P, C), F32), "mT": ((P, 2, P), F32), "qs": ((P, 2, P), F32), "LG": ((P, NT, NEXP), F32),
                      "mx": ((P, NT), F32), "fr": ((P, NT), F32), "eq": ((P, NT, NEXP), F32), "sel": ((P, NT, NEXP), F32),
                      "rank": ((P, NEXP), F32), "rank_i": ((P, NEXP), I32)})
            psum(ph, {"ps_s2": ((P, 2 * C), F32), "ps_d": ((P, 2, 512), F32), "ps_t2": ((P, 2, P), F32), "ps_y": ((P, 2 * C), F32)})
            phase_combine(nc, sem, T, d)
        with ExitStack() as ph:
            sbuf(ph, {"W1": ((P, 2, 2, HID), F32), "W2": ((P, 2, HID // P, C), F32), "b1": ((P, 2, HID // P), F32),
                      "b2": ((NEXP, C), F32), "cT": ((NEXP, P), F32), "HT": ((P, HID // P, 5 * P), F32)})
            psum(ph, {"ps_w": ((P, P), F32), "ps_o2": ((P, 2, 512), F32), "ps_h": ((P, 2, 2, 512), F32)})
            phase_experts(nc, sem, T, d)
DBG=None
OUTS={"out":(N,C)}


def lay_out(inputs):
    import numpy as np
    g = {k: np.ascontiguousarray(v) for k, v in inputs.items()}
    a = {}
    a["x"] = np.concatenate([g["x"], np.zeros((NT * P - N, C), np.float32)])
    npad = ET * P - E_REAL
    pad = np.full((npad,), PADDST, np.int32)
    dst = np.concatenate([np.full((1,), -1, np.int32), g["dst"], pad, pad[:1]])
    z = np.zeros((npad,), np.int32)
    a["edges"] = np.ascontiguousarray(np.concatenate([v.reshape(ET, P) for v in (
        dst[1:-1], dst[:-2], dst[2:], np.concatenate([g["src"], z]), np.concatenate([g["edge_type_64"], z]))], axis=1))
    for n, m in (("g_query", "gnn_query_emb"), ("g_Wq", "gnn_Wq"), ("g_bq", "gnn_bq"), ("g_Wk", "gnn_Wk"), ("g_bk", "gnn_bk"),
                 ("g_Wv", "gnn_Wv"), ("g_bv", "gnn_bv"), ("g_rel_w", "gnn_rel_w"), ("g_Wo", "gnn_Wo"), ("g_bo", "gnn_bo"),
                 ("g_gamma", "gnn_gamma"), ("g_beta", "gnn_beta"), ("m_bproj", "mix_bproj"), ("f_gate_w", "ffn_gate_w"),
                 ("f_gate_b", "ffn_gate_b"), ("f_W1", "ffn_W1"), ("f_b1", "ffn_b1"), ("f_W2", "ffn_W2"), ("f_b2", "ffn_b2")):
        a[n] = g["L0_" + m]
    for n, m in (("m_WqT", "mix_Wq"), ("m_WkvT", "mix_Wkv"), ("m_WprojT", "mix_Wproj")):
        a[n] = np.ascontiguousarray(g["L0_" + m].T)
    return a


def kernel(**inputs):
    import concourse.bacc as _bacc
    from concourse import mybir as _mybir
    from concourse.bass_utils import run_bass_kernel_spmd as _run

    nc = _bacc.Bacc("TRN2", target_bir_lowering=False, num_devices=1)
    a = lay_out(inputs)
    d = {n: nc.dram_tensor(f"in_{n}_dram", a[n].shape, _mybir.dt.from_np(a[n].dtype), kind="ExternalInput").ap() for n in DRAM_IN}
    for n, (shape) in OUTS.items():
        d[n] = nc.dram_tensor(n + "_dram", shape, F32, kind="ExternalOutput").ap()
    build(nc, d, DBG)
    r = _run(nc, [{f"in_{n}_dram": a[n] for n in DRAM_IN}], core_ids=[0])
    res = r.results[0]
    return tuple(res[n + "_dram"] for n in OUTS) if len(OUTS) > 1 else res["out_dram"][0:N]
```

```python
from contextlib import ExitStack

import concourse.bass as bass
from concourse import mybir

F32 = mybir.dt.float32
BF16 = mybir.dt.bfloat16
I32 = mybir.dt.int32
ALU = mybir.AluOpType
ACT = mybir.ActivationFunctionType
AX = mybir.AxisListType

P = 128
N = 3125
C = 256
NT = (N + P - 1) // P
E_REAL = 53125
ET = (E_REAL + P - 1) // P
H, D = 4, 64
NREL = 64
MD = 32
NS = ET + NT - 1
SC = 4
SP_ = NS // SC
G = 4
NG = NS // G
UN = 10
RG = 5
BIG = 1.0e30
EPS = 1.0e-5
NEXP, HID = 8, 512
PADDST = 4095
assert SC * SP_ == NS and NG * G == NS and NG % UN == 0 and UN % RG == 0 and UN % 2 == 0


class Seq:

    def __init__(self, eng, sem, base=0, per=None):
        self.eng, self.sem, self.base, self.n, self.per = eng, sem, base, 0, per

    def __call__(self, ins):
        ins.then_inc(self.sem, 1)
        self.n += 1
        self.eng.wait_ge(self.sem, self.base + self.n)

    def close(self):
        assert self.per is None or self.n == self.per, (self.n, self.per)


def wait(eng, sem, count):
    if isinstance(count, int) and count <= 0:
        return
    eng.wait_ge(sem, count)


def each_tile(eng, body):
    for i in range(NT):
        body(i, i % 2)


def load_values(nc, engine, ap, high):
    return nc.values_load_multi_w_load_instructions(ap, engines=(engine,), min_val=0, max_val=high,
                                                    skip_runtime_bounds_check_because="the step list holds node blocks only")[1]


def phase_project(nc, sem, T, d):
    s_ld, s_x, s_id, s_one, s_v, s_sq, s_a, s_p = (sem("pj_" + n) for n in
        ("loads", "x", "iota", "constants", "vector", "variance", "deviation", "pool"))
    s_xn, s_t, s_tc, s_mm, s_r, s_e, s_vb, s_k, s_qf, s_q3, s_kvb, s_ctx = (sem("pj_" + n) for n in
        ("normed", "turned", "turned_copied", "products", "negative_part", "exp", "v_copied", "evacuated", "q_ready", "q_split",
         "kv_ready", "context"))
    s_kv = [sem(f"pj_kv_stored{h}") for h in range(2)]
    X, W, WQM, rstd, nmr = T["X"], T["W"], T["WQM"], T["rstd"], T["nmr"]
    xnb, xnT, kvb, ex, kb, vb, qf = (T[n] for n in ("xnb", "xnT", "kvb", "ex", "kb", "vb", "qf"))
    ps_t, ps_n, ps_c = T["ps_t"], T["ps_n"], T["ps_c"]
    XQ = 5
    with nc.Block() as block:
        @block.sync
        def _(sp):
            for t in range(0, NT, NT // XQ):
                sp.dma_start(X[:, t:t + NT // XQ, :], d["x"][t * P:(t + NT // XQ) * P, :].rearrange("(t p) c -> p t c", p=P)).then_inc(s_x, 16)
            for j, n in enumerate(("g_Wq", "g_Wk", "g_Wv")):
                sp.dma_start(W[:, :, j * C:(j + 1) * C], d[n].rearrange("(k p) n -> p k n", p=P)).then_inc(s_ld, 16)
            sp.dma_start(W[:, :, 3 * C:5 * C], d["m_WkvT"].rearrange("(k p) n -> p k n", p=P)).then_inc(s_ld, 16)
            sp.dma_start(WQM[:, :, :], d["m_WqT"].rearrange("(k p) n -> p k n", p=P)).then_inc(s_ld, 16)
            for j, n in enumerate(("g_bq", "g_bk", "g_bv")):
                sp.dma_start(T["brow"][0:1, j * C:(j + 1) * C], d[n].rearrange("(a n) -> a n", a=1)).then_inc(s_ld, 16)
            for k in range(2):
                sp.dma_start(T["qe"][:, k:k + 1], d["g_query"][k * P:(k + 1) * P].rearrange("(p a) -> p a", a=1)).then_inc(s_ld, 16)

            def store(i, h):
                sp.wait_ge(s_kvb, 2 * i + 2)
                sp.dma_start(d["ktab"][i * P:(i + 1) * P, :], kvb[:, h, 0:C]).then_inc(s_kv[h], 16)
                sp.dma_start(d["vtab"][i * P:(i + 1) * P, :], kvb[:, h, C:2 * C]).then_inc(s_kv[h], 16)
            each_tile(sp, store)
            for h in range(2):
                sp.wait_ge(s_kv[h], 32 * ((NT + 1 - h) // 2))

        @block.gpsimd
        def _(pool):
            pool.iota(T["iota_i"][:, :], [[1, P]], base=0, channel_multiplier=0).then_inc(s_id, 1)
            pool.iota(T["iota_pi"][:, :], [[1, 1]], base=0, channel_multiplier=1).then_inc(s_id, 1)
            pool.iota(T["node_i"][:, :], [[P, NT]], base=0, channel_multiplier=1).then_inc(s_id, 1)

            def split(i, h):
                q = Seq(pool, s_p, 4 * i, 4)

                def part(n):
                    return T["Q3"][:, (i * 3 + n) * C:(i * 3 + n + 1) * C]
                pool.wait_ge(s_qf, i + 1)
                q(pool.tensor_copy(part(0), qf[:, h, :]))
                q(pool.tensor_tensor(qf[:, h, :], qf[:, h, :], part(0), ALU.subtract))
                q(pool.tensor_copy(part(1), qf[:, h, :]))
                q(pool.tensor_tensor(qf[:, h, :], qf[:, h, :], part(1), ALU.subtract))
                q.close()
                pool.tensor_copy(part(2), qf[:, h, :]).then_inc(s_q3, 1)
            each_tile(pool, split)

        @block.vector
        def _(v):
            q = Seq(v, s_v)
            v.memset(T["onesr"][:, :], 1.0).then_inc(s_one, 1)
            v.memset(T["zero"][:, :], 0.0).then_inc(s_one, 1)
            v.wait_ge(s_id, 3)
            q(v.tensor_copy(T["iota_f"][:, :], T["iota_i"][:, :]))
            q(v.tensor_copy(T["iota_p"][:, :], T["iota_pi"][:, :]))
            q(v.tensor_copy(T["mask"][:, :], T["node_i"][:, :]))
            q(v.tensor_scalar(T["mask"][:, :], T["mask"][:, :], float(N), None, ALU.is_lt))
            v.tensor_scalar(T["ident"][:, :], T["iota_f"][:, :], T["iota_p"][:, 0:1], None, ALU.is_equal).then_inc(s_one, 1)
            v.wait_ge(s_ld, 16 * 10)
            q(v.tensor_scalar(T["qe"][:, :], T["qe"][:, :], 0.1, None, ALU.mult))
            v.wait_ge(s_one, 3)
            for k in range(2):
                v.tensor_scalar(T["qbc"][:, k, :], T["onesr"][:, :], T["qe"][:, k:k + 1], None, ALU.mult).then_inc(s_sq, 1)
            for t in range(NT):
                if t == 0:
                    v.wait_ge(s_x, 16 * XQ)
                v.bn_stats(T["stats"][:, t, :], X[:, t, :]).then_inc(s_v, 1)
                q.n += 1
            for t in range(NT):
                v.wait_ge(s_v, q.n - NT + t + 1)
                v.bn_aggr(T["mv"][:, t, :], T["stats"][:, t, :]).then_inc(s_v, 1)
            q.n += NT
            v.wait_ge(s_v, q.n)
            v.tensor_scalar(rstd[:, :], T["mv"][:, :, 1], EPS, None, ALU.add).then_inc(s_sq, 1)
            v.wait_ge(s_mm, 1)
            q(v.tensor_copy(T["bias"][:, 0:512], ps_n[:, 0, 0, :]))
            q(v.tensor_copy(T["bias"][:, 512:768], ps_n[:, 0, 1, 0:256]))
            q(v.tensor_scalar(T["bias"][:, 0:C], T["bias"][:, 0:C], 0.125, None, ALU.mult))
            v.wait_ge(s_a, 1)
            q(v.reciprocal(rstd[:, :], rstd[:, :]))
            q(v.tensor_tensor(nmr[:, :], T["mv"][:, :, 0], rstd[:, :], ALU.mult))
            q(v.tensor_scalar(nmr[:, :], nmr[:, :], -1.0, None, ALU.mult))
            for h in range(2):
                q(v.tensor_copy(vb[:, h, :, P:P + 1], T["onesr"][:, 0:2].unsqueeze(2)))

            def normalise(i):
                wait(v, s_t, i - 2)
                v.tensor_scalar(xnb[:, i % 3, :], X[:, i, :], rstd[:, i:i + 1],
                                nmr[:, i:i + 1], ALU.mult, ALU.add).then_inc(s_xn, 1)

            def evacuate(i, h):
                v.wait_ge(s_mm, i + 2)
                wait(v, s_q3, i - 1)
                v.scalar_tensor_tensor(out=qf[:, h, :], in0=ps_n[:, h, 0, 0:C], scalar=0.125,
                                       in1=T["bias"][:, 0:C], op0=ALU.mult, op1=ALU.add).then_inc(s_qf, 1)
                wait(v, s_kv[h], (i - h) * 16)
                v.tensor_tensor(kvb[:, h, 0:C], ps_n[:, h, 0, C:2 * C], T["bias"][:, C:2 * C], ALU.add).then_inc(s_kvb, 1)
                v.wait_ge(s_e, i + 1)
                v.tensor_tensor(kvb[:, h, C:2 * C], ps_n[:, h, 1, 0:C], T["bias"][:, 2 * C:3 * C], ALU.add).then_inc(s_kvb, 1)
                v.scalar_tensor_tensor(out=T["QT"][:, :, i * P:(i + 1) * P], in0=ps_n[:, h, 2, C:2 * C].rearrange("p (a c) -> p a c", a=2),
                                       scalar=0.0, in1=ex[:, h, C:2 * C].rearrange("p (a c) -> p a c", a=2), op0=ALU.max, op1=ALU.add).then_inc(s_v, 1)
                wait(v, s_ctx, i - 1)
                v.scalar_tensor_tensor(out=kb[:, h, :], in0=ps_n[:, h, 1, C:2 * C], scalar=0.0, in1=ex[:, h, 0:C], op0=ALU.max,
                                       op1=ALU.add).then_inc(s_v, 1)
                v.wait_ge(s_v, q.n + 2 * i + 2)
                v.tensor_scalar(kb[:, h, :], kb[:, h, :], T["mask"][:, i:i + 1], None, ALU.mult).then_inc(s_k, 1)

            normalise(0)
            normalise(1)
            for i in range(NT):
                if i + 2 < NT:
                    normalise(i + 2)
                evacuate(i, i % 2)
            v.wait_ge(s_ctx, NT + 1)
            v.tensor_copy(T["CTX"][:, :, :], ps_c[:, :, :]).then_inc(s_v, 1)

        @block.scalar
        def _(a):
            a.wait_ge(s_sq, 3)
            a.activation(rstd[:, :], rstd[:, :], ACT.Sqrt).then_inc(s_a, 1)

            def copy_turned(i, h):
                a.wait_ge(s_t, i + 1)
                wait(a, s_mm, i)
                a.copy(xnT[:, h, :, :], ps_t[:, :, :]).then_inc(s_tc, 1)

            def parts(i, h):
                a.wait_ge(s_mm, i + 2)
                wait(a, s_k, i - 1)
                a.activation(ex[:, h, 0:C], ps_n[:, h, 1, C:2 * C], ACT.Relu, scale=-1.0).then_inc(s_r, 1)
                a.activation(ex[:, h, C:2 * C], ps_n[:, h, 2, C:2 * C], ACT.Relu, scale=-1.0).then_inc(s_r, 1)
                wait(a, s_ctx, i - 1)
                a.copy(vb[:, h, :, 0:P], ps_n[:, h, 2, 0:C].rearrange("p (a c) -> p a c", a=2)).then_inc(s_vb, 1)
                a.wait_ge(s_r, 2 * i + 2)
                a.wait_ge(s_vb, i + 1)
                a.activation(ex[:, h, :], ex[:, h, :], ACT.Exp, scale=-1.0).then_inc(s_e, 1)

            copy_turned(0, 0)
            for i in range(NT):
                if i + 1 < NT:
                    copy_turned(i + 1, (i + 1) % 2)
                parts(i, i % 2)

        @block.tensor
        def _(pe):
            pe.wait_ge(s_one, 3)
            pe.wait_ge(s_ld, 160)
            pe.wait_ge(s_sq, 2)
            for b, (c0, c1) in enumerate(((0, 512), (512, 768))):
                for k in range(2):
                    pe.matmul(ps_n[:, 0, b, 0:c1 - c0], T["qbc"][:, k, :], W[:, k, c0:c1], start=(k == 0), stop=False)
                m = pe.matmul(ps_n[:, 0, b, 0:c1 - c0], T["onesr"][0:1, :], T["brow"][0:1, c0:c1], start=False, stop=True)
            m.then_inc(s_mm, 1)
            for a in range(2):
                pe.matmul(ps_c[:, a, :], T["zero"][:, 0:P], T["zero"][:, 0:P + 1], start=True, stop=False, skip_group_check=True)

            def turn(i, h):
                pe.wait_ge(s_xn, i + 1)
                wait(pe, s_tc, i)
                pe.transpose(ps_t[:, 0, :], xnb[:, i % 3, 0:P], T["ident"][:, :])
                pe.transpose(ps_t[:, 1, :], xnb[:, i % 3, P:C], T["ident"][:, :]).then_inc(s_t, 1)

            def project(i, h):
                pe.wait_ge(s_tc, i + 1)
                wait(pe, s_k, i - 1)
                wait(pe, s_vb, i - 1)
                for b, (c0, c1) in enumerate(((0, 512), (512, 1024), (1024, 1280))):
                    for k in range(2):
                        pe.matmul(ps_n[:, h, b, 0:c1 - c0], xnT[:, h, k, :], W[:, k, c0:c1], start=(k == 0), stop=(k == 1))
                for o in range(2):
                    for k in range(2):
                        m = pe.matmul(ps_n[:, h, 2, C + o * P:C + (o + 1) * P], WQM[:, k, o * P:(o + 1) * P], xnT[:, h, k, :],
                                      start=(k == 0), stop=(k == 1), skip_group_check=True)
                m.then_inc(s_mm, 1)

            def context(i, h):
                pe.wait_ge(s_k, i + 1)
                pe.wait_ge(s_vb, i + 1)
                for a in range(2):
                    m = pe.matmul(ps_c[:, a, :], kb[:, h, a * P:(a + 1) * P], vb[:, h, a, :], start=False, stop=False, skip_group_check=True)
                m.then_inc(s_ctx, 1)

            pe.wait_ge(s_v, 5 + 2 * NT + 3)
            turn(0, 0)
            for i in range(NT):
                if i + 1 < NT:
                    turn(i + 1, (i + 1) % 2)
                project(i, i % 2)
                if i:
                    context(i - 1, (i - 1) % 2)
            context(NT - 1, (NT - 1) % 2)
            for a in range(2):
                m = pe.matmul(ps_c[:, a, :], T["zero"][:, 0:P], T["zero"][:, 0:P + 1], start=False, stop=True, skip_group_check=True)
            m.then_inc(s_ctx, 1)


def phase_steps(nc, sem, T, d):
    s_ld, s_v, s_io, s_pe, s_cp, s_g, s_st, s_rdy, s_tr, s_ev = (sem("st_" + n) for n in
        ("loads", "vector", "iota", "products", "copied", "gathered", "stored", "ready", "transposed", "evac"))
    EI, rows, DL = T["EI"], T["rows"], T["DL"]
    with nc.Block() as block:
        @block.sync
        def _(sp):
            sp.dma_start(T["last_i"][0:1, :], d["edges"][:, P - 1:P].rearrange("t a -> a t"), allow_slow_non_contiguous=True).then_inc(s_ld, 16)
            sp.wait_ge(s_rdy, 2)
            for c in range(SC):
                sp.dma_start(d["dl_rows"][c * SP_:(c + 1) * SP_, :], rows[0:SP_, 0, c, :]).then_inc(s_st, 16)
                sp.dma_start(d["ty_rows"][c * SP_:(c + 1) * SP_, :], rows[0:SP_, 1, c, :]).then_inc(s_st, 16)
            sp.wait_ge(s_st, 2 * SC * 16)

        @block.gpsimd
        def _(pool):
            pool.iota(T["t_i"][0:1, :], [[1, ET]], base=0, channel_multiplier=0).then_inc(s_io, 1)
            pool.iota(T["s_i"][:, :], [[SP_, SC]], base=0, channel_multiplier=1).then_inc(s_io, 1)
            pool.wait_ge(s_cp, 1)
            for c in range(SC):
                pool.indirect_dma_start(EI[0:SP_, c, :], None, d["edges"], bass.IndirectOffsetOnAxis(ap=T["tI"][0:SP_, c:c + 1], axis=0)).then_inc(s_g, 16)

        @block.vector
        def _(v):
            q = Seq(v, s_v)
            v.wait_ge(s_ld, 16)
            v.wait_ge(s_io, 2)
            q(v.tensor_scalar(T["last_i"][0:1, :], T["last_i"][0:1, :], 7, None, ALU.logical_shift_right))
            q(v.tensor_copy(T["hi"][0:1, :], T["last_i"][0:1, :]))
            q(v.tensor_scalar(T["hi"][0:1, :], T["hi"][0:1, :], float(NT - 1), None, ALU.min))
            q(v.tensor_copy(T["st"][0:1, :], T["t_i"][0:1, :]))
            v.tensor_tensor(T["st"][0:1, 1:ET], T["st"][0:1, 1:ET], T["hi"][0:1, 0:ET - 1], ALU.add).then_inc(s_rdy, 1)
            q(v.tensor_copy(T["s_f"][:, :], T["s_i"][:, :]))
            v.wait_ge(s_pe, 1)
            for c in range(SC):
                q(v.tensor_scalar(T["junk"][:, :], T["ps_a"][:, 0:ET], T["s_f"][:, c:c + 1], None, ALU.is_le, ALU.add,
                                  accum_out=T["cnt"][:, c:c + 1]))
            q(v.tensor_scalar(T["cnt"][:, :], T["cnt"][:, :], -1.0, None, ALU.add))
            q(v.tensor_tensor(T["bS"][:, :], T["s_f"][:, :], T["cnt"][:, :], ALU.subtract))
            v.tensor_copy(T["tI"][:, :], T["cnt"][:, :]).then_inc(s_cp, 1)
            q(v.tensor_scalar(T["b128"][:, :], T["bS"][:, :], float(P), None, ALU.mult))
            v.wait_ge(s_pe, 2)
            q(v.tensor_scalar(T["qRow"][0:1, :], T["ps_a"][0:1, 0:NS], float(3 * C), None, ALU.mult))
            q(v.tensor_scalar(T["aRow"][0:1, :], T["ps_a"][0:1, 0:NS], float(C + H), None, ALU.mult))
            v.wait_ge(s_g, 16 * SC)
            R = SP_
            for c in range(SC):
                q(v.tensor_copy(DL[0:R, c, :], EI[0:R, c, 0:P]))
                q(v.tensor_scalar(DL[0:R, c, :], DL[0:R, c, :], T["b128"][0:R, c:c + 1], -1.0, ALU.subtract, ALU.max))
                q(v.tensor_scalar(DL[0:R, c, :], DL[0:R, c, :], float(P), None, ALU.min))
                q(v.tensor_scalar(T["valid"][0:R, c, :], DL[0:R, c, :], 0.0, None, ALU.is_ge))
                q(v.tensor_scalar(T["junk"][0:R, 0:P], DL[0:R, c, :], float(P), None, ALU.is_lt))
                q(v.tensor_tensor(T["valid"][0:R, c, :], T["valid"][0:R, c, :], T["junk"][0:R, 0:P], ALU.mult))
                for nb, pen in ((1, "penf"), (2, "penb")):
                    q(v.tensor_tensor(T[pen][0:R, c, :], EI[0:R, c, 0:P], EI[0:R, c, nb * P:(nb + 1) * P], ALU.not_equal))
                    q(v.tensor_tensor(T[pen][0:R, c, :], T[pen][0:R, c, :], T["valid"][0:R, c, :], ALU.mult))
                    q(v.tensor_scalar(T[pen][0:R, c, :], T[pen][0:R, c, :], -BIG, None, ALU.mult))
                q(v.tensor_scalar(T["valid"][0:R, c, :], T["valid"][0:R, c, :], -1.0, BIG, ALU.add, ALU.mult))
                q(v.tensor_copy(T["srow"][0:R, c, :], EI[0:R, c, 3 * P:4 * P]))
                q(v.tensor_copy(rows[0:R, 1, c, :], EI[0:R, c, 4 * P:5 * P]))
                q(v.tensor_copy(rows[0:R, 0, c, :], DL[0:R, c, :]))
            v.engine_nop().then_inc(s_rdy, 1)
            v.wait_ge(s_pe, 3)
            q(v.tensor_copy(T["SRC"][:, :], T["ps_a"][:, 0:NS]))
            q(v.tensor_copy(T["DC"][:, :], T["ps_b"][:, 0:NS]))

        @block.tensor
        def _(pe):
            pe.wait_ge(s_rdy, 1)
            pe.matmul(T["ps_a"][:, 0:ET], T["onesr"][0:1, :], T["st"][0:1, :], start=True, stop=True).then_inc(s_pe, 1)
            pe.wait_ge(s_v, 12)
            for c in range(SC):
                m = pe.transpose(T["ps_a"][0:1, c * SP_:(c + 1) * SP_], T["bS"][0:SP_, c:c + 1], T["ident"][0:SP_, 0:SP_])
            m.then_inc(s_pe, 1)
            pe.wait_ge(s_rdy, 2)
            for c in range(SC):
                pe.transpose(T["ps_a"][:, c * SP_:(c + 1) * SP_], T["srow"][0:SP_, c, :], T["ident"][0:SP_, 0:SP_])
                m = pe.transpose(T["ps_b"][:, c * SP_:(c + 1) * SP_], DL[0:SP_, c, :], T["ident"][0:SP_, 0:SP_])
            m.then_inc(s_pe, 1)


def each_group(eng, body):
    for u in range(UN):
        body(0, u)
    with eng.Fori(1, NG // UN, 1) as j:
        for u in range(UN):
            body(j, u)


def landed(j, u):
    return 16 * (j * (UN // RG) + u // RG + 1)


def feed_group(a, T, ixs, s_ix, s_used, g, u):
    wait(a, s_used, g - RG + 1)
    a.copy(ixs[:, u % RG, :], T["SRC"][:, bass.ds(g * G, G)]).then_inc(s_ix, 1)


def gather_rows(pool, table, ixs, rows, s_ix, s_g):
    def group(j, u):
        pool.wait_ge(s_ix, UN * j + u + 1)
        pool.nop(nofuse=True)
        for k in range(G):
            c0 = ((u % RG) * G + k) * C
            pool.indirect_dma_start(rows[:, c0:c0 + C], None, table,
                                    bass.IndirectOffsetOnAxis(ap=ixs[:, u % RG, k:k + 1], axis=0)).then_inc(s_g[u % RG][k], 16)
    with pool.Fori(0, NG // UN, 1) as j:
        for u in range(UN):
            group(j, u)


def phase_scores(nc, sem, T, d):
    s_bc = [sem(f"sc_rows{h}") for h in range(2)]
    s_g = [[sem(f"sc_gathered{h}{k}") for k in range(G)] for h in range(RG)]
    s_ix, s_oh, s_q, s_ku, s_pr, s_done, s_ld, s_rel = (sem("sc_" + n) for n in
        ("indices", "onehots", "products", "modified", "multiplied", "reduced", "loads", "relations"))
    with nc.Block() as block:
        @block.sync
        def _(sp):
            sp.dma_start(T["rel"][:, :], d["g_rel_w"]).then_inc(s_ld, 16)

            def group(j, u):
                g, h = UN * j + u, u % 2
                wait(sp, s_oh, 2 * g - 2)
                sp.dma_start(T["dlb"][:, h, :], d["dl_rows"][bass.ds(g * G, G), :].rearrange("s e -> (s e)").unsqueeze(0).broadcast_to([P, G * P])).then_inc(s_bc[h], 16)
                sp.dma_start(T["tyb"][:, h, :], d["ty_rows"][bass.ds(g * G, G), :].rearrange("s e -> (s e)").unsqueeze(0).broadcast_to([NREL, G * P])).then_inc(s_bc[h], 16)
            each_group(sp, group)

        @block.scalar
        def _(a):
            each_group(a, lambda j, u: feed_group(a, T, T["ixs"], s_ix, s_ku, UN * j + u, u))

        @block.gpsimd
        def _(pool):
            gather_rows(pool, d["ktab"], T["ixs"], T["KG"], s_ix, s_g)

        @block.tensor
        def _(pe):
            pe.wait_ge(s_rel, 6)

            def group(j, u):
                g, h = UN * j + u, u % 2
                pe.wait_ge(s_oh, 2 * g + 2)
                wait(pe, s_pr, g - 1)
                at = load_values(nc, mybir.EngineType.PE, T["qRow"][0:1, bass.ds(g * G, G)], (NT - 1) * 3 * C)
                for k in range(G):
                    for n in range(3):
                        pe.matmul(T["ps_qe"][:, h, k, :], T["PT"][:, h, k * P:(k + 1) * P], T["Q3"][:, bass.ds(at[k] + n * C, C)],
                                  start=(n == 0), stop=(n == 2))
                    for n in range(3):
                        m = pe.matmul(T["ps_u"][:, h, k, :], T["OT"][:, h, k * P:(k + 1) * P], T["rel3"][:, n, :],
                                      start=(n == 0), stop=(n == 2))
                m.then_inc(s_q, 1)
            each_group(pe, group)

        @block.vector
        def _(v):
            v.wait_ge(s_ld, 16)
            q = Seq(v, s_rel)
            q(v.tensor_scalar(T["rel"][:, :], T["rel"][:, :], 0.2, None, ALU.mult))
            q(v.tensor_copy(T["rel3"][:, 0, :], T["rel"][:, :]))
            q(v.tensor_tensor(T["rel"][:, :], T["rel"][:, :], T["rel3"][:, 0, :], ALU.subtract))
            q(v.tensor_copy(T["rel3"][:, 1, :], T["rel"][:, :]))
            q(v.tensor_tensor(T["rel"][:, :], T["rel"][:, :], T["rel3"][:, 1, :], ALU.subtract))
            q(v.tensor_copy(T["rel3"][:, 2, :], T["rel"][:, :]))

            def onehots(j, u):
                g, h = UN * j + u, u % 2
                v.wait_ge(s_bc[h], 32 * (j * (UN // 2) + u // 2 + 1))
                wait(v, s_q, g - 1)
                v.tensor_scalar(T["PT"][:, h, :], T["dlb"][:, h, :], T["iota_p"][:, 0:1], None, ALU.is_equal).then_inc(s_oh, 1)
                v.tensor_scalar(T["OT"][:, h, :], T["tyb"][:, h, :], T["iota_p"][0:NREL, 0:1], None, ALU.is_equal).then_inc(s_oh, 1)

            def modify(j, u):
                g, h = UN * j + u, u % 2
                for k in range(G):
                    v.wait_ge(s_g[u % RG][k], landed(j, u))
                v.wait_ge(s_q, g + 1)
                wait(v, s_done, g - 1)
                KG = T["KG"][:, (u % RG) * G * C:(u % RG + 1) * G * C]
                v.tensor_tensor(T["KU"][:, h, :].rearrange("p (s h d) -> p s h d", s=G, h=H), KG.rearrange("p (s h d) -> p s h d", s=G, h=H),
                                T["ps_u"][:, h, :, :].unsqueeze(2).broadcast_to([P, G, H, D]), ALU.add).then_inc(s_ku, 1)

            def multiply(j, u):
                g, h = UN * j + u, u % 2
                v.wait_ge(s_ku, g + 1)
                v.tensor_tensor(T["KU"][:, h, :], T["KU"][:, h, :], T["ps_qe"][:, h, :, :].rearrange("p s c -> p (s c)"), ALU.mult).then_inc(s_pr, 1)

            def reduce(j, u):
                g, h = UN * j + u, u % 2
                v.wait_ge(s_pr, g + 1)
                v.tensor_reduce(T["S"][:, bass.ds(g * G * H, G * H)], T["KU"][:, h, :].rearrange("p (x d) -> p x d", d=D), AX.X, ALU.add).then_inc(s_done, 1)

            def ahead(j, u):
                return (j, u - 1) if u else (j - 1, UN - 1)

            onehots(0, 0)
            onehots(0, 1)
            modify(0, 0)
            for u in range(2, UN):
                multiply(0, u - 2)
                onehots(0, u)
                modify(0, u - 1)
                reduce(0, u - 2)
            with v.Fori(1, NG // UN, 1) as j:
                for u in range(UN):
                    one = ahead(j, u)
                    two = ahead(*one)
                    multiply(*two)
                    onehots(j, u)
                    modify(*one)
                    reduce(*two)
            last = NG // UN - 1
            multiply(last, UN - 2)
            modify(last, UN - 1)
            reduce(last, UN - 2)
            multiply(last, UN - 1)
            reduce(last, UN - 1)
def phase_softmax_weights(nc, sem, T, d):
    s_v, s_pe, s_in, s_lr, s_e, s_c, s_x, s_ev = (sem("sm_" + n) for n in
        ("vector", "rows", "ready", "ends", "ends_turned", "carry", "exp", "evac"))
    R, B = SP_, SC * H
    ST, SX, F, penL, LR, E4, CR = (T[n] for n in ("ST", "SX", "F", "penL", "LR", "E4", "CR"))
    S4 = T["S"][:, :].rearrange("p (c s h) -> p c h s", c=SC, h=H)

    def flat(t):
        return t[0:R, :, :].rearrange("p b e -> p (b e)")

    def by_head(pen):
        return pen[0:R, :, :].unsqueeze(2).broadcast_to([R, SC, H, P])

    with nc.Block() as block:
        @block.tensor
        def _(pe):
            for c in range(SC):
                for h in range(H):
                    m = pe.transpose(T["ps_s"][0:R, c, h * P:(h + 1) * P], S4[:, c, h, :], T["ident"][:, :])
            m.then_inc(s_pe, 1)
            for w in range(2):
                pe.wait_ge(s_lr, w + 1)
                for x in range(2):
                    for c in range(SC):
                        m = pe.transpose(T["ps_e"][0:H, x, c * SP_:(c + 1) * SP_], LR[0:R, x, c * H:(c + 1) * H], T["ident"][0:R, 0:R])
                m.then_inc(s_e, 1)
                pe.wait_ge(s_c, w + 1)
                for c in range(SC):
                    m = pe.transpose(T["ps_c2"][0:R, c * H:(c + 1) * H], CR[0:H, c * SP_:(c + 1) * SP_], T["ident"][0:H, 0:H])
                m.then_inc(s_pe, 1)
            pe.wait_ge(s_x, 1)
            for c in range(SC):
                for h in range(H):
                    m = pe.transpose(T["ps_s"][:, c, h * P:h * P + R], ST[0:R, c * H + h, :], T["ident"][0:R, 0:R])
            m.then_inc(s_pe, 1)

        @block.scalar
        def _(a):
            a.wait_ge(s_in, 1)
            a.activation(ST[0:R, :, :], ST[0:R, :, :], ACT.Exp).then_inc(s_x, 1)

        @block.vector
        def _(v):
            q = Seq(v, s_v)
            v.wait_ge(s_pe, 1)
            q(v.tensor_tensor(ST[0:R, :, :].rearrange("p (c h) e -> p c h e", h=H), T["ps_s"][0:R, :, :].rearrange("p c (h e) -> p c h e", h=H),
                              by_head(T["valid"]), ALU.add))
            q(v.tensor_copy(flat(SX), flat(ST)))

            def direction(w, src, out, pen, edge, end, order):
                q(v.tensor_copy(penL[0:R, :, :].rearrange("p (c h) e -> p c h e", h=H), by_head(pen)))
                q(v.memset(penL[0:R, :, edge:edge + 1], -BIG))
                q(v.tensor_tensor_scan(order(out), order(penL), order(src), -BIG, ALU.add, ALU.max))
                q(v.tensor_copy(LR[0:R, 0, :], out[0:R, :, end]))
                q(v.tensor_reduce(T["rp"][0:R, :], pen[0:R, :, :], AX.X, ALU.min))
                v.tensor_copy(LR[0:R, 1, :].rearrange("p (c h) -> p c h", h=H),
                              T["rp"][0:R, :].unsqueeze(2).broadcast_to([R, SC, H])).then_inc(s_lr, 1)
                v.wait_ge(s_e, w + 1)
                q(v.tensor_copy(T["E2"][0:H, :, :], T["ps_e"][0:H, :, 0:NS]))
                if w == 0:
                    q(v.tensor_tensor_scan(E4[0:H, :], T["E2"][0:H, 1, :], T["E2"][0:H, 0, :], -BIG, ALU.add, ALU.max))
                    q(v.memset(CR[0:H, 0:1], -BIG))
                    v.tensor_copy(CR[0:H, 1:NS], E4[0:H, 0:NS - 1]).then_inc(s_c, 1)
                else:
                    q(v.tensor_tensor_scan(E4[0:H, ::-1], T["E2"][0:H, 1, ::-1], T["E2"][0:H, 0, ::-1], -BIG, ALU.add, ALU.max))
                    q(v.memset(CR[0:H, NS - 1:NS], -BIG))
                    v.tensor_copy(CR[0:H, 0:NS - 1], E4[0:H, 1:NS]).then_inc(s_c, 1)
                v.wait_ge(s_pe, w + 2)
                q(v.tensor_tensor(T["inj"][0:R, :].rearrange("p (c h) -> p c h", h=H), T["ps_c2"][0:R, :].rearrange("p (c h) -> p c h", h=H),
                                  pen[0:R, :, edge:edge + 1].broadcast_to([R, SC, H]), ALU.add))
                q(v.tensor_tensor(src[0:R, :, edge], src[0:R, :, edge], T["inj"][0:R, :], ALU.max))
                q(v.tensor_tensor_scan(order(out), order(penL), order(src), -BIG, ALU.add, ALU.max))

            direction(0, SX, F, T["penf"], 0, P - 1, flat)
            direction(1, F, SX, T["penb"], P - 1, 0, lambda t: flat(t)[:, ::-1])
            v.tensor_tensor(flat(ST), flat(ST), flat(SX), ALU.subtract).then_inc(s_in, 1)
            v.wait_ge(s_pe, 4)
            for c in range(SC):
                q(v.tensor_copy(S4[:, c, :, :], T["ps_s"][:, c, :].rearrange("p (h s) -> p h s", h=H)[:, :, 0:R]))


def phase_aggregate(nc, sem, T, d):
    s_g = [[sem(f"ag_gathered{h}{k}") for k in range(G)] for h in range(RG)]
    s_ix, s_oh, s_w, s_wc, s_o, s_acc = (sem("ag_" + n) for n in ("indices", "onehots", "weighted", "weights", "products", "added"))
    A = C + H
    WV = T["WV"]
    with nc.Block() as block:
        @block.scalar
        def _(a):
            def group(j, u):
                g, h = UN * j + u, u % 2
                feed_group(a, T, T["ixv"], s_ix, s_w, g, u)
                wait(a, s_o, (g - 1) * G)
                a.copy(WV[:, h, :, C:A], T["S"][:, bass.ds(g * G * H, G * H)].rearrange("p (k h) -> p k h", h=H)).then_inc(s_wc, 1)
            each_group(a, group)

        @block.gpsimd
        def _(pool):
            gather_rows(pool, d["vtab"], T["ixv"], T["VG"], s_ix, s_g)

        @block.tensor
        def _(pe):
            def group(j, u):
                g, h = UN * j + u, u % 2
                pe.wait_ge(s_oh, (g + 1) * G)
                pe.wait_ge(s_w, g + 1)
                pe.wait_ge(s_wc, g + 1)
                wait(pe, s_acc, (g - 1) * G + 1)
                for k in range(G):
                    pe.matmul(T["ps_o"][:, h * G + k, 0:A], T["PM"][:, h, k, :], WV[:, h, k, :], start=True, stop=True).then_inc(s_o, 1)
            each_group(pe, group)

        @block.vector
        def _(v):
            v.memset(T["ACC"][:, :], 0.0).then_inc(s_acc, 1)

            def weigh(j, u):
                g, h = UN * j + u, u % 2
                wait(v, s_o, (g - 1) * G)
                for k in range(G):
                    v.tensor_scalar(T["PM"][:, h, k, :], T["iota_f"][:, :], T["DC"][:, bass.ds(g * G + k, 1)], None, ALU.is_equal).then_inc(s_oh, 1)
                for k in range(G):
                    v.wait_ge(s_g[u % RG][k], landed(j, u))
                v.tensor_tensor(WV[:, h, :, 0:C].rearrange("p k (x d) -> p k x d", d=D),
                                T["VG"][:, (u % RG) * G * C:(u % RG + 1) * G * C].rearrange("p (k x d) -> p k x d", d=D, x=H),
                                T["S"][:, bass.ds(g * G * H, G * H)].rearrange("p (k x) -> p k x", x=H).unsqueeze(3).broadcast_to([P, G, H, D]), ALU.mult).then_inc(s_w, 1)

            def add(j, u):
                g, h = UN * j + u, u % 2
                at = load_values(nc, mybir.EngineType.DVE, T["aRow"][0:1, bass.ds(g * G, G)], (NT - 1) * A)
                for k in range(G):
                    v.wait_ge(s_o, g * G + k + 1)
                    v.wait_ge(s_acc, g * G + k + 1)
                    acc = T["ACC"][:, bass.ds(at[k], A)]
                    v.tensor_tensor(acc, acc, T["ps_o"][:, h * G + k, 0:A], ALU.add).then_inc(s_acc, 1)

            weigh(0, 0)
            for u in range(1, UN):
                weigh(0, u)
                add(0, u - 1)
            with v.Fori(1, NG // UN, 1) as j:
                weigh(j, 0)
                add(j - 1, UN - 1)
                for u in range(1, UN):
                    weigh(j, u)
                    add(j, u - 1)
            add(NG // UN - 1, UN - 1)
def phase_combine(nc, sem, T, d):
    s_ld, s_vt, s_i, s_v, s_c, s_pe, s_ct, s_m, s_a, s_t, s_tc, s_y, s_q, s_sq, s_xf, s_nd, s_ra, s_gl, s_ms, s_xn, s_pb, s_yn, s_yg = (sem("cb_" + n) for n in
        ("loads", "v_rows", "iota", "vector", "context", "context_turned", "context_copied", "mix_matrix", "scalar",
         "turned", "turned_copied", "rows", "mixed", "variance", "normed", "denominators", "reciprocals", "logits",
         "messages", "first_normed", "biases_added", "second_normed", "scaled"))
    A = C + H
    CT_ = 5
    NC_ = NT // CT_
    X, rstd, nmr, QT, ACC, Y, VB = (T[n] for n in ("X", "rstd", "nmr", "QT", "ACC", "Y", "VB"))
    ps_t2, ps_y, mT = T["ps_t2"], T["ps_y"], T["mT"]
    CH = [(n0, min(512, NT * P - n0)) for n0 in range(0, NT * P, 512)]
    acc3 = ACC[:, :].rearrange("p (t a) -> p t a", a=A)

    def chunk(t, c):
        return t[:, c * CT_:(c + 1) * CT_, :]

    def over_chunk(row):
        return row.unsqueeze(1).broadcast_to([P, CT_, C])

    with nc.Block() as block:
        @block.sync
        def _(sp):
            sp.dma_start(T["WP"][:, :, :], d["m_WprojT"].rearrange("(k p) n -> p k n", p=P)).then_inc(s_ld, 16)
            for c in range(NC_):
                sp.dma_start(chunk(VB, c), d["vtab"][c * CT_ * P:(c + 1) * CT_ * P, :].rearrange("(t p) c -> p t c", p=P)).then_inc(s_vt, 16)
            for n in ("gamma", "beta"):
                sp.dma_start(T[n][:, :], d["g_" + n].rearrange("(a n) -> a n", a=1).broadcast_to([P, C])).then_inc(s_ld, 16)
            for j, n in enumerate(("g_bo", "m_bproj")):
                sp.dma_start(T["bias2"][:, j, :], d[n].rearrange("(a n) -> a n", a=1).broadcast_to([P, C])).then_inc(s_ld, 16)
            sp.dma_start(T["Wo"][:, :, :], d["g_Wo"].rearrange("(k p) n -> p k n", p=P)).then_inc(s_ld, 16)
            sp.dma_start(T["GW"][:, :, :], d["f_gate_w"].rearrange("(k p) n -> p k n", p=P)).then_inc(s_ld, 16)
            sp.dma_start(T["gb"][:, :], d["f_gate_b"].rearrange("(a n) -> a n", a=1).broadcast_to([P, NEXP])).then_inc(s_ld, 16)

        @block.gpsimd
        def _(pool):
            pool.iota(T["bd_o"][:, :], [[0, P]], base=0, channel_multiplier=1).then_inc(s_i, 1)
            pool.iota(T["rank_i"][:, :], [[-1, NEXP]], base=NEXP, channel_multiplier=0).then_inc(s_i, 1)
            pool.iota(T["bd_e"][:, :], [[1, P]], base=0, channel_multiplier=0).then_inc(s_i, 1)
            pool.wait_ge(s_ld, 16 * 8)
            pool.tensor_tensor(T["bias2"][:, 1, :], T["bias2"][:, 1, :], T["beta"][:, :], ALU.add).then_inc(s_i, 1)
            pool.wait_ge(s_i, 4)
            for c in range(NC_):
                pool.wait_ge(s_xn, (c + 1) * CT_)
                pool.tensor_tensor(chunk(Y, c), chunk(Y, c), over_chunk(T["bias2"][:, 0, :]), ALU.add).then_inc(s_pb, 1)
                pool.tensor_tensor(chunk(X, c), chunk(X, c), over_chunk(T["bias2"][:, 1, :]), ALU.add).then_inc(s_pb, 1)
            for c in range(NC_):
                pool.wait_ge(s_yn, (c + 1) * CT_)
                pool.tensor_tensor(chunk(Y, c), chunk(Y, c), over_chunk(T["gamma"][:, :]), ALU.mult).then_inc(s_yg, 1)

        @block.vector
        def _(v):
            q = Seq(v, s_v)
            v.wait_ge(s_i, 3)
            q(v.tensor_copy(T["rank"][:, :], T["rank_i"][:, :]))
            q(v.tensor_scalar(T["bd_o"][:, :], T["bd_o"][:, :], 5, None, ALU.logical_shift_right))
            q(v.tensor_scalar(T["bd_e"][:, :], T["bd_e"][:, :], 5, None, ALU.logical_shift_right))
            q(v.tensor_tensor(T["BD"][:, :], T["bd_o"][:, :], T["bd_e"][:, :], ALU.is_equal))
            for a in range(2):
                q(v.tensor_scalar(T["KS"][:, a, :], T["BD"][:, :], T["CTX"][:, a, P:P + 1], None, ALU.mult))
                v.tensor_tensor(T["CB"][:, a, :], T["CTX"][:, a, 0:P], T["BD"][:, :], ALU.mult).then_inc(s_c, 1)
            v.wait_ge(s_pe, 1)
            v.tensor_copy(T["CT"][:, :, :], T["ps_s2"][:, 0:2 * P].rearrange("p (a c) -> p a c", a=2)).then_inc(s_ct, 1)
            v.wait_ge(s_pe, 2)
            v.tensor_copy(T["M"][:, :, :], T["ps_s2"][:, :].rearrange("p (a c) -> p a c", a=2)).then_inc(s_m, 1)
            for j, (a, n0, w) in enumerate([(a, n0, w) for a in range(2) for n0, w in CH]):
                v.wait_ge(s_nd, j + 1)
                wait(v, s_ra, j)
                q(v.tensor_scalar(T["dv"][:, 0:w], T["ps_d"][:, j % 2, 0:w], 1e-6, None, ALU.max))
                q(v.reciprocal(T["dv"][:, 0:w], T["dv"][:, 0:w]))
                v.tensor_tensor(QT[:, a, n0:n0 + w], QT[:, a, n0:n0 + w], T["dv"][:, 0:w], ALU.mult).then_inc(s_ra, 1)
            iz, dn = T["iz"], T["dn"]
            q(v.tensor_scalar(iz[:, :, :], acc3[:, :, C:A], 0.0, None, ALU.is_equal))
            q(v.tensor_tensor(dn[:, :, :], acc3[:, :, C:A], iz[:, :, :], ALU.add))
            q(v.reciprocal(dn[:, :, :], dn[:, :, :]))

            def messages(c):
                def by_head(t):
                    return t.rearrange("p t (h d) -> p t h d", h=H)

                def spread(t):
                    return chunk(t, c).unsqueeze(3).broadcast_to([P, CT_, H, D])
                vb, m = chunk(VB, c), acc3[:, c * CT_:(c + 1) * CT_, 0:C]
                v.wait_ge(s_vt, 16 * NC_)
                q(v.tensor_tensor(by_head(vb), by_head(vb), spread(iz), ALU.mult))
                q(v.tensor_tensor(m, m, vb, ALU.add))
                v.tensor_tensor(by_head(m), by_head(m), spread(dn), ALU.mult).then_inc(s_ms, 1)

            def head(i):
                v.wait_ge(s_y, i + 1)
                v.wait_ge(s_pb, 2 * (i // CT_) + 2)
                v.tensor_tensor(Y[:, i, :], Y[:, i, :], ps_y[:, i % 3, 0:C], ALU.add).then_inc(s_v, 1)
                v.tensor_tensor(X[:, i, :], X[:, i, :], ps_y[:, i % 3, C:2 * C], ALU.add).then_inc(s_q, 1)
                q.n += 1
                v.wait_ge(s_v, q.n)
                v.bn_stats(T["stats2"][:, i, :], Y[:, i, :]).then_inc(s_v, 1)
                q.n += 1

            messages(0)
            for i in range(NT):
                if i % CT_ == 0 and i // CT_ + 1 < NC_:
                    messages(i // CT_ + 1)
                head(i)

            def inverse_deviation(k):
                v.wait_ge(s_v, q.n)
                for t in range(NT):
                    v.bn_aggr(T["mv2"][:, t, :], T["stats2"][:, t, :]).then_inc(s_v, 1)
                q.n += NT
                v.wait_ge(s_v, q.n)
                v.tensor_scalar(rstd[:, :], T["mv2"][:, :, 1], EPS, None, ALU.add).then_inc(s_sq, 1)
                v.wait_ge(s_a, k)
                q(v.reciprocal(rstd[:, :], rstd[:, :]))
                q(v.tensor_tensor(nmr[:, :], T["mv2"][:, :, 0], rstd[:, :], ALU.mult))
                v.tensor_scalar(nmr[:, :], nmr[:, :], -1.0, None, ALU.mult).then_inc(s_sq, 1)
            inverse_deviation(1)
            v.wait_ge(s_q, NT)
            for c in range(NC_):
                v.wait_ge(s_yg, c + 1)
                q(v.tensor_tensor(chunk(X, c), chunk(X, c), chunk(Y, c), ALU.add))
                for t in range(c * CT_, (c + 1) * CT_):
                    v.bn_stats(T["stats2"][:, t, :], X[:, t, :]).then_inc(s_v, 1)
                q.n += CT_
            inverse_deviation(2)
            v.wait_ge(s_sq, 4)
            for i in range(NT):
                v.tensor_scalar(Y[:, i, :], X[:, i, :], rstd[:, i:i + 1], nmr[:, i:i + 1], ALU.mult, ALU.add).then_inc(s_xf, 1)
            v.wait_ge(s_gl, NT)
            LG, mx, eq = T["LG"], T["mx"], T["eq"]
            b3 = lambda t: t[:, :].unsqueeze(2).broadcast_to([P, NT, NEXP])
            q(v.tensor_tensor(LG[:, :, :], T["ps_s2"][:, 0:NT * NEXP].rearrange("p (t e) -> p t e", e=NEXP),
                              T["gb"][:, :].unsqueeze(1).broadcast_to([P, NT, NEXP]), ALU.add))
            q(v.tensor_reduce(mx[:, :], LG[:, :, :], AX.X, ALU.max))
            v.tensor_tensor(LG[:, :, :], LG[:, :, :], b3(mx), ALU.subtract).then_inc(s_sq, 1)
            v.wait_ge(s_a, 3)
            q(v.tensor_reduce(mx[:, :], LG[:, :, :], AX.X, ALU.add))
            q(v.reciprocal(mx[:, :], mx[:, :]))
            q(v.tensor_tensor(LG[:, :, :], LG[:, :, :], b3(mx), ALU.mult))
            q(v.memset(T["CW"][:, :, :], 0.0))
            for r in range(2):
                q(v.tensor_reduce(mx[:, :], LG[:, :, :], AX.X, ALU.max))
                q(v.tensor_tensor(eq[:, :, :], LG[:, :, :], b3(mx), ALU.is_equal))
                q(v.tensor_tensor(eq[:, :, :], eq[:, :, :], T["rank"][:, :].unsqueeze(1).broadcast_to([P, NT, NEXP]), ALU.mult))
                q(v.tensor_reduce(T["fr"][:, :], eq[:, :, :], AX.X, ALU.max))
                q(v.tensor_tensor(eq[:, :, :], T["rank"][:, :].unsqueeze(1).broadcast_to([P, NT, NEXP]), b3(T["fr"]), ALU.is_equal))
                q(v.tensor_tensor(T["sel"][:, :, :], eq[:, :, :], LG[:, :, :], ALU.mult))
                q(v.tensor_tensor(T["CW"][:, :, :], T["CW"][:, :, :], T["sel"][:, :, :], ALU.add))
                q(v.tensor_scalar(eq[:, :, :], eq[:, :, :], -2.0, None, ALU.mult))
                q(v.tensor_tensor(LG[:, :, :], LG[:, :, :], eq[:, :, :], ALU.add))

        @block.scalar
        def _(a):
            for i in range(NT):
                a.activation(Y[:, i, :], X[:, i, :], ACT.Identity, scale=rstd[:, i:i + 1], bias=nmr[:, i:i + 1]).then_inc(s_xn, 1)
            for i in range(NT):
                a.wait_ge(s_t, i + 1)
                wait(a, s_y, i - 1)
                a.copy(mT[:, i % 2, :, :], ps_t2[:, i % 2, 0:C].rearrange("p (k n) -> p k n", k=2)).then_inc(s_tc, 1)
            a.wait_ge(s_sq, 1)
            a.activation(rstd[:, :], rstd[:, :], ACT.Sqrt).then_inc(s_a, 1)
            a.wait_ge(s_sq, 2)
            for i in range(NT):
                a.activation(Y[:, i, :], Y[:, i, :], ACT.Identity, scale=rstd[:, i:i + 1], bias=nmr[:, i:i + 1]).then_inc(s_yn, 1)
            a.wait_ge(s_sq, 3)
            a.activation(rstd[:, :], rstd[:, :], ACT.Sqrt).then_inc(s_a, 1)
            for i in range(NT):
                a.wait_ge(s_t, NT + i + 1)
                a.copy(T["XF"][:, :, i * P:(i + 1) * P], ps_t2[:, i % 2, 0:C].rearrange("p (k n) -> p k n", k=2)).then_inc(s_tc, 1)
            a.wait_ge(s_sq, 5)
            a.activation(T["LG"][:, :, :], T["LG"][:, :, :], ACT.Exp).then_inc(s_a, 1)

        @block.tensor
        def _(pe):
            pe.wait_ge(s_c, 2)
            for a in range(2):
                m = pe.transpose(T["ps_s2"][:, a * P:(a + 1) * P], T["CB"][:, a, :], T["ident"][:, :])
            m.then_inc(s_pe, 1)
            pe.wait_ge(s_ld, 16 * 8)
            pe.wait_ge(s_ct, 1)
            for a in range(2):
                m = pe.matmul(T["ps_s2"][:, a * C:(a + 1) * C], T["CT"][:, a, :], T["WP"][:, a, :], start=True, stop=True)
            m.then_inc(s_pe, 1)
            for j, (a, n0, w) in enumerate([(a, n0, w) for a in range(2) for n0, w in CH]):
                wait(pe, s_ra, j - 1)
                pe.matmul(T["ps_d"][:, j % 2, 0:w], T["KS"][:, a, :], QT[:, a, n0:n0 + w], start=True, stop=True).then_inc(s_nd, 1)
            pe.wait_ge(s_m, 1)
            pe.wait_ge(s_ra, 2 * len(CH))

            def turn(n, rows):
                for k in range(2):
                    m = pe.transpose(ps_t2[:, n % 2, k * P:(k + 1) * P], rows[:, k * P:(k + 1) * P], T["ident"][:, :])
                m.then_inc(s_t, 1)

            def turn_messages(i):
                pe.wait_ge(s_ms, i // CT_ + 1)
                wait(pe, s_tc, i - 1)
                turn(i, acc3[:, i, 0:C])

            turn_messages(0)
            for i in range(NT):
                if i + 1 < NT:
                    turn_messages(i + 1)
                pe.wait_ge(s_tc, i + 1)
                wait(pe, s_q, i - 2)
                for k in range(2):
                    pe.matmul(ps_y[:, i % 3, 0:C], mT[:, i % 2, k, :], T["Wo"][:, k, :], start=(k == 0), stop=(k == 1))
                for k in range(2):
                    m = pe.matmul(ps_y[:, i % 3, C:2 * C], QT[:, k, i * P:(i + 1) * P], T["M"][:, k, :], start=(k == 0), stop=(k == 1))
                m.then_inc(s_y, 1)

            def turn_normed(i):
                pe.wait_ge(s_xf, i + 1)
                pe.wait_ge(s_tc, NT + i - 1)
                turn(i, Y[:, i, :])

            turn_normed(0)
            for i in range(NT):
                if i + 1 < NT:
                    turn_normed(i + 1)
                pe.wait_ge(s_tc, NT + i + 1)
                for k in range(2):
                    m = pe.matmul(T["ps_s2"][:, i * NEXP:(i + 1) * NEXP], T["XF"][:, k, i * P:(i + 1) * P], T["GW"][:, k, :],
                                  start=(k == 0), stop=(k == 1))
                m.then_inc(s_gl, 1)
def phase_experts(nc, sem, T, d):
    s_w = [sem(f"ex_weights{h}") for h in range(2)]
    s_b, s_h, s_hg, s_y, s_acc, s_ct, s_cc, s_o = (sem("ex_" + n) for n in
        ("b2", "hidden", "activated", "rows", "added", "weights_turned", "weights_copied", "stored"))
    TC = 5
    NCH, CW_ = NT // TC, TC * P
    HC = HID // P
    X, XF = T["X"], T["XF"]
    with nc.Block() as block:
        @block.sync
        def _(sp):
            sp.dma_start(T["b2"][:, :], d["f_b2"]).then_inc(s_b, 16)
            for e in range(NEXP):
                if e >= 2:
                    sp.wait_ge(s_acc, NT + (e - 1) * NT)
                sp.dma_start(T["W1"][:, e % 2, :, :], d["f_W1"][e].rearrange("(k p) n -> p k n", p=P)).then_inc(s_w[e % 2], 16)
                sp.dma_start(T["W2"][:, e % 2, :, :], d["f_W2"][e].rearrange("(k p) n -> p k n", p=P)).then_inc(s_w[e % 2], 16)
                sp.dma_start(T["b1"][:, e % 2, :], d["f_b1"][e].rearrange("(k p) -> p k", p=P), allow_slow_non_contiguous=True).then_inc(s_w[e % 2], 16)
            sp.wait_ge(s_acc, NT * (NEXP + 1))
            for t in range(NT):
                r = min(P, N - t * P)
                sp.dma_start(d["out"][t * P:t * P + r, :], X[0:r, t, :]).then_inc(s_o, 16)
            sp.wait_ge(s_o, 16 * NT)

        @block.tensor
        def _(pe):
            pe.wait_ge(s_b, 16)
            for t in range(NT):
                if t:
                    pe.wait_ge(s_cc, t)
                pe.transpose(T["ps_w"][0:NEXP, 0:P], T["CW"][:, t, :], T["ident"][:, :]).then_inc(s_ct, 1)
                pe.wait_ge(s_cc, t + 1)
                if t:
                    pe.wait_ge(s_acc, t)
                pe.matmul(T["ps_o2"][:, 0, 0:C], T["cT"][0:NEXP, :], T["b2"][:, :], start=True, stop=True).then_inc(s_y, 1)
            for e in range(NEXP):
                pe.wait_ge(s_w[e % 2], 48 * (e // 2 + 1))

                def chunk(j):
                    g = e * NCH + j
                    for m in range(HC):
                        if e > 0 or not isinstance(j, int):
                            pe.wait_ge(s_hg, (g - 1) * HC + m + 1)
                        for w in range(2):
                            for k in range(2):
                                r = pe.matmul(T["ps_h"][:, m % 2, w, 0:CW_ // 2], T["W1"][:, e % 2, k, m * P:(m + 1) * P],
                                              XF[:, k, bass.ds(j * CW_ + w * CW_ // 2, CW_ // 2)], start=(k == 0), stop=(k == 1))
                        r.then_inc(s_h, 1)
                        if m < HC - 1 and m >= 1:
                            pe.wait_ge(s_hg, g * HC + m)
                    pe.wait_ge(s_hg, (g + 1) * HC)
                    for t in range(TC):
                        n = g * TC + t
                        pe.wait_ge(s_acc, (n - 1 if t else n) + NT)
                        for m in range(HC):
                            r = pe.matmul(T["ps_o2"][:, t % 2, 0:C],
                                          T["HT"][:, m, t * P:(t + 1) * P], T["W2"][:, e % 2, m, :], start=(m == 0), stop=(m == HC - 1))
                        r.then_inc(s_y, 1)
                chunk(0)
                with pe.Fori(1, NCH, 1) as j:
                    chunk(j)

        @block.scalar
        def _(a):
            for t in range(NT):
                a.wait_ge(s_ct, t + 1)
                a.copy(T["cT"][0:NEXP, :], T["ps_w"][0:NEXP, 0:P]).then_inc(s_cc, 1)
            for e in range(NEXP):
                a.wait_ge(s_w[e % 2], 48 * (e // 2 + 1))

                def chunk(j):
                    g = e * NCH + j
                    a.wait_ge(s_y, g * TC + NT)
                    for m in range(HC):
                        a.wait_ge(s_h, g * HC + m + 1)
                        a.activation(T["HT"][:, m, :].rearrange("p (w n) -> p w n", w=2), T["ps_h"][:, m % 2, :, 0:CW_ // 2], ACT.Gelu,
                                     bias=T["b1"][:, e % 2, m:m + 1]).then_inc(s_hg, 1)
                chunk(0)
                with a.Fori(1, NCH, 1) as j:
                    chunk(j)

        @block.vector
        def _(v):
            for t in range(NT):
                v.wait_ge(s_y, t + 1)
                v.tensor_tensor(X[:, t, :], X[:, t, :], T["ps_o2"][:, 0, 0:C], ALU.add).then_inc(s_acc, 1)
            for e in range(NEXP):
                with v.Fori(0, NCH, 1) as j:
                    for t in range(TC):
                        n = (e * NCH + j) * TC + t
                        v.wait_ge(s_y, n + 1 + NT)
                        v.wait_ge(s_acc, n + NT)
                        x = X[:, bass.ds(j * TC + t, 1), :].rearrange("p a c -> p (a c)")
                        v.scalar_tensor_tensor(out=x, in0=T["ps_o2"][:, t % 2, 0:C], scalar=T["CW"][:, bass.ds(j * TC + t, 1), e:e + 1].rearrange("p a b -> p (a b)"),
                                               in1=x, op0=ALU.mult, op1=ALU.add).then_inc(s_acc, 1)
DRAM_IN = ["x", "edges", "g_query", "g_Wq", "g_bq", "g_Wk", "g_bk", "g_Wv", "g_bv", "g_rel_w", "g_Wo", "g_bo", "g_gamma",
           "g_beta", "m_WqT", "m_WkvT", "m_WprojT", "m_bproj", "f_gate_w", "f_gate_b", "f_W1", "f_b1", "f_W2", "f_b2"]


def build(nc, d, dbg=None):
    d["ktab"] = nc.dram_tensor("ktab", (NT * P, C), F32).ap()
    d["vtab"] = nc.dram_tensor("vtab", (NT * P, C), F32).ap()
    d["dl_rows"] = nc.dram_tensor("dl_rows", (NS, P), BF16).ap()
    d["ty_rows"] = nc.dram_tensor("ty_rows", (NS, P), BF16).ap()
    with ExitStack() as ctx:
        def sem(name):
            return ctx.enter_context(nc.semaphore(name))

        T = {}

        def sbuf(stack, spec):
            for n, (shape, dt) in spec.items():
                T[n] = stack.enter_context(nc.sbuf_tensor(n, list(shape), dt))

        def psum(stack, spec):
            for n, (shape, dt) in spec.items():
                T[n] = stack.enter_context(nc.psum_tensor(n, list(shape), dt))

        sbuf(ctx, {"X": ((P, NT, C), F32), "rstd": ((P, NT), F32), "nmr": ((P, NT), F32), "QT": ((P, 2, NT * P), F32),
                   "CTX": ((P, 2, P + 1), F32), "iota_f": ((P, P), F32), "iota_p": ((P, 1), F32), "ident": ((P, P), F32),
                   "onesr": ((P, P), F32), "zero": ((P, P + 1), F32)})
        sbuf(ctx, {"CW": ((P, NT, NEXP), F32), "ACC": ((P, NT * (C + H)), F32)})
        with ExitStack() as gnn:
            sbuf(gnn, {"Q3": ((P, NT * 3 * C), BF16)})
            with ExitStack() as ph:
                sbuf(ph, {"W": ((P, 2, 5 * C), F32), "WQM": ((P, 2, C), F32), "brow": ((1, 3 * C), F32), "qe": ((P, 2), F32),
                          "qbc": ((P, 2, P), F32), "bias": ((P, 3 * C), F32), "stats": ((P, NT, 6), F32), "qf": ((P, 2, C), F32), "mv": ((P, NT, 2), F32),
                          "xnb": ((P, 3, C), F32), "xnT": ((P, 2, 2, P), F32), "kvb": ((P, 2, 2 * C), F32),
                          "ex": ((P, 2, 2 * C), F32), "kb": ((P, 2, C), F32), "vb": ((P, 2, 2, P + 1), F32), "mask": ((P, NT), F32),
                          "iota_i": ((P, P), I32), "iota_pi": ((P, 1), I32), "node_i": ((P, NT), I32)})
                psum(ph, {"ps_n": ((P, 2, 3, 512), F32), "ps_t": ((P, 2, P), F32), "ps_c": ((P, 2, P + 1), F32)})
                phase_project(nc, sem, T, d)
            sbuf(gnn, {"SRC": ((P, NS), I32), "DC": ((P, NS), F32), "qRow": ((1, NS), I32), "aRow": ((1, NS), I32), "penf": ((P, SC, P), F32),
                       "penb": ((P, SC, P), F32), "valid": ((P, SC, P), F32), "S": ((P, NS * H), F32)})
            with ExitStack() as ph:
                sbuf(ph, {"last_i": ((1, ET), I32), "t_i": ((1, ET), I32), "hi": ((1, ET), F32), "st": ((1, ET), F32),
                          "s_i": ((P, SC), I32), "s_f": ((P, SC), F32), "junk": ((P, ET), F32), "cnt": ((P, SC), F32),
                          "bS": ((P, SC), F32), "b128": ((P, SC), F32), "tI": ((P, SC), I32), "EI": ((P, SC, 5 * P), I32),
                          "DL": ((P, SC, P), F32), "rows": ((P, 2, SC, P), BF16), "srow": ((P, SC, P), F32)})
                psum(ph, {"ps_a": ((P, 512), F32), "ps_b": ((P, 512), F32)})
                phase_steps(nc, sem, T, d)
            with ExitStack() as ph:
                sbuf(ph, {"dlb": ((P, 2, G * P), BF16), "tyb": ((NREL, 2, G * P), BF16), "ixs": ((P, RG, G), I32),
                          "KG": ((P, RG * G * C), F32), "PT": ((P, 2, G * P), BF16), "OT": ((NREL, 2, G * P), BF16), "rel3": ((NREL, 3, D), BF16),
                          "rel": ((NREL, D), F32), "KU": ((P, 2, G * C), F32)})
                psum(ph, {"ps_qe": ((P, 2, G, C), F32), "ps_u": ((P, 2, G, 2 * D), F32)})
                T["ps_u"] = T["ps_u"][:, :, :, 0:D]
                phase_scores(nc, sem, T, d)
            with ExitStack() as ph:
                sbuf(ph, {"ST": ((P, SC * H, P), F32), "SX": ((P, SC * H, P), F32), "F": ((P, SC * H, P), F32),
                          "penL": ((P, SC * H, P), F32), "LR": ((P, 2, SC * H), F32), "rp": ((P, SC), F32),
                          "E2": ((H, 2, NS), F32), "E4": ((H, NS), F32), "CR": ((H, NS), F32), "inj": ((P, SC * H), F32)})
                psum(ph, {"ps_s": ((P, SC, 512), F32), "ps_e": ((P, 2, 512), F32), "ps_c2": ((P, SC * H), F32)})
                phase_softmax_weights(nc, sem, T, d)
            with ExitStack() as ph:
                sbuf(ph, {"VG": ((P, RG * G * C), F32), "WV": ((P, 2, G, C + H), F32), "PM": ((P, 2, G, P), F32), "ixv": ((P, RG, G), I32)})
                psum(ph, {"ps_o": ((P, 2 * G, 512), F32)})
                phase_aggregate(nc, sem, T, d)
            if dbg == "S":
                s_o = sem("s_o")
                with nc.Block() as block:
                    @block.sync
                    def _(sp):
                        sp.dma_start(d["out_S"], T["S"][:, :]).then_inc(s_o, 16)
                        sp.dma_start(d["out_A"], T["ACC"][:, :]).then_inc(s_o, 16)
                        sp.wait_ge(s_o, 32)
                return
        sbuf(ctx, {"XF": ((P, 2, NT * P), F32)})
        with ExitStack() as ph:
            sbuf(ph, {"Y": ((P, NT, C), F32), "VB": ((P, NT, C), F32), "Wo": ((P, 2, C), F32), "WP": ((P, 2, C), F32), "GW": ((P, 2, NEXP), F32),
                      "bias2": ((P, 2, C), F32), "gb": ((P, NEXP), F32), "gamma": ((P, C), F32), "beta": ((P, C), F32),
                      "bd_o": ((P, P), I32), "bd_e": ((P, P), I32), "BD": ((P, P), F32), "KS": ((P, 2, P), F32),
                      "CB": ((P, 2, P), F32), "CT": ((P, 2, P), F32), "M": ((P, 2, C), F32), "dv": ((P, 512), F32),
                      "iz": ((P, NT, H), F32), "dn": ((P, NT, H), F32), "stats2": ((P, NT, 6), F32),
                      "mv2": ((P, NT, 2), F32), "mT": ((P, 2, 2, P), F32), "LG": ((P, NT, NEXP), F32),
                      "mx": ((P, NT), F32), "fr": ((P, NT), F32), "eq": ((P, NT, NEXP), F32), "sel": ((P, NT, NEXP), F32),
                      "rank": ((P, NEXP), F32), "rank_i": ((P, NEXP), I32)})
            psum(ph, {"ps_s2": ((P, 2 * C), F32), "ps_d": ((P, 2, 512), F32), "ps_t2": ((P, 2, 512), F32), "ps_y": ((P, 3, 2 * C), F32)})
            phase_combine(nc, sem, T, d)
        with ExitStack() as ph:
            sbuf(ph, {"W1": ((P, 2, 2, HID), F32), "W2": ((P, 2, HID // P, C), F32), "b1": ((P, 2, HID // P), F32),
                      "b2": ((NEXP, C), F32), "cT": ((NEXP, P), F32), "HT": ((P, HID // P, 5 * P), F32)})
            psum(ph, {"ps_w": ((P, P), F32), "ps_o2": ((P, 2, 512), F32), "ps_h": ((P, 2, 2, 512), F32)})
            phase_experts(nc, sem, T, d)
DBG=None
OUTS={"out":(N,C)}


def lay_out(inputs):
    import numpy as np
    g = {k: np.ascontiguousarray(v) for k, v in inputs.items()}
    a = {}
    a["x"] = np.concatenate([g["x"], np.zeros((NT * P - N, C), np.float32)])
    npad = ET * P - E_REAL
    pad = np.full((npad,), PADDST, np.int32)
    dst = np.concatenate([np.full((1,), -1, np.int32), g["dst"], pad, pad[:1]])
    z = np.zeros((npad,), np.int32)
    a["edges"] = np.ascontiguousarray(np.concatenate([v.reshape(ET, P) for v in (
        dst[1:-1], dst[:-2], dst[2:], np.concatenate([g["src"], z]), np.concatenate([g["edge_type_64"], z]))], axis=1))
    for n, m in (("g_query", "gnn_query_emb"), ("g_Wq", "gnn_Wq"), ("g_bq", "gnn_bq"), ("g_Wk", "gnn_Wk"), ("g_bk", "gnn_bk"),
                 ("g_Wv", "gnn_Wv"), ("g_bv", "gnn_bv"), ("g_rel_w", "gnn_rel_w"), ("g_Wo", "gnn_Wo"), ("g_bo", "gnn_bo"),
                 ("g_gamma", "gnn_gamma"), ("g_beta", "gnn_beta"), ("m_bproj", "mix_bproj"), ("f_gate_w", "ffn_gate_w"),
                 ("f_gate_b", "ffn_gate_b"), ("f_W1", "ffn_W1"), ("f_b1", "ffn_b1"), ("f_W2", "ffn_W2"), ("f_b2", "ffn_b2")):
        a[n] = g["L0_" + m]
    for n, m in (("m_WqT", "mix_Wq"), ("m_WkvT", "mix_Wkv"), ("m_WprojT", "mix_Wproj")):
        a[n] = np.ascontiguousarray(g["L0_" + m].T)
    return a


def kernel(**inputs):
    import concourse.bacc as _bacc
    from concourse import mybir as _mybir
    from concourse.bass_utils import run_bass_kernel_spmd as _run

    nc = _bacc.Bacc("TRN2", target_bir_lowering=False, num_devices=1)
    a = lay_out(inputs)
    d = {n: nc.dram_tensor(f"in_{n}_dram", a[n].shape, _mybir.dt.from_np(a[n].dtype), kind="ExternalInput").ap() for n in DRAM_IN}
    for n, (shape) in OUTS.items():
        d[n] = nc.dram_tensor(n + "_dram", shape, F32, kind="ExternalOutput").ap()
    build(nc, d, DBG)
    r = _run(nc, [{f"in_{n}_dram": a[n] for n in DRAM_IN}], core_ids=[0])
    res = r.results[0]
    return tuple(res[n + "_dram"] for n in OUTS) if len(OUTS) > 1 else res["out_dram"][0:N]
```

```python
from contextlib import ExitStack

import concourse.bass as bass
from concourse import mybir

F32 = mybir.dt.float32
BF16 = mybir.dt.bfloat16
I32 = mybir.dt.int32
ALU = mybir.AluOpType
ACT = mybir.ActivationFunctionType
AX = mybir.AxisListType

P = 128
N = 3125
C = 256
NT = (N + P - 1) // P
E_REAL = 53125
ET = (E_REAL + P - 1) // P
H, D = 4, 64
NREL = 64
MD = 32
NS = ET + NT - 1
SC = 4
SP_ = NS // SC
G = 4
NG = NS // G
UN = 10
RG = 5
RV = 10
BIG = 1.0e30
EPS = 1.0e-5
NEXP, HID = 8, 512
LAST = N - (NT - 1) * P
HC = HID // P
W1C = 2 * HID + HC
SLOTS = 128
NTILE = (2 * N + NEXP * (SLOTS - 1)) // SLOTS
UE = 4
NSLOT = NTILE * SLOTS
PADDST = 4095
assert NTILE % UE == 0 and N % P != 0
assert SC * SP_ == NS and NG * G == NS and NG % UN == 0 and UN % RG == 0 and RV == UN and UN % 2 == 0


class Seq:

    def __init__(self, eng, sem, base=0, per=None):
        self.eng, self.sem, self.base, self.n, self.per = eng, sem, base, 0, per

    def __call__(self, ins):
        ins.then_inc(self.sem, 1)
        self.n += 1
        self.eng.wait_ge(self.sem, self.base + self.n)

    def close(self):
        assert self.per is None or self.n == self.per, (self.n, self.per)


def wait(eng, sem, count):
    if isinstance(count, int) and count <= 0:
        return
    eng.wait_ge(sem, count)


def each_tile(eng, body):
    for i in range(NT):
        body(i, i % 2)


def load_values(nc, engine, ap, high):
    return nc.values_load_multi_w_load_instructions(ap, engines=(engine,), min_val=0, max_val=high,
                                                    skip_runtime_bounds_check_because="the step list holds node blocks only")[1]


def phase_project(nc, sem, T, d):
    s_ld, s_bias, s_id, s_one, s_v, s_sq, s_a, s_p = (sem("pj_" + n) for n in
        ("loads", "bias_rows", "iota", "constants", "vector", "variance", "deviation", "pool"))
    s_xn, s_t, s_tc, s_mm, s_r, s_e, s_vb, s_k, s_qf, s_q3, s_kvb, s_ctx = (sem("pj_" + n) for n in
        ("normed", "turned", "turned_copied", "products", "negative_part", "exp", "v_copied", "evacuated", "q_ready", "q_split",
         "kv_ready", "context"))
    s_kv = [sem(f"pj_kv_stored{h}") for h in range(2)]
    X, W, WQM, rstd, nmr = T["X"], T["W"], T["WQM"], T["rstd"], T["nmr"]
    xnb, xnT, kvb, ex, kb, vb, qf = (T[n] for n in ("xnb", "xnT", "kvb", "ex", "kb", "vb", "qf"))
    ps_t, ps_n, ps_c = T["ps_t"], T["ps_n"], T["ps_c"]
    XQ = 5
    XT_ = NT // XQ
    s_x = [sem(f"pj_x{c}") for c in range(XQ)]
    with nc.Block() as block:
        @block.sync
        def _(sp):
            def load_x(c):
                t = c * XT_
                sp.dma_start(X[:, t:t + XT_, :], d["x"][t * P:(t + XT_) * P, :].rearrange("(t p) c -> p t c", p=P)).then_inc(s_x[c], 16)
            load_x(0)
            for j, n in enumerate(("g_Wq", "g_Wk", "g_Wv")):
                sp.dma_start(W[:, :, j * C:(j + 1) * C], d[n].rearrange("(k p) n -> p k n", p=P)).then_inc(s_ld, 16)
            sp.dma_start(W[:, :, 3 * C:5 * C], d["m_WkvT"].rearrange("(k p) n -> p k n", p=P)).then_inc(s_ld, 16)
            sp.dma_start(WQM[:, :, :], d["m_WqT"].rearrange("(k p) n -> p k n", p=P)).then_inc(s_ld, 16)
            for j, n in enumerate(("g_bq", "g_bk", "g_bv")):
                sp.dma_start(T["brow"][0:1, j * C:(j + 1) * C], d[n].rearrange("(a n) -> a n", a=1)).then_inc(s_ld, 16)
            for k in range(2):
                sp.dma_start(T["qe"][:, k:k + 1], d["g_query"][k * P:(k + 1) * P].rearrange("(p a) -> p a", a=1)).then_inc(s_ld, 16)
            for c in range(1, XQ):
                load_x(c)

            def store(i, h):
                sp.wait_ge(s_kvb, 2 * i + 2)
                sp.dma_start(d["ktab"][i * P:(i + 1) * P, :], kvb[:, h, 0:C]).then_inc(s_kv[h], 16)
                sp.dma_start(d["vtab"][i * P:(i + 1) * P, :], kvb[:, h, C:2 * C]).then_inc(s_kv[h], 16)
            each_tile(sp, store)
            for h in range(2):
                sp.wait_ge(s_kv[h], 32 * ((NT + 1 - h) // 2))

        @block.gpsimd
        def _(pool):
            pool.iota(T["iota_i"][:, :], [[1, P]], base=0, channel_multiplier=0).then_inc(s_id, 1)
            pool.iota(T["iota_pi"][:, :], [[1, 1]], base=0, channel_multiplier=1).then_inc(s_id, 1)
            pool.iota(T["node_i"][:, :], [[P, NT]], base=0, channel_multiplier=1).then_inc(s_id, 1)

            def split(i, h):
                q = Seq(pool, s_p, 4 * i, 4)

                def part(n):
                    return T["Q3"][:, (i * 3 + n) * C:(i * 3 + n + 1) * C]
                pool.wait_ge(s_qf, i + 1)
                q(pool.tensor_copy(part(0), qf[:, h, :]))
                q(pool.tensor_tensor(qf[:, h, :], qf[:, h, :], part(0), ALU.subtract))
                q(pool.tensor_copy(part(1), qf[:, h, :]))
                q(pool.tensor_tensor(qf[:, h, :], qf[:, h, :], part(1), ALU.subtract))
                q.close()
                pool.tensor_copy(part(2), qf[:, h, :]).then_inc(s_q3, 1)
            each_tile(pool, split)

        @block.vector
        def _(v):
            q = Seq(v, s_v)
            v.memset(T["onesr"][:, :], 1.0).then_inc(s_one, 1)
            v.memset(T["zero"][:, :], 0.0).then_inc(s_one, 1)
            v.wait_ge(s_id, 3)
            q(v.tensor_copy(T["iota_f"][:, :], T["iota_i"][:, :]))
            q(v.tensor_copy(T["iota_p"][:, :], T["iota_pi"][:, :]))
            q(v.tensor_copy(T["mask"][:, :], T["node_i"][:, :]))
            q(v.tensor_scalar(T["mask"][:, :], T["mask"][:, :], float(N), None, ALU.is_lt))
            v.tensor_scalar(T["ident"][:, :], T["iota_f"][:, :], T["iota_p"][:, 0:1], None, ALU.is_equal).then_inc(s_one, 1)
            v.wait_ge(s_ld, 16 * 10)
            q(v.tensor_scalar(T["qe"][:, :], T["qe"][:, :], 0.1, None, ALU.mult))
            v.wait_ge(s_one, 3)
            for k in range(2):
                v.tensor_scalar(T["qbc"][:, k, :], T["onesr"][:, :], T["qe"][:, k:k + 1], None, ALU.mult).then_inc(s_sq, 1)

            def statistics(c):
                t0, t1 = c * XT_, (c + 1) * XT_
                v.wait_ge(s_x[c], 16)
                for t in range(t0, t1):
                    v.bn_stats(T["stats"][:, t, :], X[:, t, :]).then_inc(s_v, 1)
                q.n += XT_
                v.wait_ge(s_v, q.n)
                for t in range(t0, t1):
                    v.bn_aggr(T["mv"][:, t, :], T["stats"][:, t, :]).then_inc(s_v, 1)
                q.n += XT_
                v.wait_ge(s_v, q.n)
                v.tensor_scalar(rstd[:, t0:t1], T["mv"][:, t0:t1, 1], EPS, None, ALU.add).then_inc(s_sq, 1)
                v.wait_ge(s_a, c + 1)
                q(v.reciprocal(rstd[:, t0:t1], rstd[:, t0:t1]))
                q(v.tensor_tensor(nmr[:, t0:t1], T["mv"][:, t0:t1, 0], rstd[:, t0:t1], ALU.mult))
                q(v.tensor_scalar(nmr[:, t0:t1], nmr[:, t0:t1], -1.0, None, ALU.mult))

            statistics(0)
            v.wait_ge(s_mm, 1)
            q(v.tensor_copy(T["bias"][:, 0:512], ps_n[:, 0, 0, :]))
            q(v.tensor_copy(T["bias"][:, 512:768], ps_n[:, 0, 1, 0:256]))
            v.tensor_scalar(T["bias"][:, 0:C], T["bias"][:, 0:C], 0.125, None, ALU.mult).then_inc(s_bias, 1)
            for h in range(2):
                q(v.tensor_copy(vb[:, h, :, P:P + 1], T["onesr"][:, 0:2].unsqueeze(2)))

            def normalise(i):
                wait(v, s_t, i - 2)
                v.tensor_scalar(xnb[:, i % 3, :], X[:, i, :], rstd[:, i:i + 1],
                                nmr[:, i:i + 1], ALU.mult, ALU.add).then_inc(s_xn, 1)

            def evacuate(i, h):
                v.wait_ge(s_mm, i + 2)
                wait(v, s_q3, i - 1)
                v.scalar_tensor_tensor(out=qf[:, h, :], in0=ps_n[:, h, 0, 0:C], scalar=0.125,
                                       in1=T["bias"][:, 0:C], op0=ALU.mult, op1=ALU.add).then_inc(s_qf, 1)
                wait(v, s_kv[h], (i - h) * 16)
                v.tensor_tensor(kvb[:, h, 0:C], ps_n[:, h, 0, C:2 * C], T["bias"][:, C:2 * C], ALU.add).then_inc(s_kvb, 1)
                v.wait_ge(s_e, i + 1)
                v.tensor_tensor(kvb[:, h, C:2 * C], ps_n[:, h, 1, 0:C], T["bias"][:, 2 * C:3 * C], ALU.add).then_inc(s_kvb, 1)
                v.scalar_tensor_tensor(out=T["QT"][:, :, i * P:(i + 1) * P], in0=ps_n[:, h, 2, C:2 * C].rearrange("p (a c) -> p a c", a=2),
                                       scalar=0.0, in1=ex[:, h, C:2 * C].rearrange("p (a c) -> p a c", a=2), op0=ALU.max, op1=ALU.add).then_inc(s_v, 1)
                wait(v, s_ctx, i - 1)
                v.scalar_tensor_tensor(out=kb[:, h, :], in0=ps_n[:, h, 1, C:2 * C], scalar=0.0, in1=ex[:, h, 0:C], op0=ALU.max,
                                       op1=ALU.add).then_inc(s_v, 1)
                q.n += 2
                v.wait_ge(s_v, q.n)
                v.tensor_scalar(kb[:, h, :], kb[:, h, :], T["mask"][:, i:i + 1], None, ALU.mult).then_inc(s_k, 1)

            normalise(0)
            normalise(1)
            v.wait_ge(s_bias, 1)
            for i in range(NT):
                if i % XT_ == 1 and i // XT_ + 1 < XQ:
                    statistics(i // XT_ + 1)
                if i + 2 < NT:
                    normalise(i + 2)
                evacuate(i, i % 2)
            v.wait_ge(s_ctx, NT + 1)
            v.tensor_copy(T["CTX"][:, :, :], ps_c[:, :, :]).then_inc(s_v, 1)

        @block.scalar
        def _(a):
            def deviation(c):
                a.wait_ge(s_sq, c + 3)
                r = rstd[:, c * XT_:(c + 1) * XT_]
                a.activation(r, r, ACT.Sqrt).then_inc(s_a, 1)

            def copy_turned(i, h):
                a.wait_ge(s_t, i + 1)
                wait(a, s_mm, i)
                a.copy(xnT[:, h, :, :], ps_t[:, :, :]).then_inc(s_tc, 1)

            def parts(i, h):
                a.wait_ge(s_mm, i + 2)
                wait(a, s_k, i - 1)
                a.activation(ex[:, h, 0:C], ps_n[:, h, 1, C:2 * C], ACT.Relu, scale=-1.0).then_inc(s_r, 1)
                a.activation(ex[:, h, C:2 * C], ps_n[:, h, 2, C:2 * C], ACT.Relu, scale=-1.0).then_inc(s_r, 1)
                wait(a, s_ctx, i - 1)
                a.copy(vb[:, h, :, 0:P], ps_n[:, h, 2, 0:C].rearrange("p (a c) -> p a c", a=2)).then_inc(s_vb, 1)
                a.wait_ge(s_r, 2 * i + 2)
                a.wait_ge(s_vb, i + 1)
                a.activation(ex[:, h, :], ex[:, h, :], ACT.Exp, scale=-1.0).then_inc(s_e, 1)

            deviation(0)
            copy_turned(0, 0)
            for i in range(NT):
                if i + 1 < NT:
                    copy_turned(i + 1, (i + 1) % 2)
                if i % XT_ == 1 and i // XT_ + 1 < XQ:
                    deviation(i // XT_ + 1)
                parts(i, i % 2)

        @block.tensor
        def _(pe):
            pe.wait_ge(s_one, 3)
            pe.wait_ge(s_ld, 160)
            pe.wait_ge(s_sq, 2)
            for b, (c0, c1) in enumerate(((0, 512), (512, 768))):
                for k in range(2):
                    pe.matmul(ps_n[:, 0, b, 0:c1 - c0], T["qbc"][:, k, :], W[:, k, c0:c1], start=(k == 0), stop=False)
                m = pe.matmul(ps_n[:, 0, b, 0:c1 - c0], T["onesr"][0:1, :], T["brow"][0:1, c0:c1], start=False, stop=True)
            m.then_inc(s_mm, 1)
            for a in range(2):
                pe.matmul(ps_c[:, a, :], T["zero"][:, 0:P], T["zero"][:, 0:P + 1], start=True, stop=False, skip_group_check=True)

            def turn(i, h):
                pe.wait_ge(s_xn, i + 1)
                wait(pe, s_tc, i)
                pe.transpose(ps_t[:, 0, :], xnb[:, i % 3, 0:P], T["ident"][:, :])
                pe.transpose(ps_t[:, 1, :], xnb[:, i % 3, P:C], T["ident"][:, :]).then_inc(s_t, 1)

            def project(i, h):
                pe.wait_ge(s_tc, i + 1)
                wait(pe, s_k, i - 1)
                wait(pe, s_vb, i - 1)
                for b, (c0, c1) in enumerate(((0, 512), (512, 1024), (1024, 1280))):
                    for k in range(2):
                        pe.matmul(ps_n[:, h, b, 0:c1 - c0], xnT[:, h, k, :], W[:, k, c0:c1], start=(k == 0), stop=(k == 1))
                for o in range(2):
                    for k in range(2):
                        m = pe.matmul(ps_n[:, h, 2, C + o * P:C + (o + 1) * P], WQM[:, k, o * P:(o + 1) * P], xnT[:, h, k, :],
                                      start=(k == 0), stop=(k == 1), skip_group_check=True)
                m.then_inc(s_mm, 1)

            def context(i, h):
                pe.wait_ge(s_k, i + 1)
                pe.wait_ge(s_vb, i + 1)
                for a in range(2):
                    m = pe.matmul(ps_c[:, a, :], kb[:, h, a * P:(a + 1) * P], vb[:, h, a, :], start=False, stop=False, skip_group_check=True)
                m.then_inc(s_ctx, 1)

            pe.wait_ge(s_bias, 1)
            turn(0, 0)
            for i in range(NT):
                if i + 1 < NT:
                    turn(i + 1, (i + 1) % 2)
                project(i, i % 2)
                if i:
                    context(i - 1, (i - 1) % 2)
            context(NT - 1, (NT - 1) % 2)
            for a in range(2):
                m = pe.matmul(ps_c[:, a, :], T["zero"][:, 0:P], T["zero"][:, 0:P + 1], start=False, stop=True, skip_group_check=True)
            m.then_inc(s_ctx, 1)


def phase_steps(nc, sem, T, d):
    s_ld, s_v, s_io, s_pe, s_cp, s_g, s_st, s_rdy, s_tr, s_ev = (sem("st_" + n) for n in
        ("loads", "vector", "iota", "products", "copied", "gathered", "stored", "ready", "transposed", "evac"))
    EI, rows, DL = T["EI"], T["rows"], T["DL"]
    with nc.Block() as block:
        @block.sync
        def _(sp):
            sp.dma_start(T["last_i"][0:1, :], d["edges"][:, P - 1:P].rearrange("t a -> a t"), allow_slow_non_contiguous=True).then_inc(s_ld, 16)
            sp.wait_ge(s_rdy, 2)
            for c in range(SC):
                sp.dma_start(d["dl_rows"][c * SP_:(c + 1) * SP_, :], rows[0:SP_, 0, c, :]).then_inc(s_st, 16)
                sp.dma_start(d["ty_rows"][c * SP_:(c + 1) * SP_, :], rows[0:SP_, 1, c, :]).then_inc(s_st, 16)
            sp.wait_ge(s_st, 2 * SC * 16)

        @block.gpsimd
        def _(pool):
            pool.iota(T["t_i"][0:1, :], [[1, ET]], base=0, channel_multiplier=0).then_inc(s_io, 1)
            pool.iota(T["s_i"][:, :], [[SP_, SC]], base=0, channel_multiplier=1).then_inc(s_io, 1)
            pool.wait_ge(s_cp, 1)
            for c in range(SC):
                pool.indirect_dma_start(EI[0:SP_, c, :], None, d["edges"], bass.IndirectOffsetOnAxis(ap=T["tI"][0:SP_, c:c + 1], axis=0)).then_inc(s_g, 16)

        @block.vector
        def _(v):
            q = Seq(v, s_v)
            v.wait_ge(s_ld, 16)
            v.wait_ge(s_io, 2)
            q(v.tensor_scalar(T["last_i"][0:1, :], T["last_i"][0:1, :], 7, None, ALU.logical_shift_right))
            q(v.tensor_copy(T["hi"][0:1, :], T["last_i"][0:1, :]))
            q(v.tensor_scalar(T["hi"][0:1, :], T["hi"][0:1, :], float(NT - 1), None, ALU.min))
            q(v.tensor_copy(T["st"][0:1, :], T["t_i"][0:1, :]))
            v.tensor_tensor(T["st"][0:1, 1:ET], T["st"][0:1, 1:ET], T["hi"][0:1, 0:ET - 1], ALU.add).then_inc(s_rdy, 1)
            q(v.tensor_copy(T["s_f"][:, :], T["s_i"][:, :]))
            v.wait_ge(s_pe, 1)
            for c in range(SC):
                q(v.tensor_scalar(T["junk"][:, :], T["ps_a"][:, 0:ET], T["s_f"][:, c:c + 1], None, ALU.is_le, ALU.add,
                                  accum_out=T["cnt"][:, c:c + 1]))
            q(v.tensor_scalar(T["cnt"][:, :], T["cnt"][:, :], -1.0, None, ALU.add))
            q(v.tensor_tensor(T["bS"][:, :], T["s_f"][:, :], T["cnt"][:, :], ALU.subtract))
            v.tensor_copy(T["tI"][:, :], T["cnt"][:, :]).then_inc(s_cp, 1)
            q(v.tensor_scalar(T["b128"][:, :], T["bS"][:, :], float(P), None, ALU.mult))
            v.wait_ge(s_pe, 2)
            q(v.tensor_scalar(T["qRow"][0:1, :], T["ps_a"][0:1, 0:NS], float(3 * C), None, ALU.mult))
            q(v.tensor_scalar(T["aRow"][0:1, :], T["ps_a"][0:1, 0:NS], float(C + H), None, ALU.mult))
            v.wait_ge(s_g, 16 * SC)
            R = SP_
            for c in range(SC):
                q(v.tensor_copy(DL[0:R, c, :], EI[0:R, c, 0:P]))
                q(v.tensor_scalar(DL[0:R, c, :], DL[0:R, c, :], T["b128"][0:R, c:c + 1], -1.0, ALU.subtract, ALU.max))
                q(v.tensor_scalar(DL[0:R, c, :], DL[0:R, c, :], float(P), None, ALU.min))
                q(v.tensor_scalar(T["valid"][0:R, c, :], DL[0:R, c, :], 0.0, None, ALU.is_ge))
                q(v.tensor_scalar(T["junk"][0:R, 0:P], DL[0:R, c, :], float(P), None, ALU.is_lt))
                q(v.tensor_tensor(T["valid"][0:R, c, :], T["valid"][0:R, c, :], T["junk"][0:R, 0:P], ALU.mult))
                for nb, pen in ((1, "penf"), (2, "penb")):
                    q(v.tensor_tensor(T[pen][0:R, c, :], EI[0:R, c, 0:P], EI[0:R, c, nb * P:(nb + 1) * P], ALU.not_equal))
                    q(v.tensor_tensor(T[pen][0:R, c, :], T[pen][0:R, c, :], T["valid"][0:R, c, :], ALU.mult))
                    q(v.tensor_scalar(T[pen][0:R, c, :], T[pen][0:R, c, :], -BIG, None, ALU.mult))
                q(v.tensor_scalar(T["valid"][0:R, c, :], T["valid"][0:R, c, :], -1.0, BIG, ALU.add, ALU.mult))
                q(v.tensor_copy(T["srow"][0:R, c, :], EI[0:R, c, 3 * P:4 * P]))
                q(v.tensor_copy(rows[0:R, 1, c, :], EI[0:R, c, 4 * P:5 * P]))
                q(v.tensor_copy(rows[0:R, 0, c, :], DL[0:R, c, :]))
            v.engine_nop().then_inc(s_rdy, 1)
            v.wait_ge(s_pe, 3)
            q(v.tensor_copy(T["SRC"][:, :], T["ps_a"][:, 0:NS]))
            q(v.tensor_copy(T["DC"][:, :], T["ps_b"][:, 0:NS]))

        @block.tensor
        def _(pe):
            pe.wait_ge(s_rdy, 1)
            pe.matmul(T["ps_a"][:, 0:ET], T["onesr"][0:1, :], T["st"][0:1, :], start=True, stop=True).then_inc(s_pe, 1)
            pe.wait_ge(s_v, 12)
            for c in range(SC):
                m = pe.transpose(T["ps_a"][0:1, c * SP_:(c + 1) * SP_], T["bS"][0:SP_, c:c + 1], T["ident"][0:SP_, 0:SP_])
            m.then_inc(s_pe, 1)
            pe.wait_ge(s_rdy, 2)
            for c in range(SC):
                pe.transpose(T["ps_a"][:, c * SP_:(c + 1) * SP_], T["srow"][0:SP_, c, :], T["ident"][0:SP_, 0:SP_])
                m = pe.transpose(T["ps_b"][:, c * SP_:(c + 1) * SP_], DL[0:SP_, c, :], T["ident"][0:SP_, 0:SP_])
            m.then_inc(s_pe, 1)


def each_group(eng, body):
    for u in range(UN):
        body(0, u)
    with eng.Fori(1, NG // UN, 1) as j:
        for u in range(UN):
            body(j, u)


def landed(ring, j, u):
    return 16 * G * (j * (UN // ring) + u // ring + 1)


def feed_group(a, T, ixs, s_ix, s_used, ring, g, u):
    wait(a, s_used, g - ring + 1)
    a.copy(ixs[:, u % ring, :], T["SRC"][:, bass.ds(g * G, G)]).then_inc(s_ix, 1)


def gather_group(pool, table, ixs, rows, s_ix, s_g, ring, j, u):
    pool.wait_ge(s_ix, UN * j + u + 1)
    pool.nop(nofuse=True)
    for k in range(G):
        c0 = ((u % ring) * G + k) * C
        pool.indirect_dma_start(rows[:, c0:c0 + C], None, table,
                                bass.IndirectOffsetOnAxis(ap=ixs[:, u % ring, k:k + 1], axis=0)).then_inc(s_g[u % ring], 16)


def gather_rows(pool, table, ixs, rows, s_ix, s_g, ring, first=0):
    for u in range(first, UN):
        gather_group(pool, table, ixs, rows, s_ix, s_g, ring, 0, u)
    with pool.Fori(1, NG // UN, 1) as j:
        for u in range(UN):
            gather_group(pool, table, ixs, rows, s_ix, s_g, ring, j, u)


def phase_scores(nc, sem, T, d):
    s_bc = [sem(f"sc_rows{h}") for h in range(2)]
    s_g = [sem(f"sc_gathered{h}") for h in range(RG)]
    s_ix, s_oh, s_q, s_ku, s_pr, s_done, s_ld, s_rel = (sem("sc_" + n) for n in
        ("indices", "onehots", "products", "modified", "multiplied", "reduced", "loads", "relations"))
    with nc.Block() as block:
        @block.sync
        def _(sp):
            sp.dma_start(T["rel"][:, :], d["g_rel_w"]).then_inc(s_ld, 16)

            def group(j, u):
                g, h = UN * j + u, u % 2
                wait(sp, s_oh, 2 * g - 2)
                sp.dma_start(T["dlb"][:, h, :], d["dl_rows"][bass.ds(g * G, G), :].rearrange("s e -> (s e)").unsqueeze(0).broadcast_to([P, G * P])).then_inc(s_bc[h], 16)
                sp.dma_start(T["tyb"][:, h, :], d["ty_rows"][bass.ds(g * G, G), :].rearrange("s e -> (s e)").unsqueeze(0).broadcast_to([NREL, G * P])).then_inc(s_bc[h], 16)
            each_group(sp, group)

        @block.scalar
        def _(a):
            each_group(a, lambda j, u: feed_group(a, T, T["ixs"], s_ix, s_ku, RG, UN * j + u, u))

        @block.gpsimd
        def _(pool):
            gather_rows(pool, d["ktab"], T["ixs"], T["KG"], s_ix, s_g, RG)

        @block.tensor
        def _(pe):
            pe.wait_ge(s_rel, 6)

            def group(j, u):
                g, h = UN * j + u, u % 2
                pe.wait_ge(s_oh, 2 * g + 2)
                wait(pe, s_pr, g - 1)
                at = load_values(nc, mybir.EngineType.PE, T["qRow"][0:1, bass.ds(g * G, G)], (NT - 1) * 3 * C)
                for k in range(G):
                    for n in range(3):
                        pe.matmul(T["ps_qe"][:, h, k, :], T["PT"][:, h, k * P:(k + 1) * P], T["Q3"][:, bass.ds(at[k] + n * C, C)],
                                  start=(n == 0), stop=(n == 2))
                    for n in range(3):
                        m = pe.matmul(T["ps_u"][:, h, k, :], T["OT"][:, h, k * P:(k + 1) * P], T["rel3"][:, n, :],
                                      start=(n == 0), stop=(n == 2))
                m.then_inc(s_q, 1)
            each_group(pe, group)

        @block.vector
        def _(v):
            v.wait_ge(s_ld, 16)
            q = Seq(v, s_rel)
            q(v.tensor_scalar(T["rel"][:, :], T["rel"][:, :], 0.2, None, ALU.mult))
            q(v.tensor_copy(T["rel3"][:, 0, :], T["rel"][:, :]))
            q(v.tensor_tensor(T["rel"][:, :], T["rel"][:, :], T["rel3"][:, 0, :], ALU.subtract))
            q(v.tensor_copy(T["rel3"][:, 1, :], T["rel"][:, :]))
            q(v.tensor_tensor(T["rel"][:, :], T["rel"][:, :], T["rel3"][:, 1, :], ALU.subtract))
            q(v.tensor_copy(T["rel3"][:, 2, :], T["rel"][:, :]))

            def onehots(j, u):
                g, h = UN * j + u, u % 2
                v.wait_ge(s_bc[h], 32 * (j * (UN // 2) + u // 2 + 1))
                wait(v, s_q, g - 1)
                v.tensor_scalar(T["PT"][:, h, :], T["dlb"][:, h, :], T["iota_p"][:, 0:1], None, ALU.is_equal).then_inc(s_oh, 1)
                v.tensor_scalar(T["OT"][:, h, :], T["tyb"][:, h, :], T["iota_p"][0:NREL, 0:1], None, ALU.is_equal).then_inc(s_oh, 1)

            def modify(j, u):
                g, h = UN * j + u, u % 2
                v.wait_ge(s_g[u % RG], landed(RG, j, u))
                v.wait_ge(s_q, g + 1)
                wait(v, s_done, g - 1)
                KG = T["KG"][:, (u % RG) * G * C:(u % RG + 1) * G * C]
                v.tensor_tensor(T["KU"][:, h, :].rearrange("p (s h d) -> p s h d", s=G, h=H), KG.rearrange("p (s h d) -> p s h d", s=G, h=H),
                                T["ps_u"][:, h, :, :].unsqueeze(2).broadcast_to([P, G, H, D]), ALU.add).then_inc(s_ku, 1)

            def multiply(j, u):
                g, h = UN * j + u, u % 2
                v.wait_ge(s_ku, g + 1)
                v.tensor_tensor(T["KU"][:, h, :], T["KU"][:, h, :], T["ps_qe"][:, h, :, :].rearrange("p s c -> p (s c)"), ALU.mult).then_inc(s_pr, 1)

            def reduce(j, u):
                g, h = UN * j + u, u % 2
                v.wait_ge(s_pr, g + 1)
                v.tensor_reduce(T["S"][:, bass.ds(g * G * H, G * H)], T["KU"][:, h, :].rearrange("p (x d) -> p x d", d=D), AX.X, ALU.add).then_inc(s_done, 1)

            def ahead(j, u):
                return (j, u - 1) if u else (j - 1, UN - 1)

            onehots(0, 0)
            onehots(0, 1)
            modify(0, 0)
            for u in range(2, UN):
                multiply(0, u - 2)
                onehots(0, u)
                modify(0, u - 1)
                reduce(0, u - 2)
            with v.Fori(1, NG // UN, 1) as j:
                for u in range(UN):
                    one = ahead(j, u)
                    two = ahead(*one)
                    multiply(*two)
                    onehots(j, u)
                    modify(*one)
                    reduce(*two)
            last = NG // UN - 1
            multiply(last, UN - 2)
            modify(last, UN - 1)
            reduce(last, UN - 2)
            multiply(last, UN - 1)
            reduce(last, UN - 1)
def phase_softmax_weights(nc, sem, T, d, s_ix, s_g):
    s_v, s_pe, s_in, s_lr, s_e, s_c, s_x, s_ev = (sem("sm_" + n) for n in
        ("vector", "rows", "ready", "ends", "ends_turned", "carry", "exp", "evac"))
    s_zero = sem("sm_sums_cleared")
    R, B = SP_, SC * H
    ST, SX, F, penL, LR, E4, CR = (T[n] for n in ("ST", "SX", "F", "penL", "LR", "E4", "CR"))
    S4 = T["S"][:, :].rearrange("p (c s h) -> p c h s", c=SC, h=H)

    def flat(t):
        return t[0:R, :, :].rearrange("p b e -> p (b e)")

    def by_head(pen):
        return pen[0:R, :, :].unsqueeze(2).broadcast_to([R, SC, H, P])

    with nc.Block() as block:
        @block.tensor
        def _(pe):
            for c in range(SC):
                for h in range(H):
                    m = pe.transpose(T["ps_s"][0:R, c, h * P:(h + 1) * P], S4[:, c, h, :], T["ident"][:, :])
            m.then_inc(s_pe, 1)
            for w in range(2):
                pe.wait_ge(s_lr, w + 1)
                for x in range(2):
                    for c in range(SC):
                        m = pe.transpose(T["ps_e"][0:H, x, c * SP_:(c + 1) * SP_], LR[0:R, x, c * H:(c + 1) * H], T["ident"][0:R, 0:R])
                m.then_inc(s_e, 1)
                pe.wait_ge(s_c, w + 1)
                for c in range(SC):
                    m = pe.transpose(T["ps_c2"][0:R, c * H:(c + 1) * H], CR[0:H, c * SP_:(c + 1) * SP_], T["ident"][0:H, 0:H])
                m.then_inc(s_pe, 1)
            pe.wait_ge(s_x, 1)
            for c in range(SC):
                for h in range(H):
                    m = pe.transpose(T["ps_s"][:, c, h * P:h * P + R], ST[0:R, c * H + h, :], T["ident"][0:R, 0:R])
            m.then_inc(s_pe, 1)

        @block.gpsimd
        def _(pool):
            for u in range(RV):
                gather_group(pool, d["vtab"], T["ixv"], T["VG"], s_ix, s_g, RV, 0, u)
            pool.memset(T["ACC"][:, :], 0.0).then_inc(s_zero, 1)

        @block.scalar
        def _(a):
            for u in range(RV):
                feed_group(a, T, T["ixv"], s_ix, None, RV, u, u)
            a.wait_ge(s_in, 1)
            a.activation(ST[0:R, :, :], ST[0:R, :, :], ACT.Exp).then_inc(s_x, 1)

        @block.vector
        def _(v):
            q = Seq(v, s_v)
            v.wait_ge(s_pe, 1)
            q(v.tensor_tensor(ST[0:R, :, :].rearrange("p (c h) e -> p c h e", h=H), T["ps_s"][0:R, :, :].rearrange("p c (h e) -> p c h e", h=H),
                              by_head(T["valid"]), ALU.add))
            q(v.tensor_copy(flat(SX), flat(ST)))

            def direction(w, src, out, pen, edge, end, order):
                q(v.tensor_copy(penL[0:R, :, :].rearrange("p (c h) e -> p c h e", h=H), by_head(pen)))
                q(v.memset(penL[0:R, :, edge:edge + 1], -BIG))
                q(v.tensor_tensor_scan(order(out), order(penL), order(src), -BIG, ALU.add, ALU.max))
                q(v.tensor_copy(LR[0:R, 0, :], out[0:R, :, end]))
                q(v.tensor_reduce(T["rp"][0:R, :], pen[0:R, :, :], AX.X, ALU.min))
                v.tensor_copy(LR[0:R, 1, :].rearrange("p (c h) -> p c h", h=H),
                              T["rp"][0:R, :].unsqueeze(2).broadcast_to([R, SC, H])).then_inc(s_lr, 1)
                v.wait_ge(s_e, w + 1)
                q(v.tensor_copy(T["E2"][0:H, :, :], T["ps_e"][0:H, :, 0:NS]))
                if w == 0:
                    q(v.tensor_tensor_scan(E4[0:H, :], T["E2"][0:H, 1, :], T["E2"][0:H, 0, :], -BIG, ALU.add, ALU.max))
                    q(v.memset(CR[0:H, 0:1], -BIG))
                    v.tensor_copy(CR[0:H, 1:NS], E4[0:H, 0:NS - 1]).then_inc(s_c, 1)
                else:
                    q(v.tensor_tensor_scan(E4[0:H, ::-1], T["E2"][0:H, 1, ::-1], T["E2"][0:H, 0, ::-1], -BIG, ALU.add, ALU.max))
                    q(v.memset(CR[0:H, NS - 1:NS], -BIG))
                    v.tensor_copy(CR[0:H, 0:NS - 1], E4[0:H, 1:NS]).then_inc(s_c, 1)
                v.wait_ge(s_pe, w + 2)
                q(v.tensor_tensor(T["inj"][0:R, :].rearrange("p (c h) -> p c h", h=H), T["ps_c2"][0:R, :].rearrange("p (c h) -> p c h", h=H),
                                  pen[0:R, :, edge:edge + 1].broadcast_to([R, SC, H]), ALU.add))
                q(v.tensor_tensor(src[0:R, :, edge], src[0:R, :, edge], T["inj"][0:R, :], ALU.max))
                q(v.tensor_tensor_scan(order(out), order(penL), order(src), -BIG, ALU.add, ALU.max))

            direction(0, SX, F, T["penf"], 0, P - 1, flat)
            direction(1, F, SX, T["penb"], P - 1, 0, lambda t: flat(t)[:, ::-1])
            v.tensor_tensor(flat(ST), flat(ST), flat(SX), ALU.subtract).then_inc(s_in, 1)
            v.wait_ge(s_pe, 4)
            for c in range(SC):
                q(v.tensor_copy(S4[:, c, :, :], T["ps_s"][:, c, :].rearrange("p (h s) -> p h s", h=H)[:, :, 0:R]))


def phase_aggregate(nc, sem, T, d, s_ix, s_g):
    s_oh, s_w, s_wc, s_o, s_acc = (sem("ag_" + n) for n in ("onehots", "weighted", "weights", "products", "added"))
    A = C + H
    WV = T["WV"]
    with nc.Block() as block:
        @block.scalar
        def _(a):
            def group(j, u, more=True):
                g, h = UN * j + u, u % 2
                wait(a, s_o, (g - 1) * G)
                a.copy(WV[:, h, :, C:A], T["S"][:, bass.ds(g * G * H, G * H)].rearrange("p (k h) -> p k h", h=H)).then_inc(s_wc, 1)
                if more:
                    feed_group(a, T, T["ixv"], s_ix, s_w, RV, g + RV, u)
            for u in range(UN):
                group(0, u)
            with a.Fori(1, NG // UN - 1, 1) as j:
                for u in range(UN):
                    group(j, u)
            for u in range(UN):
                group(NG // UN - 1, u, more=False)

        @block.gpsimd
        def _(pool):
            gather_rows(pool, d["vtab"], T["ixv"], T["VG"], s_ix, s_g, RV, RV)

        @block.tensor
        def _(pe):
            def group(j, u):
                g, h = UN * j + u, u % 2
                pe.wait_ge(s_oh, (g + 1) * G)
                pe.wait_ge(s_w, g + 1)
                pe.wait_ge(s_wc, g + 1)
                wait(pe, s_acc, (g - 1) * G)
                for k in range(G):
                    pe.matmul(T["ps_o"][:, h * G + k, 0:A], T["PM"][:, h, k, :], WV[:, h, k, :], start=True, stop=True).then_inc(s_o, 1)
            each_group(pe, group)

        @block.vector
        def _(v):
            def blocks(j, u):
                return load_values(nc, mybir.EngineType.DVE, T["aRow"][0:1, bass.ds((UN * j + u) * G, G)], (NT - 1) * A)

            def add(j, u, k, at):
                g, h = UN * j + u, u % 2
                v.wait_ge(s_o, g * G + k + 1)
                if k or u or not isinstance(j, int):
                    v.wait_ge(s_acc, g * G + k)
                acc = T["ACC"][:, bass.ds(at, A)]
                v.tensor_tensor(acc, acc, T["ps_o"][:, h * G + k, 0:A], ALU.add).then_inc(s_acc, 1)

            def weigh(j, u, before=None):
                g, h = UN * j + u, u % 2
                wait(v, s_o, (g - 1) * G)
                at = blocks(*before) if before else None
                for k in range(G):
                    v.tensor_scalar(T["PM"][:, h, k, :], T["iota_f"][:, :], T["DC"][:, bass.ds(g * G + k, 1)], None, ALU.is_equal).then_inc(s_oh, 1)
                    if before:
                        add(*before, k, at[k])
                v.wait_ge(s_g[u % RV], landed(RV, j, u))
                v.tensor_tensor(WV[:, h, :, 0:C].rearrange("p k (x d) -> p k x d", d=D),
                                T["VG"][:, (u % RV) * G * C:(u % RV + 1) * G * C].rearrange("p (k x d) -> p k x d", d=D, x=H),
                                T["S"][:, bass.ds(g * G * H, G * H)].rearrange("p (k x) -> p k x", x=H).unsqueeze(3).broadcast_to([P, G, H, D]), ALU.mult).then_inc(s_w, 1)

            weigh(0, 0)
            weigh(0, 1)
            for u in range(2, UN):
                weigh(0, u, (0, u - 2))
            with v.Fori(1, NG // UN, 1) as j:
                weigh(j, 0, (j - 1, UN - 2))
                weigh(j, 1, (j - 1, UN - 1))
                for u in range(2, UN):
                    weigh(j, u, (j, u - 2))
            for u in (UN - 2, UN - 1):
                at = blocks(NG // UN - 1, u)
                for k in range(G):
                    add(NG // UN - 1, u, k, at[k])
def phase_combine(nc, sem, T, d):
    s_ld, s_vt, s_i, s_v, s_c, s_pe, s_ct, s_m, s_a, s_t, s_tc, s_y, s_q, s_sq, s_xf, s_nd, s_ra, s_gl, s_ms, s_xn, s_pb, s_yn, s_yg, s_xt, s_rs = (sem("cb_" + n) for n in
        ("loads", "v_rows", "iota", "vector", "context", "context_turned", "context_copied", "mix_matrix", "scalar",
         "turned", "turned_copied", "rows", "mixed", "variance", "normed", "denominators", "reciprocals", "logits",
         "messages", "first_normed", "biases_added", "second_normed", "scaled", "rows_stored", "divisors_spread"))
    A = C + H
    CT_ = 5
    NC_ = NT // CT_
    X, rstd, nmr, QT, ACC, Y, VB = (T[n] for n in ("X", "rstd", "nmr", "QT", "ACC", "Y", "VB"))
    ps_t2, ps_y, mT = T["ps_t2"], T["ps_y"], T["mT"]
    MH = C // MD
    CH = [(a, n0, min(512, NT * P - n0)) for n0 in range(0, NT * P, 512) for a in range(2)]
    acc3 = ACC[:, :].rearrange("p (t a) -> p t a", a=A)

    def chunk(t, c):
        return t[:, c * CT_:(c + 1) * CT_, :]

    def over_chunk(row):
        return row.unsqueeze(1).broadcast_to([P, CT_, C])

    with nc.Block() as block:
        @block.sync
        def _(sp):
            sp.dma_start(T["WP"][:, :, :], d["m_WprojT"].rearrange("(k p) n -> p k n", p=P)).then_inc(s_ld, 16)
            for c in range(NC_):
                sp.dma_start(chunk(VB, c), d["vtab"][c * CT_ * P:(c + 1) * CT_ * P, :].rearrange("(t p) c -> p t c", p=P)).then_inc(s_vt, 16)
            for n in ("gamma", "beta"):
                sp.dma_start(T[n][:, :], d["g_" + n].rearrange("(a n) -> a n", a=1).broadcast_to([P, C])).then_inc(s_ld, 16)
            for j, n in enumerate(("g_bo", "m_bproj")):
                sp.dma_start(T["bias2"][:, j, :], d[n].rearrange("(a n) -> a n", a=1).broadcast_to([P, C])).then_inc(s_ld, 16)
            sp.dma_start(T["Wo"][:, :, :], d["g_Wo"].rearrange("(k p) n -> p k n", p=P)).then_inc(s_ld, 16)
            sp.dma_start(T["GW"][:, :, :], d["f_gate_w"].rearrange("(k p) n -> p k n", p=P)).then_inc(s_ld, 16)
            sp.dma_start(T["gb"][:, :], d["f_gate_b"].rearrange("(a n) -> a n", a=1).broadcast_to([P, NEXP])).then_inc(s_ld, 16)
            for c in range(NC_):
                sp.wait_ge(s_xf, (c + 1) * CT_)
                sp.dma_start(d["xtab"][c * CT_ * P:(c + 1) * CT_ * P, :].rearrange("(t p) c -> p t c", p=P), chunk(Y, c)).then_inc(s_xt, 16)
            sp.wait_ge(s_xt, 16 * NC_)

        @block.gpsimd
        def _(pool):
            pool.iota(T["bd_o"][:, :], [[0, P]], base=0, channel_multiplier=1).then_inc(s_i, 1)
            pool.iota(T["rank_i"][:, :], [[-1, NEXP]], base=NEXP, channel_multiplier=0).then_inc(s_i, 1)
            pool.iota(T["bd_e"][:, :], [[1, P]], base=0, channel_multiplier=0).then_inc(s_i, 1)
            pool.wait_ge(s_ld, 16 * 8)
            pool.tensor_tensor(T["bias2"][:, 1, :], T["bias2"][:, 1, :], T["beta"][:, :], ALU.add).then_inc(s_i, 1)
            pool.wait_ge(s_i, 4)
            for c in range(NC_):
                pool.wait_ge(s_xn, (c + 1) * CT_)
                pool.tensor_tensor(chunk(Y, c), chunk(Y, c), over_chunk(T["bias2"][:, 0, :]), ALU.add).then_inc(s_pb, 1)
                pool.tensor_tensor(chunk(X, c), chunk(X, c), over_chunk(T["bias2"][:, 1, :]), ALU.add).then_inc(s_pb, 1)
            for c in range(NC_):
                pool.wait_ge(s_yn, (c + 1) * CT_)
                pool.tensor_tensor(chunk(Y, c), chunk(Y, c), over_chunk(T["gamma"][:, :]), ALU.mult).then_inc(s_yg, 1)

        @block.vector
        def _(v):
            q = Seq(v, s_v)
            v.wait_ge(s_i, 3)
            q(v.tensor_copy(T["rank"][:, :], T["rank_i"][:, :]))
            q(v.tensor_scalar(T["bd_o"][:, :], T["bd_o"][:, :], 5, None, ALU.logical_shift_right))
            q(v.tensor_scalar(T["bd_e"][:, :], T["bd_e"][:, :], 5, None, ALU.logical_shift_right))
            q(v.tensor_tensor(T["BD"][:, :], T["bd_o"][:, :], T["bd_e"][:, :], ALU.is_equal))
            for a in range(2):
                q(v.tensor_scalar(T["KS"][:, a, :], T["BD"][:, ::MD], T["CTX"][:, a, P:P + 1], None, ALU.mult))
                v.tensor_tensor(T["CB"][:, a, :], T["CTX"][:, a, 0:P], T["BD"][:, :], ALU.mult).then_inc(s_c, 1)
            v.wait_ge(s_pe, 1)
            v.tensor_copy(T["CT"][:, :, :], T["ps_s2"][:, 0:2 * P].rearrange("p (a c) -> p a c", a=2)).then_inc(s_ct, 1)
            iz, dn = T["iz"], T["dn"]
            q(v.tensor_scalar(iz[:, :, :], acc3[:, :, C:A], 0.0, None, ALU.is_equal))
            q(v.tensor_tensor(dn[:, :, :], acc3[:, :, C:A], iz[:, :, :], ALU.add))
            q(v.reciprocal(dn[:, :, :], dn[:, :, :]))
            rd = T["rd"]
            v.wait_ge(s_nd, 1)
            q(v.tensor_scalar(rd[:, :], T["ps_d"][:, 1, 0:NT * MH], 1e-6, None, ALU.max))
            v.reciprocal(rd[:, :], rd[:, :]).then_inc(s_ra, 1)

            def messages(c):
                def by_head(t):
                    return t.rearrange("p t (h d) -> p t h d", h=H)

                def spread(t):
                    return chunk(t, c).unsqueeze(3).broadcast_to([P, CT_, H, D])
                vb, m = chunk(VB, c), acc3[:, c * CT_:(c + 1) * CT_, 0:C]
                v.wait_ge(s_vt, 16 * NC_)
                q(v.tensor_tensor(by_head(vb), by_head(vb), spread(iz), ALU.mult))
                q(v.tensor_tensor(m, m, vb, ALU.add))
                v.tensor_tensor(by_head(m), by_head(m), spread(dn), ALU.mult).then_inc(s_ms, 1)

            def head(i):
                v.wait_ge(s_y, i + 1)
                v.wait_ge(s_pb, 2 * (i // CT_) + 2)
                v.tensor_tensor(Y[:, i, :], Y[:, i, :], ps_y[:, i % 3, 0:C], ALU.add).then_inc(s_v, 1)
                v.tensor_tensor(X[:, i, :], X[:, i, :], ps_y[:, i % 3, C:2 * C], ALU.add).then_inc(s_q, 1)
                q.n += 1
                v.wait_ge(s_v, q.n)
                v.bn_stats(T["stats2"][:, i, :], Y[:, i, :]).then_inc(s_v, 1)
                q.n += 1

            messages(0)
            messages(1)
            for j, (a, n0, w) in enumerate(CH):
                v.wait_ge(s_nd, j + 2)
                v.tensor_tensor(QT[:, a, n0:n0 + w], QT[:, a, n0:n0 + w], T["ps_d"][:, j % 2, 0:w], ALU.mult).then_inc(s_ra, 1)
            v.wait_ge(s_pe, 2)
            v.tensor_copy(T["M"][:, :, :], T["ps_s2"][:, :].rearrange("p (a c) -> p a c", a=2)).then_inc(s_m, 1)
            for i in range(NT):
                if i % CT_ == 0 and i // CT_ + 2 < NC_:
                    messages(i // CT_ + 2)
                head(i)

            def inverse_deviation(k):
                v.wait_ge(s_v, q.n)
                for t in range(NT):
                    v.bn_aggr(T["mv2"][:, t, :], T["stats2"][:, t, :]).then_inc(s_v, 1)
                q.n += NT
                v.wait_ge(s_v, q.n)
                v.tensor_scalar(rstd[:, :], T["mv2"][:, :, 1], EPS, None, ALU.add).then_inc(s_sq, 1)
                v.wait_ge(s_a, k)
                q(v.reciprocal(rstd[:, :], rstd[:, :]))
                q(v.tensor_tensor(nmr[:, :], T["mv2"][:, :, 0], rstd[:, :], ALU.mult))
                v.tensor_scalar(nmr[:, :], nmr[:, :], -1.0, None, ALU.mult).then_inc(s_sq, 1)
            inverse_deviation(1)
            v.wait_ge(s_q, NT)
            for c in range(NC_):
                v.wait_ge(s_yg, c + 1)
                q(v.tensor_tensor(chunk(X, c), chunk(X, c), chunk(Y, c), ALU.add))
                for t in range(c * CT_, (c + 1) * CT_):
                    v.bn_stats(T["stats2"][:, t, :], X[:, t, :]).then_inc(s_v, 1)
                q.n += CT_
            inverse_deviation(2)
            v.wait_ge(s_sq, 4)
            for i in range(NT):
                v.tensor_scalar(Y[:, i, :], X[:, i, :], rstd[:, i:i + 1], nmr[:, i:i + 1], ALU.mult, ALU.add).then_inc(s_xf, 1)
            v.wait_ge(s_gl, NT)
            LG, mx, eq = T["LG"], T["mx"], T["eq"]
            b3 = lambda t: t[:, :].unsqueeze(2).broadcast_to([P, NT, NEXP])
            q(v.tensor_tensor(LG[:, :, :], T["ps_s2"][:, 0:NT * NEXP].rearrange("p (t e) -> p t e", e=NEXP),
                              T["gb"][:, :].unsqueeze(1).broadcast_to([P, NT, NEXP]), ALU.add))
            q(v.tensor_reduce(mx[:, :], LG[:, :, :], AX.X, ALU.max))
            v.tensor_tensor(LG[:, :, :], LG[:, :, :], b3(mx), ALU.subtract).then_inc(s_sq, 1)
            v.wait_ge(s_a, 3)
            q(v.tensor_reduce(mx[:, :], LG[:, :, :], AX.X, ALU.add))
            q(v.reciprocal(mx[:, :], mx[:, :]))
            q(v.tensor_tensor(LG[:, :, :], LG[:, :, :], b3(mx), ALU.mult))
            for r in range(2):
                top, sel = T["PV"][:, r, :], T["SEL"][:, r, :, :]
                q(v.tensor_reduce(top, LG[:, :, :], AX.X, ALU.max))
                q(v.tensor_tensor(eq[:, :, :], LG[:, :, :], top.unsqueeze(2).broadcast_to([P, NT, NEXP]), ALU.is_equal))
                q(v.tensor_tensor(eq[:, :, :], eq[:, :, :], T["rank"][:, :].unsqueeze(1).broadcast_to([P, NT, NEXP]), ALU.mult))
                q(v.tensor_reduce(mx[:, :], eq[:, :, :], AX.X, ALU.max))
                q(v.tensor_tensor(sel, T["rank"][:, :].unsqueeze(1).broadcast_to([P, NT, NEXP]), b3(mx), ALU.is_equal))
                q(v.tensor_scalar(eq[:, :, :], sel, -2.0, None, ALU.mult))
                q(v.tensor_tensor(LG[:, :, :], LG[:, :, :], eq[:, :, :], ALU.add))

        @block.scalar
        def _(a):
            for i in range(NT):
                a.activation(Y[:, i, :], X[:, i, :], ACT.Identity, scale=rstd[:, i:i + 1], bias=nmr[:, i:i + 1]).then_inc(s_xn, 1)
            a.wait_ge(s_ra, 1)
            for t in range(0, NT, 4):
                n = min(4, NT - t)
                a.copy(T["RS"][:, t:t + n, :].rearrange("p t (h d) -> p (t h) d", d=MD),
                       T["rd"][:, t * MH:(t + n) * MH].unsqueeze(2).broadcast_to([P, n * MH, MD])).then_inc(s_rs, 1)
            for i in range(NT):
                a.wait_ge(s_t, i + 1)
                wait(a, s_y, i - 1)
                a.copy(mT[:, i % 2, :, :], ps_t2[:, i % 2, 0:C].rearrange("p (k n) -> p k n", k=2)).then_inc(s_tc, 1)
            a.wait_ge(s_sq, 1)
            a.activation(rstd[:, :], rstd[:, :], ACT.Sqrt).then_inc(s_a, 1)
            a.wait_ge(s_sq, 2)
            for i in range(NT):
                a.activation(Y[:, i, :], Y[:, i, :], ACT.Identity, scale=rstd[:, i:i + 1], bias=nmr[:, i:i + 1]).then_inc(s_yn, 1)
            a.wait_ge(s_sq, 3)
            a.activation(rstd[:, :], rstd[:, :], ACT.Sqrt).then_inc(s_a, 1)
            for i in range(NT):
                a.wait_ge(s_t, NT + i + 1)
                wait(a, s_gl, i - 1)
                a.copy(mT[:, i % 2, :, :], ps_t2[:, i % 2, 0:C].rearrange("p (k n) -> p k n", k=2)).then_inc(s_tc, 1)
            a.wait_ge(s_sq, 5)
            a.activation(T["LG"][:, :, :], T["LG"][:, :, :], ACT.Exp).then_inc(s_a, 1)

        @block.tensor
        def _(pe):
            pe.wait_ge(s_c, 2)
            for a in range(2):
                m = pe.transpose(T["ps_s2"][:, a * P:(a + 1) * P], T["CB"][:, a, :], T["ident"][:, :])
            m.then_inc(s_pe, 1)
            for i in range(NT):
                for a in range(2):
                    m = pe.matmul(T["ps_d"][:, 1, i * MH + a * MH // 2:i * MH + (a + 1) * MH // 2], QT[:, a, i * P:(i + 1) * P], T["KS"][:, a, :],
                                  start=True, stop=True)
            m.then_inc(s_nd, 1)
            for j, (a, n0, w) in enumerate(CH):
                pe.wait_ge(s_rs, j // 2 + 1)
                pe.wait_ge(s_ra, max(j, 1))
                for t in range(w // P):
                    m = pe.transpose(T["ps_d"][:, j % 2, t * P:(t + 1) * P], T["RS"][:, n0 // P + t, a * P:(a + 1) * P], T["ident"][:, :])
                m.then_inc(s_nd, 1)
            pe.wait_ge(s_ld, 16 * 8)
            pe.wait_ge(s_ct, 1)
            for a in range(2):
                m = pe.matmul(T["ps_s2"][:, a * C:(a + 1) * C], T["CT"][:, a, :], T["WP"][:, a, :], start=True, stop=True)
            m.then_inc(s_pe, 1)
            pe.wait_ge(s_m, 1)
            pe.wait_ge(s_ra, 1 + len(CH))

            def turn(n, rows):
                for k in range(2):
                    m = pe.transpose(ps_t2[:, n % 2, k * P:(k + 1) * P], rows[:, k * P:(k + 1) * P], T["ident"][:, :])
                m.then_inc(s_t, 1)

            def turn_messages(i):
                pe.wait_ge(s_ms, i // CT_ + 1)
                wait(pe, s_tc, i - 1)
                turn(i, acc3[:, i, 0:C])

            turn_messages(0)
            for i in range(NT):
                if i + 1 < NT:
                    turn_messages(i + 1)
                pe.wait_ge(s_tc, i + 1)
                wait(pe, s_q, i - 2)
                for k in range(2):
                    pe.matmul(ps_y[:, i % 3, 0:C], mT[:, i % 2, k, :], T["Wo"][:, k, :], start=(k == 0), stop=(k == 1))
                for k in range(2):
                    m = pe.matmul(ps_y[:, i % 3, C:2 * C], QT[:, k, i * P:(i + 1) * P], T["M"][:, k, :], start=(k == 0), stop=(k == 1))
                m.then_inc(s_y, 1)

            def turn_normed(i):
                pe.wait_ge(s_xf, i + 1)
                pe.wait_ge(s_tc, NT + i - 1)
                turn(i, Y[:, i, :])

            turn_normed(0)
            for i in range(NT):
                if i + 1 < NT:
                    turn_normed(i + 1)
                pe.wait_ge(s_tc, NT + i + 1)
                for k in range(2):
                    m = pe.matmul(T["ps_s2"][:, i * NEXP:(i + 1) * NEXP], mT[:, i % 2, k, :], T["GW"][:, k, :],
                                  start=(k == 0), stop=(k == 1))
                m.then_inc(s_gl, 1)
def phase_route(nc, sem, T, d):
    s_ld, s_i, s_v, s_m, s_pe, s_oh, s_mm, s_inv, s_hi, s_ohh = (sem("rt_" + n) for n in
        ("loads", "iota", "vector", "chosen", "counts", "onehots", "placed", "slots", "rows_of_slots", "row_onehots"))
    s_w = sem("rt_weights")
    SEL, M, TE, INC, posf = (T[n] for n in ("SEL", "Msel", "TE", "INC", "posf"))
    NA = 2 * NT
    NB = NSLOT // P
    ps_m, ps_inv = T["ps_m"], T["ps_inv"]
    with nc.Block() as block:
        @block.sync
        def _(sp):
            for e in range(NEXP):
                w1 = T["W1"][:, e * W1C:(e + 1) * W1C]
                sp.dma_start(w1[:, 0:2 * HID].rearrange("p (k n) -> p k n", k=2), d["f_W1"][e].rearrange("(k p) n -> p k n", p=P)).then_inc(s_w, 16)
                sp.dma_start(w1[:, 2 * HID:W1C], d["f_b1"][e].rearrange("(k p) -> p k", p=P), allow_slow_non_contiguous=True).then_inc(s_w, 16)
                sp.dma_start(T["W2"][:, e * HC * C:(e + 1) * HC * C].rearrange("p (k n) -> p k n", k=HC),
                             d["f_W2"][e].rearrange("(k p) n -> p k n", p=P)).then_inc(s_w, 16)
                sp.dma_start(T["B2"][:, e * C:(e + 1) * C], d["f_b2"][e:e + 1, :].broadcast_to([P, C])).then_inc(s_w, 16)
            sp.wait_ge(s_w, 64 * NEXP)

        @block.gpsimd
        def _(pool):
            pool.iota(T["as_i"][:, :], [[P, NA]], base=1, channel_multiplier=1).then_inc(s_i, 1)
            pool.iota(T["sl_i"][:, :], [[P, NB]], base=0, channel_multiplier=1).then_inc(s_i, 1)
            pool.iota(T["tl_i"][:, :], [[1, NTILE]], base=0, channel_multiplier=0).then_inc(s_i, 1)
            pool.wait_ge(s_hi, 1)
            for a in range(NA):
                wait(pool, s_mm, a - 3)
                pool.tensor_scalar(T["OHh"][:, a % 4, :], T["iota_f"][:, 0:NB], T["hi_f"][:, a:a + 1], None, ALU.is_equal).then_inc(s_ohh, 1)

        @block.vector
        def _(v):
            q = Seq(v, s_v)
            v.wait_ge(s_i, 3)
            q(v.tensor_copy(T["asg"][:, :], T["as_i"][:, :]))
            q(v.tensor_copy(T["slot"][:, :], T["sl_i"][:, :]))
            q(v.tensor_copy(T["tl"][:, :], T["tl_i"][:, :]))
            q(v.tensor_scalar(T["LT"][:, :], T["iota_f"][:, :], T["iota_p"][:, 0:1], None, ALU.is_gt))
            q(v.tensor_scalar(T["real"][:, :], T["asg"][:, 0:NT], float(N), None, ALU.is_le))
            q(v.tensor_tensor(M[:, :, :], SEL[:, 0, :, :], SEL[:, 1, :, :], ALU.add))
            v.tensor_tensor(M[:, :, :], M[:, :, :], T["real"][:, :].unsqueeze(2).broadcast_to([P, NT, NEXP]), ALU.mult).then_inc(s_m, 1)
            q(v.memset(T["keep"][:, :, :], 1.0))
            q(v.memset(T["keep"][:, :, 0:1], 0.0))
            v.wait_ge(s_pe, 1)
            q(v.tensor_copy(TE[:, :, :], ps_m[:, 1, 0:NT * NEXP].rearrange("p (t e) -> p e t", e=NEXP)))
            q(v.tensor_tensor_scan(INC[:, :, :].rearrange("p e t -> p (e t)"), T["keep"][:, :, :].rearrange("p e t -> p (e t)"),
                                   TE[:, :, :].rearrange("p e t -> p (e t)"), 0.0, ALU.mult, ALU.add))
            q(v.tensor_scalar(T["cnt_e"][:, :], INC[:, :, NT - 1], float(SLOTS - 1), None, ALU.add))
            q(v.tensor_copy(T["cnt_i"][:, :], T["cnt_e"][:, :]))
            q(v.tensor_scalar(T["cnt_i"][:, :], T["cnt_i"][:, :], SLOTS.bit_length() - 1, None, ALU.logical_shift_right))
            q(v.tensor_copy(T["cnt_e"][:, :], T["cnt_i"][:, :]))
            q(v.tensor_tensor_scan(T["base"][:, :], T["onesr"][:, 0:NEXP], T["cnt_e"][:, :], 0.0, ALU.mult, ALU.add))
            q(v.tensor_tensor(T["base"][:, :], T["base"][:, :], T["cnt_e"][:, :], ALU.subtract))
            q(v.tensor_tensor(T["ge"][:, :, :], T["tl"][:, :].unsqueeze(2).broadcast_to([P, NTILE, NEXP]),
                              T["base"][:, :].unsqueeze(1).broadcast_to([P, NTILE, NEXP]), ALU.is_ge))
            q(v.tensor_reduce(T["ex_t"][:, :], T["ge"][:, :, :], AX.X, ALU.add))
            for n, width in enumerate((W1C, HC * C, C)):
                q(v.tensor_scalar(T["tl"][:, :], T["ex_t"][:, :], -1.0, float(width), ALU.add, ALU.mult))
                q(v.tensor_copy(T["off"][:, n, :], T["tl"][:, :]))
            q(v.tensor_scalar(T["base"][:, :], T["base"][:, :], float(SLOTS), None, ALU.mult))
            q(v.tensor_tensor(INC[:, :, :], INC[:, :, :], TE[:, :, :], ALU.subtract))
            q(v.tensor_tensor(INC[:, :, :], INC[:, :, :], T["base"][:, :].unsqueeze(2).broadcast_to([P, NEXP, NT]), ALU.add))
            q(v.tensor_tensor(M[:, :, :], ps_m[:, 0, 0:NT * NEXP].rearrange("p (t e) -> p t e", e=NEXP),
                              INC[:, :, :].rearrange("p e t -> p t e"), ALU.add))
            q(v.tensor_scalar(T["real"][:, :], T["real"][:, :], -1.0, -float(NSLOT), ALU.add, ALU.mult))
            for r in range(2):
                q(v.tensor_tensor(SEL[:, r, :, :], SEL[:, r, :, :], M[:, :, :], ALU.mult))
                q(v.tensor_reduce(posf[:, r * NT:(r + 1) * NT], SEL[:, r, :, :], AX.X, ALU.add))
                q(v.tensor_tensor(posf[:, r * NT:(r + 1) * NT], posf[:, r * NT:(r + 1) * NT], T["real"][:, :], ALU.add))
            q(v.tensor_copy(T["pos_i"][:, :], posf[:, :]))
            q(v.tensor_scalar(T["pos_h"][:, :], T["pos_i"][:, :], P.bit_length() - 1, None, ALU.logical_shift_right))
            q(v.tensor_scalar(T["pos_i"][:, :], T["pos_i"][:, :], P - 1, None, ALU.bitwise_and))
            v.tensor_copy(T["hi_f"][:, :], T["pos_h"][:, :]).then_inc(s_hi, 1)
            q(v.tensor_copy(T["lo_f"][:, :], T["pos_i"][:, :]))
            for a in range(NA):
                wait(v, s_mm, a - 3)
                v.tensor_scalar(T["OHl"][:, a % 4, :], T["iota_f"][:, :], T["lo_f"][:, a:a + 1], T["asg"][:, a:a + 1], ALU.is_equal,
                                ALU.mult).then_inc(s_oh, 1)
            v.wait_ge(s_mm, NA)
            v.tensor_copy(T["inv"][0:NB, :], ps_inv[0:NB, 0:P]).then_inc(s_inv, 1)
            v.wait_ge(s_mm, NA + 1)
            vv, t1 = T["vv"][:, :], T["t1"][:, :]
            q(v.tensor_copy(vv, ps_inv[:, 128:128 + NB]))
            q(v.tensor_scalar(t1, vv, 0.0, None, ALU.is_equal))
            q(v.tensor_scalar(T["slot"][:, :], T["slot"][:, :], float(NA * P + 1), None, ALU.add))
            q(v.tensor_tensor(t1, t1, T["slot"][:, :], ALU.mult))
            q(v.tensor_tensor(t1, t1, vv, ALU.add))
            q(v.tensor_scalar(t1, t1, -1.0, None, ALU.add))
            q(v.tensor_copy(T["DI"][:, :], t1))
            q(v.tensor_scalar(t1, vv, float(NT * P), -float(NT * P), ALU.is_gt, ALU.mult))
            q(v.tensor_tensor(vv, vv, t1, ALU.add))
            q(v.tensor_scalar(vv, vv, -1.0, 0.0, ALU.add, ALU.max))
            q(v.tensor_copy(T["GI"][:, :], vv))

        @block.tensor
        def _(pe):
            pe.wait_ge(s_m, 1)
            flat = M[:, :, :].rearrange("p t e -> p (t e)")
            pe.matmul(ps_m[:, 0, 0:NT * NEXP], T["LT"][:, :], flat, start=True, stop=True)
            pe.matmul(ps_m[:, 1, 0:NT * NEXP], T["onesr"][:, :], flat, start=True, stop=True).then_inc(s_pe, 1)
            for a in range(NA):
                pe.wait_ge(s_oh, a + 1)
                pe.wait_ge(s_ohh, a + 1)
                pe.matmul(ps_inv[0:NB, 0:P], T["OHh"][:, a % 4, :], T["OHl"][:, a % 4, :], start=(a == 0), stop=(a == NA - 1)).then_inc(s_mm, 1)
            pe.wait_ge(s_inv, 1)
            pe.transpose(ps_inv[:, 128:128 + NB], T["inv"][0:NB, :], T["ident"][0:NB, 0:NB]).then_inc(s_mm, 1)


def phase_experts(nc, sem, T, d):
    s_gx = [sem(f"ex_gathered{u}") for u in range(UE)]
    s_sc = [sem(f"ex_scattered{u}") for u in range(UE)]
    s_gi, s_di, s_t, s_xt, s_wc, s_h, s_hg, s_y, s_ye = (sem("ex_" + n) for n in
        ("gather_indices", "scatter_indices", "turned", "turned_copied", "weights_copied", "hidden", "activated", "rows", "rows_copied"))
    NI = NTILE // UE
    YB = 2
    HB = SLOTS // P
    XG, XT, WB, HT, YG = (T[n] for n in ("XG", "XT", "WB", "HT", "YG"))

    def offset(engine, n, g, high):
        return load_values(nc, engine, T["off"][0:1, n, bass.ds(g, 1)], high)[0]

    def each_group_of_tiles(eng, body):
        for u in range(UE):
            body(0, u, True)
        with eng.Fori(1, NI - 1, 1) as j:
            for u in range(UE):
                body(j, u, True)
        for u in range(UE):
            body(NI - 1, u, False)

    with nc.Block() as block:
        @block.gpsimd
        def _(pool):
            def gather(j, u):
                pool.wait_ge(s_gi, UE * j + u + 1)
                pool.nop(nofuse=True)
                for w in range(HB):
                    pool.indirect_dma_start(XG[:, (u * HB + w) * C:(u * HB + w + 1) * C], None, d["xtab"],
                                            bass.IndirectOffsetOnAxis(ap=T["GX"][:, u, w:w + 1], axis=0)).then_inc(s_gx[u], 16)

            def scatter(j, u, more):
                if more:
                    gather(j + 1, u)
                pool.wait_ge(s_di, UE * j + u + 1)
                pool.wait_ge(s_ye, (UE * j + u + 1) * HB)
                pool.nop(nofuse=True)
                for w in range(HB):
                    pool.indirect_dma_start(d["ytab"], bass.IndirectOffsetOnAxis(ap=T["DX"][:, u, w:w + 1], axis=0),
                                            YG[:, (u * HB + w) * C:(u * HB + w + 1) * C], None).then_inc(s_sc[u], 16)
            for u in range(UE):
                gather(0, u)
            each_group_of_tiles(pool, scatter)
            for u in range(UE):
                pool.wait_ge(s_sc[u], 16 * HB * NI)

        @block.scalar
        def _(a):
            def gather_indices(j, u):
                g = UE * j + u
                wait(a, s_t, g - UE + 1)
                a.copy(T["GX"][:, u, :], T["GI"][:, bass.ds(g * HB, HB)]).then_inc(s_gi, 1)

            def weights(j, u):
                g = UE * j + u
                at = offset(mybir.EngineType.Activation, 0, g, (NEXP - 1) * W1C)
                wait(a, s_hg, (g - 1) * HC)
                a.copy(WB[:, u % 2, :], T["W1"][:, bass.ds(at, W1C)]).then_inc(s_wc, 1)

            def activate(j, u):
                g = UE * j + u
                wait(a, s_y, (g - 1) * HB)
                for m in range(HC):
                    a.wait_ge(s_h, g * HC + m + 1)
                    a.activation(HT[:, u % 2, m, :], T["ps_h"][:, m, 0:SLOTS], ACT.Gelu, bias=WB[:, u % 2, 2 * HID + m:2 * HID + m + 1]).then_inc(s_hg, 1)

            def tile(j, u, more):
                g = UE * j + u
                if more:
                    gather_indices(j + 1, u)
                wait(a, s_sc[u], j * 16 * HB)
                a.copy(T["DX"][:, u, :], T["DI"][:, bass.ds(g * HB, HB)]).then_inc(s_di, 1)
                if more or u + 1 < UE:
                    activate(j + (u + 1) // UE, (u + 1) % UE)
                if more or u + 2 < UE:
                    weights(j + (u + 2) // UE, (u + 2) % UE)
            for u in range(UE):
                gather_indices(0, u)
            weights(0, 0)
            weights(0, 1)
            activate(0, 0)
            each_group_of_tiles(a, tile)

        @block.tensor
        def _(pe):
            def turn(j, u):
                g = UE * j + u
                pe.wait_ge(s_gx[u], (j + 1) * 16 * HB)
                wait(pe, s_xt, g - 1)
                for w in range(HB):
                    for k in range(2):
                        c0 = (u * HB + w) * C + k * P
                        m = pe.transpose(T["ps_x"][:, u % 2, k * SLOTS + w * P:k * SLOTS + (w + 1) * P], XG[:, c0:c0 + P], T["ident"][:, :])
                m.then_inc(s_t, 1)

            def hidden(j, u):
                g = UE * j + u
                pe.wait_ge(s_xt, g + 1)
                pe.wait_ge(s_wc, g + 1)
                for m in range(HC):
                    wait(pe, s_hg, (g - 1) * HC + m + 1)
                    for k in range(2):
                        r = pe.matmul(T["ps_h"][:, m, 0:SLOTS], WB[:, u % 2, k * HID + m * P:k * HID + (m + 1) * P], XT[:, u % 2, k, :],
                                      start=(k == 0), stop=(k == 1))
                    r.then_inc(s_h, 1)

            def tile(j, u, more):
                g = UE * j + u
                at = offset(mybir.EngineType.PE, 1, g, (NEXP - 1) * HC * C)
                if more or u + 2 < UE:
                    turn(j + (u + 2) // UE, (u + 2) % UE)
                if more or u + 1 < UE:
                    hidden(j + (u + 1) // UE, (u + 1) % UE)
                pe.wait_ge(s_hg, (g + 1) * HC)
                for w in range(HB):
                    wait(pe, s_ye, (g - YB) * HB + w + 1)
                    for m in range(HC):
                        r = pe.matmul(T["ps_y2"][:, (u % YB) * HB + w, 0:C], HT[:, u % 2, m, w * P:(w + 1) * P], T["W2"][:, bass.ds(at + m * C, C)],
                                      start=(m == 0), stop=(m == HC - 1))
                    r.then_inc(s_y, 1)
            turn(0, 0)
            turn(0, 1)
            hidden(0, 0)
            each_group_of_tiles(pe, tile)

        @block.vector
        def _(v):
            def turned(j, u):
                g = UE * j + u
                v.wait_ge(s_t, g + 1)
                wait(v, s_h, (g - 1) * HC)
                v.tensor_copy(XT[:, u % 2, :, :], T["ps_x"][:, u % 2, 0:2 * SLOTS].rearrange("p (k n) -> p k n", k=2)).then_inc(s_xt, 1)

            def tile(j, u, more):
                g = UE * j + u
                if more or u + 2 < UE:
                    turned(j + (u + 2) // UE, (u + 2) % UE)
                at = offset(mybir.EngineType.DVE, 2, g, (NEXP - 1) * C)
                wait(v, s_sc[u], j * 16 * HB)
                for w in range(HB):
                    v.wait_ge(s_y, g * HB + w + 1)
                    v.tensor_tensor(YG[:, (u * HB + w) * C:(u * HB + w + 1) * C], T["ps_y2"][:, (u % YB) * HB + w, 0:C], T["B2"][:, bass.ds(at, C)], ALU.add).then_inc(s_ye, 1)
            turned(0, 0)
            turned(0, 1)
            each_group_of_tiles(v, tile)


def phase_finish(nc, sem, T, d):
    s_y = [sem(f"fi_rows{c}") for c in range(5)]
    s_a, s_o = sem("fi_added"), sem("fi_stored")
    X, YF = T["X"], T["YF"]
    CT_ = NT // 5
    with nc.Block() as block:
        @block.sync
        def _(sp):
            for c in range(5):
                for r in range(2):
                    r0, full = (r * NT + c * CT_) * P, min(CT_, N // P - c * CT_)
                    sp.dma_start(YF[:, r, c * CT_:c * CT_ + full, :], d["ytab"][r0:r0 + full * P, :].rearrange("(t p) c -> p t c", p=P)).then_inc(s_y[c], 16)
            for r in range(2):
                r0 = (r * NT + NT - 1) * P
                sp.dma_start(YF[0:LAST, r, NT - 1, :], d["ytab"][r0:r0 + LAST, :]).then_inc(s_y[4], 16)
            for c in range(5):
                sp.wait_ge(s_a, (c + 1) * CT_ * 2)
                full = min(CT_, N // P - c * CT_)
                sp.dma_start(d["out"][c * CT_ * P:(c * CT_ + full) * P, :].rearrange("(t p) c -> p t c", p=P), X[:, c * CT_:c * CT_ + full, :]).then_inc(s_o, 16)
            sp.dma_start(d["out"][(NT - 1) * P:N, :], X[0:LAST, NT - 1, :]).then_inc(s_o, 16)
            sp.wait_ge(s_o, 16 * 6)

        @block.vector
        def _(v):
            for c in range(5):
                v.wait_ge(s_y[c], 64 if c == 4 else 32)
                for r in range(2):
                    for t in range(c * CT_, (c + 1) * CT_):
                        if r:
                            v.wait_ge(s_a, c * CT_ * 2 + t - c * CT_ + 1)
                        n = LAST if t == NT - 1 else P
                        v.scalar_tensor_tensor(out=X[0:n, t, :], in0=YF[0:n, r, t, :], scalar=T["PV"][0:n, r, t:t + 1], in1=X[0:n, t, :],
                                               op0=ALU.mult, op1=ALU.add).then_inc(s_a, 1)
DRAM_IN = ["x", "edges", "g_query", "g_Wq", "g_bq", "g_Wk", "g_bk", "g_Wv", "g_bv", "g_rel_w", "g_Wo", "g_bo", "g_gamma",
           "g_beta", "m_WqT", "m_WkvT", "m_WprojT", "m_bproj", "f_gate_w", "f_gate_b", "f_W1", "f_b1", "f_W2", "f_b2"]


def build(nc, d, dbg=None):
    d["ktab"] = nc.dram_tensor("ktab", (NT * P, C), F32).ap()
    d["vtab"] = nc.dram_tensor("vtab", (NT * P, C), F32).ap()
    d["dl_rows"] = nc.dram_tensor("dl_rows", (NS, P), BF16).ap()
    d["ty_rows"] = nc.dram_tensor("ty_rows", (NS, P), BF16).ap()
    d["xtab"] = nc.dram_tensor("xtab", (NT * P, C), F32).ap()
    d["ytab"] = nc.dram_tensor("ytab", (2 * NT * P + NSLOT, C), F32).ap()
    with ExitStack() as ctx:
        def sem(name):
            return ctx.enter_context(nc.semaphore(name))

        T = {}

        def sbuf(stack, spec):
            for n, (shape, dt) in spec.items():
                T[n] = stack.enter_context(nc.sbuf_tensor(n, list(shape), dt))

        def psum(stack, spec):
            for n, (shape, dt) in spec.items():
                T[n] = stack.enter_context(nc.psum_tensor(n, list(shape), dt))

        sbuf(ctx, {"X": ((P, NT, C), F32), "rstd": ((P, NT), F32), "nmr": ((P, NT), F32), 
                   "SEL": ((P, 2, NT, NEXP), F32), "PV": ((P, 2, NT), F32),
                   "CTX": ((P, 2, P + 1), F32), "iota_f": ((P, P), F32), "iota_p": ((P, 1), F32), "ident": ((P, P), F32),
                   "onesr": ((P, P), F32), "zero": ((P, P + 1), F32)})
        mid = ctx.enter_context(ExitStack())
        sbuf(mid, {"QT": ((P, 2, NT * P), F32), "ACC": ((P, NT * (C + H)), F32)})
        with ExitStack() as gnn:
            sbuf(gnn, {"SRC": ((P, NS), I32), "DC": ((P, NS), F32), "qRow": ((1, NS), I32), "aRow": ((1, NS), I32), "penf": ((P, SC, P), F32),
                       "penb": ((P, SC, P), F32), "valid": ((P, SC, P), F32), "S": ((P, NS * H), F32)})
            keys = ExitStack()
            sbuf(keys, {"Q3": ((P, NT * 3 * C), BF16)})
            with ExitStack() as ph:
                sbuf(ph, {"W": ((P, 2, 5 * C), F32), "WQM": ((P, 2, C), F32), "brow": ((1, 3 * C), F32), "qe": ((P, 2), F32),
                          "qbc": ((P, 2, P), F32), "bias": ((P, 3 * C), F32), "stats": ((P, NT, 6), F32), "qf": ((P, 2, C), F32), "mv": ((P, NT, 2), F32),
                          "xnb": ((P, 3, C), F32), "xnT": ((P, 2, 2, P), F32), "kvb": ((P, 2, 2 * C), F32),
                          "ex": ((P, 2, 2 * C), F32), "kb": ((P, 2, C), F32), "vb": ((P, 2, 2, P + 1), F32), "mask": ((P, NT), F32),
                          "iota_i": ((P, P), I32), "iota_pi": ((P, 1), I32), "node_i": ((P, NT), I32)})
                psum(ph, {"ps_n": ((P, 2, 3, 512), F32), "ps_t": ((P, 2, P), F32), "ps_c": ((P, 2, P + 1), F32)})
                phase_project(nc, sem, T, d)
            with ExitStack() as ph:
                sbuf(ph, {"last_i": ((1, ET), I32), "t_i": ((1, ET), I32), "hi": ((1, ET), F32), "st": ((1, ET), F32),
                          "s_i": ((P, SC), I32), "s_f": ((P, SC), F32), "junk": ((P, ET), F32), "cnt": ((P, SC), F32),
                          "bS": ((P, SC), F32), "b128": ((P, SC), F32), "tI": ((P, SC), I32), "EI": ((P, SC, 5 * P), I32),
                          "DL": ((P, SC, P), F32), "rows": ((P, 2, SC, P), BF16), "srow": ((P, SC, P), F32)})
                psum(ph, {"ps_a": ((P, 512), F32), "ps_b": ((P, 512), F32)})
                phase_steps(nc, sem, T, d)
            with ExitStack() as ph:
                sbuf(ph, {"dlb": ((P, 2, G * P), BF16), "tyb": ((NREL, 2, G * P), BF16), "ixs": ((P, RG, G), I32),
                          "KG": ((P, RG * G * C), F32), "PT": ((P, 2, G * P), BF16), "OT": ((NREL, 2, G * P), BF16), "rel3": ((NREL, 3, D), BF16),
                          "rel": ((NREL, D), F32), "KU": ((P, 2, G * C), F32)})
                psum(ph, {"ps_qe": ((P, 2, G, C), F32), "ps_u": ((P, 2, G, 2 * D), F32)})
                T["ps_u"] = T["ps_u"][:, :, :, 0:D]
                phase_scores(nc, sem, T, d)
            keys.close()
            sbuf(gnn, {"VG": ((P, RV * G * C), F32), "ixv": ((P, RV, G), I32)})
            s_ix, s_g = sem("ag_indices"), [sem(f"ag_gathered{h}") for h in range(RV)]
            with ExitStack() as ph:
                sbuf(ph, {"ST": ((P, SC * H, P), F32), "SX": ((P, SC * H, P), F32), "F": ((P, SC * H, P), F32),
                          "penL": ((P, SC * H, P), F32), "LR": ((P, 2, SC * H), F32), "rp": ((P, SC), F32),
                          "E2": ((H, 2, NS), F32), "E4": ((H, NS), F32), "CR": ((H, NS), F32), "inj": ((P, SC * H), F32)})
                psum(ph, {"ps_s": ((P, SC, 512), F32), "ps_e": ((P, 2, 512), F32), "ps_c2": ((P, SC * H), F32)})
                phase_softmax_weights(nc, sem, T, d, s_ix, s_g)
            with ExitStack() as ph:
                sbuf(ph, {"WV": ((P, 2, G, C + H), F32), "PM": ((P, 2, G, P), F32)})
                psum(ph, {"ps_o": ((P, 2 * G, 512), F32)})
                phase_aggregate(nc, sem, T, d, s_ix, s_g)
            if dbg == "S":
                s_o = sem("s_o")
                with nc.Block() as block:
                    @block.sync
                    def _(sp):
                        sp.dma_start(d["out_S"], T["S"][:, :]).then_inc(s_o, 16)
                        sp.dma_start(d["out_A"], T["ACC"][:, :]).then_inc(s_o, 16)
                        sp.wait_ge(s_o, 32)
                return
        with ExitStack() as ph:
            sbuf(ph, {"Y": ((P, NT, C), F32), "VB": ((P, NT, C), F32), "Wo": ((P, 2, C), F32), "WP": ((P, 2, C), F32), "GW": ((P, 2, NEXP), F32),
                      "bias2": ((P, 2, C), F32), "gb": ((P, NEXP), F32), "gamma": ((P, C), F32), "beta": ((P, C), F32),
                      "bd_o": ((P, P), I32), "bd_e": ((P, P), I32), "BD": ((P, P), F32), "KS": ((P, 2, P // MD), F32),
                      "CB": ((P, 2, P), F32), "CT": ((P, 2, P), F32), "M": ((P, 2, C), F32), "rd": ((P, NT * C // MD), F32), "RS": ((P, NT, C), F32),
                      "iz": ((P, NT, H), F32), "dn": ((P, NT, H), F32), "stats2": ((P, NT, 6), F32),
                      "mv2": ((P, NT, 2), F32), "mT": ((P, 2, 2, P), F32), "LG": ((P, NT, NEXP), F32),
                      "mx": ((P, NT), F32), "eq": ((P, NT, NEXP), F32),
                      "rank": ((P, NEXP), F32), "rank_i": ((P, NEXP), I32)})
            psum(ph, {"ps_s2": ((P, 2 * C), F32), "ps_d": ((P, 2, 512), F32), "ps_t2": ((P, 2, 512), F32), "ps_y": ((P, 3, 2 * C), F32)})
            phase_combine(nc, sem, T, d)
        mid.close()
        with ExitStack() as ffn:
            NB, HB = NSLOT // P, SLOTS // P
            sbuf(ffn, {"W1": ((P, NEXP * W1C), F32), "W2": ((P, NEXP * HC * C), F32), "B2": ((P, NEXP * C), F32),
                       "GI": ((P, NB), I32), "DI": ((P, NB), I32), "off": ((P, 3, NTILE), I32)})
            with ExitStack() as ph:
                sbuf(ph, {"Msel": ((P, NT, NEXP), F32), "TE": ((P, NEXP, NT), F32), "INC": ((P, NEXP, NT), F32), "keep": ((P, NEXP, NT), F32),
                          "posf": ((P, 2 * NT), F32), "as_i": ((P, 2 * NT), I32), "sl_i": ((P, NB), I32), "tl_i": ((P, NTILE), I32),
                          "asg": ((P, 2 * NT), F32), "slot": ((P, NB), F32), "tl": ((P, NTILE), F32), "LT": ((P, P), F32),
                          "real": ((P, NT), F32), "cnt_e": ((P, NEXP), F32), "cnt_i": ((P, NEXP), I32), "base": ((P, NEXP), F32),
                          "ge": ((P, NTILE, NEXP), F32), "ex_t": ((P, NTILE), F32), "pos_i": ((P, 2 * NT), I32),
                          "pos_h": ((P, 2 * NT), I32), "hi_f": ((P, 2 * NT), F32), "lo_f": ((P, 2 * NT), F32),
                          "OHh": ((P, 4, NB), F32), "OHl": ((P, 4, P), F32), "inv": ((NB, P), F32), "vv": ((P, NB), F32), "t1": ((P, NB), F32)})
                psum(ph, {"ps_m": ((P, 2, 512), F32), "ps_inv": ((P, 512), F32)})
                phase_route(nc, sem, T, d)
            with ExitStack() as ph:
                sbuf(ph, {"XG": ((P, UE * SLOTS * C // P), F32), "YG": ((P, UE * SLOTS * C // P), F32), "GX": ((P, UE, HB), I32),
                          "DX": ((P, UE, HB), I32), "WB": ((P, 2, W1C), F32), "XT": ((P, 2, 2, SLOTS), F32), "HT": ((P, 2, HC, SLOTS), F32)})
                psum(ph, {"ps_h": ((P, HC, 512), F32), "ps_x": ((P, 2, 512), F32), "ps_y2": ((P, 2 * HB, 512), F32)})
                phase_experts(nc, sem, T, d)
        with ExitStack() as ph:
            sbuf(ph, {"YF": ((P, 2, NT, C), F32)})
            phase_finish(nc, sem, T, d)


DBG=None
OUTS={"out":(N,C)}


def lay_out(inputs):
    import numpy as np
    g = {k: np.ascontiguousarray(v) for k, v in inputs.items()}
    a = {}
    a["x"] = np.concatenate([g["x"], np.zeros((NT * P - N, C), np.float32)])
    npad = ET * P - E_REAL
    pad = np.full((npad,), PADDST, np.int32)
    dst = np.concatenate([np.full((1,), -1, np.int32), g["dst"], pad, pad[:1]])
    z = np.zeros((npad,), np.int32)
    a["edges"] = np.ascontiguousarray(np.concatenate([v.reshape(ET, P) for v in (
        dst[1:-1], dst[:-2], dst[2:], np.concatenate([g["src"], z]), np.concatenate([g["edge_type_64"], z]))], axis=1))
    for n, m in (("g_query", "gnn_query_emb"), ("g_Wq", "gnn_Wq"), ("g_bq", "gnn_bq"), ("g_Wk", "gnn_Wk"), ("g_bk", "gnn_bk"),
                 ("g_Wv", "gnn_Wv"), ("g_bv", "gnn_bv"), ("g_rel_w", "gnn_rel_w"), ("g_Wo", "gnn_Wo"), ("g_bo", "gnn_bo"),
                 ("g_gamma", "gnn_gamma"), ("g_beta", "gnn_beta"), ("m_bproj", "mix_bproj"), ("f_gate_w", "ffn_gate_w"),
                 ("f_gate_b", "ffn_gate_b"), ("f_W1", "ffn_W1"), ("f_b1", "ffn_b1"), ("f_W2", "ffn_W2"), ("f_b2", "ffn_b2")):
        a[n] = g["L0_" + m]
    for n, m in (("m_WqT", "mix_Wq"), ("m_WkvT", "mix_Wkv"), ("m_WprojT", "mix_Wproj")):
        a[n] = np.ascontiguousarray(g["L0_" + m].T)
    return a


def kernel(**inputs):
    import concourse.bacc as _bacc
    from concourse import mybir as _mybir
    from concourse.bass_utils import run_bass_kernel_spmd as _run

    nc = _bacc.Bacc("TRN2", target_bir_lowering=False, num_devices=1)
    a = lay_out(inputs)
    d = {n: nc.dram_tensor(f"in_{n}_dram", a[n].shape, _mybir.dt.from_np(a[n].dtype), kind="ExternalInput").ap() for n in DRAM_IN}
    for n, (shape) in OUTS.items():
        d[n] = nc.dram_tensor(n + "_dram", shape, F32, kind="ExternalOutput").ap()
    build(nc, d, DBG)
    r = _run(nc, [{f"in_{n}_dram": a[n] for n in DRAM_IN}], core_ids=[0])
    res = r.results[0]
    return tuple(res[n + "_dram"] for n in OUTS) if len(OUTS) > 1 else res["out_dram"][0:N]
```
